# Optimizing a Trainium2 kernel written in Bass

```python
import numpy as np
import jax
import jax.numpy as jnp

def _softmax(x, axis=-1):
    return jax.nn.softmax(x, axis=axis)

def _gelu(x):
    return jax.nn.gelu(x, approximate=True)

def _silu(x):
    return jax.nn.silu(x)

def _sigmoid(x):
    return jax.nn.sigmoid(x)

def _layernorm(x, axis=-1, eps=1e-05):
    m = jnp.mean(x, axis=axis, keepdims=True)
    v = jnp.var(x, axis=axis, keepdims=True)
    return (x - m) / jnp.sqrt(v + eps)

def _scatter_add(tgt, idx, src, axis=0):
    return tgt.at[idx].add(src)

def _segment_sum(src, seg, n):
    return jax.ops.segment_sum(src, seg, n)
kernel_name = 'mk_seq_postln_d4_jaxref_r8_47ed63'

def setup_inputs(seed: int=0):
    np.random.seed(seed)
    _w = jnp.asarray

    def _L0_attn_setup():
        import math
        import jax, jax.numpy as jnp
        import numpy as np
        B, T, C = (2, 256, 256)
        H, G = (16, 4)
        D = C // H
        KV = G * D
        SOFT_CAP = 50.0
        EPS = 1e-06

        def _rmsnorm(x, w):
            rms = jnp.linalg.norm(x, axis=-1, keepdims=True) / math.sqrt(x.shape[-1])
            return w * (x / (rms + EPS))

        def _rotary_tables(seq_len, dim):
            inv_freq = 1.0 / 10000.0 ** (jnp.arange(0, dim, 2, dtype=jnp.float32) / dim)
            t = jnp.arange(seq_len, dtype=jnp.float32)
            freqs = jnp.outer(t, inv_freq)
            return (jnp.cos(freqs), jnp.sin(freqs))

        def _apply_rope(x, cos, sin):
            d = x.shape[-1] // 2
            x1, x2 = (x[..., :d], x[..., d:])
            c = cos[None, :, None, :]
            s = sin[None, :, None, :]
            return jnp.concatenate([x1 * c + x2 * s, -x1 * s + x2 * c], axis=-1)
        key = jax.random.key(seed)
        ks = jax.random.split(key, 5)
        s = 1.0 / math.sqrt(C)
        return {'x': jax.random.normal(ks[0], (B, T, C), jnp.float32), 'Wq': jax.random.normal(ks[1], (C, C), jnp.float32) * s, 'Wk': jax.random.normal(ks[2], (KV, C), jnp.float32) * s, 'Wv': jax.random.normal(ks[3], (KV, C), jnp.float32) * s, 'Wo': jax.random.normal(ks[4], (C, C), jnp.float32) * s, 'bo': jnp.zeros((C,), jnp.float32), 'q_norm_w': jnp.ones((D,), jnp.float32), 'k_norm_w': jnp.ones((D,), jnp.float32)}
    _L0_attn_in = _L0_attn_setup()

    def _L0_ffn_setup():
        import jax, jax.numpy as jnp
        import numpy as np
        D_MODEL = 256
        D_FF = 1024

        def absmean_quant(w):
            scale = jnp.mean(jnp.abs(w))
            mask = (jnp.abs(w) >= scale * 0.7).astype(w.dtype)
            return jnp.sign(w) * mask
        key = jax.random.key(seed)
        k_x, k_w1, k_w2 = jax.random.split(key, 3)
        x = jax.random.normal(k_x, (4, 512, D_MODEL), dtype=jnp.float32)
        w1 = jax.random.normal(k_w1, (D_FF, D_MODEL), dtype=jnp.float32)
        b1 = jnp.zeros((D_FF,), dtype=jnp.float32)
        w2 = jax.random.normal(k_w2, (D_MODEL, D_FF), dtype=jnp.float32)
        b2 = jnp.zeros((D_MODEL,), dtype=jnp.float32)
        return {'x': x, 'w1': w1, 'b1': b1, 'w2': w2, 'b2': b2}
    _L0_ffn_in = _L0_ffn_setup()

    def _L1_attn_setup():
        import jax, jax.numpy as jnp
        import numpy as np
        from jax import lax

        def _causal_depthwise_conv(x, conv_w, conv_b):
            K = conv_w.shape[-1]
            xc = jnp.transpose(x, (0, 2, 1))
            xc = jnp.pad(xc, ((0, 0), (0, 0), (K - 1, 0)))
            D = xc.shape[1]
            y = lax.conv_general_dilated(xc, conv_w, window_strides=(1,), padding='VALID', dimension_numbers=('NCH', 'OIH', 'NCH'), feature_group_count=D)
            y = y + conv_b[None, :, None]
            return jnp.transpose(y, (0, 2, 1))
        key = jax.random.key(seed)
        ks = jax.random.split(key, 7)
        B, L, Dm, S, K = (4, 512, 256, 64, 4)
        s = 0.02
        x = jax.random.normal(ks[0], (B, L, Dm), dtype=jnp.float32)
        Wxproj = jax.random.normal(ks[1], (2 * S + 1, Dm), dtype=jnp.float32) * s
        Winproj = jax.random.normal(ks[2], (S, Dm), dtype=jnp.float32) * s
        Woutproj = jax.random.normal(ks[3], (Dm, S), dtype=jnp.float32) * s
        conv_w = jax.random.normal(ks[4], (Dm, 1, K), dtype=jnp.float32) * 0.5
        conv_b = jax.random.normal(ks[5], (Dm,), dtype=jnp.float32) * 0.02
        A_log = jnp.log(jnp.arange(1, S + 1, dtype=jnp.float32))
        D = jnp.ones((Dm,), dtype=jnp.float32)
        return {'x': x, 'Wxproj': Wxproj, 'Winproj': Winproj, 'Woutproj': Woutproj, 'conv_w': conv_w, 'conv_b': conv_b, 'A_log': A_log, 'D': D}
    _L1_attn_in = _L1_attn_setup()

    def _L1_ffn_setup():
        import jax, jax.numpy as jnp
        import numpy as np
        DIM_IN = 256
        DIM_HIDDEN = 1024
        key = jax.random.key(seed)
        k_x, k_g, k_u, k_d = jax.random.split(key, 4)
        s_in = 1.0 / np.sqrt(DIM_IN)
        s_hid = 1.0 / np.sqrt(DIM_HIDDEN)
        x = jax.random.normal(k_x, (4, 256, DIM_IN), dtype=jnp.float32)
        w_gate = jax.random.uniform(k_g, (DIM_HIDDEN, DIM_IN), jnp.float32, -s_in, s_in)
        w_up = jax.random.uniform(k_u, (DIM_HIDDEN, DIM_IN), jnp.float32, -s_in, s_in)
        w_down = jax.random.uniform(k_d, (DIM_IN, DIM_HIDDEN), jnp.float32, -s_hid, s_hid)
        return {'x': x, 'w_gate': w_gate, 'w_up': w_up, 'w_down': w_down}
    _L1_ffn_in = _L1_ffn_setup()

    def _L2_attn_setup():
        import jax, jax.numpy as jnp
        import numpy as np
        HEADS = 8
        CHUNK = 32

        def _gammas(heads):
            betas = jnp.linspace(np.log2(1.0 / 32.0), np.log2(1.0 / 512.0), heads)
            return 1.0 - jnp.exp2(betas)
        key = jax.random.key(seed)
        ks = jax.random.split(key, 4)
        H = 256
        x = jax.random.normal(ks[0], (4, 512, H), dtype=jnp.float32)
        sc = 1.0 / np.sqrt(H)
        Wq = jax.random.normal(ks[1], (H, H), dtype=jnp.float32) * sc
        Wk = jax.random.normal(ks[2], (H, H), dtype=jnp.float32) * sc
        Wv = jax.random.normal(ks[3], (H, H), dtype=jnp.float32) * sc
        z = jnp.zeros((H,), dtype=jnp.float32)
        return {'x': x, 'Wq': Wq, 'bq': z, 'Wk': Wk, 'bk': z, 'Wv': Wv, 'bv': z}
    _L2_attn_in = _L2_attn_setup()

    def _L2_ffn_setup():
        import jax, jax.numpy as jnp
        import numpy as np
        N_HEAD = 16
        N_EMBD = 256
        R = 8
        HEAD_DIM = N_EMBD // N_HEAD
        D_STD = HEAD_DIM - R
        THRESHOLD = 0.1
        B, T = (4, 128)
        key = jax.random.key(seed)
        k1, k2, k3, k4, k5 = jax.random.split(key, 5)
        fused_dim = 2 * N_HEAD * D_STD + N_EMBD + 2 * N_HEAD * R
        x = jax.random.normal(k1, (B, T, N_EMBD), dtype=jnp.float32)
        Wa = jax.random.normal(k2, (N_EMBD, fused_dim), dtype=jnp.float32) * 0.02
        Wp = jax.random.normal(k3, (N_EMBD, N_EMBD), dtype=jnp.float32) * 0.02
        w_std = jax.random.uniform(k4, (N_HEAD,), dtype=jnp.float32, minval=0.3, maxval=0.7)
        w_rec = jax.random.uniform(k5, (N_HEAD,), dtype=jnp.float32)
        return {'x': x, 'Wa': Wa, 'Wp': Wp, 'w_std': w_std, 'w_rec': w_rec}
    _L2_ffn_in = _L2_ffn_setup()

    def _L3_attn_setup():
        import jax, jax.numpy as jnp
        import numpy as np
        HEAD_DIM = 32
        ROPE_THETA = 1000000.0
        EPS = 1e-06

        def rmsnorm(x, w):
            var = jnp.mean(jnp.square(x), axis=-1, keepdims=True)
            return x * jax.lax.rsqrt(var + EPS) * w

        def apply_rope(x):
            L, hd = (x.shape[-2], x.shape[-1])
            half = hd // 2
            pos = jnp.arange(L, dtype=x.dtype)
            idx = jnp.arange(half, dtype=x.dtype)
            inv_freq = 1.0 / ROPE_THETA ** (2.0 * idx / hd)
            freqs = pos[:, None] * inv_freq[None, :]
            cos = jnp.cos(freqs)[None, None]
            sin = jnp.sin(freqs)[None, None]
            x1, x2 = (x[..., :half], x[..., half:])
            return jnp.concatenate([x1 * cos - x2 * sin, x1 * sin + x2 * cos], axis=-1)
        key = jax.random.key(seed)
        ks = jax.random.split(key, 7)
        B, L, D = (2, 256, 256)
        H, HD = (8, HEAD_DIM)
        s = lambda fan_in: 1.0 / np.sqrt(fan_in)
        return {'x': jax.random.normal(ks[0], (B, L, D), jnp.float32), 'q_proj': jax.random.normal(ks[1], (H * HD, D), jnp.float32) * s(D), 'k_proj': jax.random.normal(ks[2], (HD, D), jnp.float32) * s(D), 'v_proj': jax.random.normal(ks[3], (HD, D), jnp.float32) * s(D), 'o_proj': jax.random.normal(ks[4], (D, H * HD), jnp.float32) * s(H * HD), 'q_norm': jnp.ones((HD,), jnp.float32), 'k_norm': jnp.ones((HD,), jnp.float32)}
    _L3_attn_in = _L3_attn_setup()

    def _L3_ffn_setup():
        import jax, jax.numpy as jnp
        import numpy as np
        HIDDEN = 256
        NUM_EXPERTS = 8
        TOP_K = 2
        MOE_INTER = 176
        SHARED_INTER = 704

        def _silu_and_mul(gu):
            i = gu.shape[-1] // 2
            return jax.nn.silu(gu[:, :i]) * gu[:, i:]
        key = jax.random.key(seed)
        ks = jax.random.split(key, 7)
        s = 0.02
        return {'hidden_states': jax.random.normal(ks[0], (2, 256, HIDDEN), dtype=jnp.float32), 'gate_w': jax.random.normal(ks[1], (NUM_EXPERTS, HIDDEN), dtype=jnp.float32) * s, 'shared_gate_w': jax.random.normal(ks[2], (1, HIDDEN), dtype=jnp.float32) * s, 'shared_gate_up_w': jax.random.normal(ks[3], (2 * SHARED_INTER, HIDDEN), dtype=jnp.float32) * s, 'shared_down_w': jax.random.normal(ks[4], (HIDDEN, SHARED_INTER), dtype=jnp.float32) * s, 'w13': jax.random.normal(ks[5], (NUM_EXPERTS, 2 * MOE_INTER, HIDDEN), dtype=jnp.float32) * s, 'w2': jax.random.normal(ks[6], (NUM_EXPERTS, HIDDEN, MOE_INTER), dtype=jnp.float32) * s}
    _L3_ffn_in = _L3_ffn_setup()
    _d = {'L0_attn_x': _L0_attn_in['x'], 'L0_attn_Wq': _L0_attn_in['Wq'], 'L0_attn_Wk': _L0_attn_in['Wk'], 'L0_attn_Wv': _L0_attn_in['Wv'], 'L0_attn_Wo': _L0_attn_in['Wo'], 'L0_attn_bo': _L0_attn_in['bo'], 'L0_attn_q_norm_w': _L0_attn_in['q_norm_w'], 'L0_attn_k_norm_w': _L0_attn_in['k_norm_w'], 'L0_ffn_w1': _L0_ffn_in['w1'], 'L0_ffn_b1': _L0_ffn_in['b1'], 'L0_ffn_w2': _L0_ffn_in['w2'], 'L0_ffn_b2': _L0_ffn_in['b2'], 'L1_attn_Wxproj': _L1_attn_in['Wxproj'], 'L1_attn_Winproj': _L1_attn_in['Winproj'], 'L1_attn_Woutproj': _L1_attn_in['Woutproj'], 'L1_attn_conv_w': _L1_attn_in['conv_w'], 'L1_attn_conv_b': _L1_attn_in['conv_b'], 'L1_attn_A_log': _L1_attn_in['A_log'], 'L1_attn_D': _L1_attn_in['D'], 'L1_ffn_w_gate': _L1_ffn_in['w_gate'], 'L1_ffn_w_up': _L1_ffn_in['w_up'], 'L1_ffn_w_down': _L1_ffn_in['w_down'], 'L2_attn_Wq': _L2_attn_in['Wq'], 'L2_attn_bq': _L2_attn_in['bq'], 'L2_attn_Wk': _L2_attn_in['Wk'], 'L2_attn_bk': _L2_attn_in['bk'], 'L2_attn_Wv': _L2_attn_in['Wv'], 'L2_attn_bv': _L2_attn_in['bv'], 'L2_ffn_Wa': _L2_ffn_in['Wa'], 'L2_ffn_Wp': _L2_ffn_in['Wp'], 'L2_ffn_w_std': _L2_ffn_in['w_std'], 'L2_ffn_w_rec': _L2_ffn_in['w_rec'], 'L3_attn_q_proj': _L3_attn_in['q_proj'], 'L3_attn_k_proj': _L3_attn_in['k_proj'], 'L3_attn_v_proj': _L3_attn_in['v_proj'], 'L3_attn_o_proj': _L3_attn_in['o_proj'], 'L3_attn_q_norm': _L3_attn_in['q_norm'], 'L3_attn_k_norm': _L3_attn_in['k_norm'], 'L3_ffn_gate_w': _L3_ffn_in['gate_w'], 'L3_ffn_shared_gate_w': _L3_ffn_in['shared_gate_w'], 'L3_ffn_shared_gate_up_w': _L3_ffn_in['shared_gate_up_w'], 'L3_ffn_shared_down_w': _L3_ffn_in['shared_down_w'], 'L3_ffn_w13': _L3_ffn_in['w13'], 'L3_ffn_w2': _L3_ffn_in['w2']}
    _x0 = _d['L0_attn_x']
    _d['L0_attn_x'] = jax.random.normal(jax.random.fold_in(jax.random.key(seed), 1), (4, 1024, 256), dtype=_x0.dtype)
    del _x0
    return _d

def reference(L0_attn_x, L0_attn_Wq, L0_attn_Wk, L0_attn_Wv, L0_attn_Wo, L0_attn_bo, L0_attn_q_norm_w, L0_attn_k_norm_w, L0_ffn_w1, L0_ffn_b1, L0_ffn_w2, L0_ffn_b2, L1_attn_Wxproj, L1_attn_Winproj, L1_attn_Woutproj, L1_attn_conv_w, L1_attn_conv_b, L1_attn_A_log, L1_attn_D, L1_ffn_w_gate, L1_ffn_w_up, L1_ffn_w_down, L2_attn_Wq, L2_attn_bq, L2_attn_Wk, L2_attn_bk, L2_attn_Wv, L2_attn_bv, L2_ffn_Wa, L2_ffn_Wp, L2_ffn_w_std, L2_ffn_w_rec, L3_attn_q_proj, L3_attn_k_proj, L3_attn_v_proj, L3_attn_o_proj, L3_attn_q_norm, L3_attn_k_norm, L3_ffn_gate_w, L3_ffn_shared_gate_w, L3_ffn_shared_gate_up_w, L3_ffn_shared_down_w, L3_ffn_w13, L3_ffn_w2):

    def _L0_attn_ref(x, Wq, Wk, Wv, Wo, bo, q_norm_w, k_norm_w):
        import math
        import jax, jax.numpy as jnp
        import numpy as np
        B, T, C = (2, 256, 256)
        H, G = (16, 4)
        D = C // H
        KV = G * D
        SOFT_CAP = 50.0
        EPS = 1e-06

        def _rmsnorm(x, w):
            rms = jnp.linalg.norm(x, axis=-1, keepdims=True) / math.sqrt(x.shape[-1])
            return w * (x / (rms + EPS))

        def _rotary_tables(seq_len, dim):
            inv_freq = 1.0 / 10000.0 ** (jnp.arange(0, dim, 2, dtype=jnp.float32) / dim)
            t = jnp.arange(seq_len, dtype=jnp.float32)
            freqs = jnp.outer(t, inv_freq)
            return (jnp.cos(freqs), jnp.sin(freqs))

        def _apply_rope(x, cos, sin):
            d = x.shape[-1] // 2
            x1, x2 = (x[..., :d], x[..., d:])
            c = cos[None, :, None, :]
            s = sin[None, :, None, :]
            return jnp.concatenate([x1 * c + x2 * s, -x1 * s + x2 * c], axis=-1)
        b, t, c = x.shape
        q = (x @ Wq.T).reshape(b, t, H, D)
        k = (x @ Wk.T).reshape(b, t, G, D)
        v = (x @ Wv.T).reshape(b, t, G, D)
        cos, sin = _rotary_tables(t, D)
        q = _apply_rope(_rmsnorm(q, q_norm_w), cos, sin)
        k = _apply_rope(_rmsnorm(k, k_norm_w), cos, sin)
        q = q.transpose(0, 2, 1, 3)
        k = jnp.repeat(k.transpose(0, 2, 1, 3), H // G, axis=1)
        v = jnp.repeat(v.transpose(0, 2, 1, 3), H // G, axis=1)
        att = jnp.einsum('bhqd,bhkd->bhqk', q, k) / math.sqrt(D)
        causal = jnp.tril(jnp.ones((t, t), bool))
        att = jnp.where(causal[None, None], att, -jnp.inf)
        att = SOFT_CAP * jnp.tanh(att / SOFT_CAP)
        att = jax.nn.softmax(att, axis=-1)
        y = jnp.einsum('bhqk,bhkd->bhqd', att, v)
        y = y.transpose(0, 2, 1, 3).reshape(b, t, c)
        return y @ Wo.T + bo

    def _L0_ffn_ref(x, w1, b1, w2, b2):
        import jax, jax.numpy as jnp
        import numpy as np
        D_MODEL = 256
        D_FF = 1024

        def absmean_quant(w):
            scale = jnp.mean(jnp.abs(w))
            mask = (jnp.abs(w) >= scale * 0.7).astype(w.dtype)
            return jnp.sign(w) * mask
        w1_q = absmean_quant(w1)
        w2_q = absmean_quant(w2)
        h = jnp.einsum('bsd,fd->bsf', x, w1_q) + b1
        h = jax.nn.gelu(h, approximate=False)
        out = jnp.einsum('bsf,df->bsd', h, w2_q) + b2
        return out

    def _L1_attn_ref(x, Wxproj, Winproj, Woutproj, conv_w, conv_b, A_log, D):
        import jax, jax.numpy as jnp
        import numpy as np
        from jax import lax

        def _causal_depthwise_conv(x, conv_w, conv_b):
            K = conv_w.shape[-1]
            xc = jnp.transpose(x, (0, 2, 1))
            xc = jnp.pad(xc, ((0, 0), (0, 0), (K - 1, 0)))
            D = xc.shape[1]
            y = lax.conv_general_dilated(xc, conv_w, window_strides=(1,), padding='VALID', dimension_numbers=('NCH', 'OIH', 'NCH'), feature_group_count=D)
            y = y + conv_b[None, :, None]
            return jnp.transpose(y, (0, 2, 1))
        S = A_log.shape[0]
        x_conv = _causal_depthwise_conv(x, conv_w, conv_b)
        ssm_params = jnp.einsum('bld,pd->blp', x, Wxproj)
        Bmat = ssm_params[..., :S]
        Cmat = ssm_params[..., S:2 * S]
        delta = jax.nn.softplus(ssm_params[..., 2 * S:])
        A = -jnp.exp(A_log)
        deltaA = jnp.exp(A[None, None, :] * delta)
        x_state = jnp.einsum('bld,sd->bls', x_conv, Winproj)
        Bu = delta * Bmat * x_state

        def combine(c1, c2):
            a1, b1 = c1
            a2, b2 = c2
            return (a1 * a2, a2 * b1 + b2)
        _, h = lax.associative_scan(combine, (deltaA, Bu), axis=1)
        h_mod = Cmat * h
        out = jnp.einsum('bls,ds->bld', h_mod, Woutproj) + D[None, None, :] * x_conv
        return out

    def _L1_ffn_ref(x, w_gate, w_up, w_down):
        import jax, jax.numpy as jnp
        import numpy as np
        DIM_IN = 256
        DIM_HIDDEN = 1024
        gate = jnp.einsum('bsd,hd->bsh', x, w_gate)
        up = jnp.einsum('bsd,hd->bsh', x, w_up)
        gated = jax.nn.silu(gate) * up
        return jnp.einsum('bsh,dh->bsd', gated, w_down)

    def _L2_attn_ref(x, Wq, bq, Wk, bk, Wv, bv):
        import jax, jax.numpy as jnp
        import numpy as np
        HEADS = 8
        CHUNK = 32

        def _gammas(heads):
            betas = jnp.linspace(np.log2(1.0 / 32.0), np.log2(1.0 / 512.0), heads)
            return 1.0 - jnp.exp2(betas)
        B, S, H = x.shape
        h, C = (HEADS, CHUNK)
        d = H // h
        N = S // C
        g = _gammas(h)
        q = x @ Wq + bq
        k = x @ Wk + bk
        v = x @ Wv + bv

        def split(t):
            return t.reshape(B, N, C, h, d).transpose(1, 0, 3, 2, 4)
        qc, kc, vc = (split(q), split(k), split(v))
        idx = jnp.arange(C)
        i, j = (idx[:, None], idx[None, :])
        D = jnp.where(i >= j, g[:, None, None] ** (i - j).astype(jnp.float32), 0.0)
        cross_scale = g[:, None] ** (idx + 1).astype(jnp.float32)
        kv_scale = g[:, None] ** (C - 1 - idx).astype(jnp.float32)
        chunk_decay = g ** C

        def step(Sstate, qkv):
            qi, ki, vi = qkv
            attn = jnp.einsum('bhid,bhjd->bhij', qi, ki) * D
            inner = jnp.einsum('bhij,bhjd->bhid', attn, vi)
            cross = jnp.einsum('bhid,bhde->bhie', qi * cross_scale[:, :, None], Sstate)
            S_new = chunk_decay[:, None, None] * Sstate + jnp.einsum('bhjd,bhje->bhde', ki * kv_scale[:, :, None], vi)
            return (S_new, inner + cross)
        S0 = jnp.zeros((B, h, d, d), dtype=x.dtype)
        _, outs = jax.lax.scan(step, S0, (qc, kc, vc))
        return outs.transpose(1, 0, 3, 2, 4).reshape(B, S, H)

    def _L2_ffn_ref(x, Wa, Wp, w_std, w_rec):
        import jax, jax.numpy as jnp
        import numpy as np
        N_HEAD = 16
        N_EMBD = 256
        R = 8
        HEAD_DIM = N_EMBD // N_HEAD
        D_STD = HEAD_DIM - R
        THRESHOLD = 0.1
        B, T = (4, 128)
        Bx, Tx, C = x.shape
        H, D, Ds, r = (N_HEAD, HEAD_DIM, D_STD, R)
        s_std = jnp.sqrt(jnp.clip(w_std, 1e-08, None))
        s_rec = jnp.sqrt(jnp.clip(w_rec, 1e-08, None))
        col_scale = jnp.concatenate([jnp.repeat(s_std, Ds), jnp.repeat(s_std, Ds), jnp.ones((C,), dtype=x.dtype), jnp.repeat(s_rec, r), jnp.repeat(s_rec, r)])
        Wb = Wa * col_scale[None, :]
        fused = x @ Wb
        q_std_end = H * Ds
        k_std_end = q_std_end + H * Ds
        v_end = k_std_end + C
        q_low_end = v_end + H * r

        def heads(t, d):
            return t.reshape(Bx, Tx, H, d).transpose(0, 2, 1, 3)
        Q_std = heads(fused[..., :q_std_end], Ds)
        K_std = heads(fused[..., q_std_end:k_std_end], Ds)
        V = heads(fused[..., k_std_end:v_end], D)
        Q_low = heads(fused[..., v_end:q_low_end], r)
        K_low = heads(fused[..., q_low_end:], r)
        use_ra = (w_rec > THRESHOLD)[None, :, None, None]
        q_tail = jnp.where(use_ra, K_low, Q_low)
        k_tail = jnp.where(use_ra, Q_low, K_low)
        Qf = jnp.concatenate([Q_std, q_tail], axis=-1)
        Kf = jnp.concatenate([K_std, k_tail], axis=-1)
        scale = 1.0 / jnp.sqrt(jnp.asarray(D, dtype=x.dtype))
        scores = jnp.einsum('bhtd,bhsd->bhts', Qf, Kf) * scale
        causal = jnp.tril(jnp.ones((Tx, Tx), dtype=bool))
        scores = jnp.where(causal[None, None], scores, jnp.finfo(scores.dtype).min)
        attn = jax.nn.softmax(scores, axis=-1)
        out = jnp.einsum('bhts,bhsd->bhtd', attn, V)
        y = out.transpose(0, 2, 1, 3).reshape(Bx, Tx, C)
        return y @ Wp

    def _L3_attn_ref(x, q_proj, k_proj, v_proj, o_proj, q_norm, k_norm):
        import jax, jax.numpy as jnp
        import numpy as np
        HEAD_DIM = 32
        ROPE_THETA = 1000000.0
        EPS = 1e-06

        def rmsnorm(x, w):
            var = jnp.mean(jnp.square(x), axis=-1, keepdims=True)
            return x * jax.lax.rsqrt(var + EPS) * w

        def apply_rope(x):
            L, hd = (x.shape[-2], x.shape[-1])
            half = hd // 2
            pos = jnp.arange(L, dtype=x.dtype)
            idx = jnp.arange(half, dtype=x.dtype)
            inv_freq = 1.0 / ROPE_THETA ** (2.0 * idx / hd)
            freqs = pos[:, None] * inv_freq[None, :]
            cos = jnp.cos(freqs)[None, None]
            sin = jnp.sin(freqs)[None, None]
            x1, x2 = (x[..., :half], x[..., half:])
            return jnp.concatenate([x1 * cos - x2 * sin, x1 * sin + x2 * cos], axis=-1)
        B, L, D = x.shape
        HD = k_proj.shape[0]
        H = q_proj.shape[0] // HD
        k = rmsnorm(x @ k_proj.T, k_norm)
        q = rmsnorm((x @ q_proj.T).reshape(B, L, H, HD), q_norm)
        v = x @ v_proj.T
        q = q.transpose(0, 2, 1, 3)
        k = k[:, None]
        v = v[:, None]
        q = apply_rope(q)
        k = apply_rope(k)
        scores = jnp.matmul(q, jnp.swapaxes(k, -1, -2)) / jnp.sqrt(jnp.asarray(256.0, x.dtype))
        causal = jnp.tril(jnp.ones((L, L), bool))
        scores = jnp.where(causal, scores, -jnp.inf)
        w = jax.nn.softmax(scores, axis=-1)
        ctx = jnp.matmul(w, v)
        ctx = ctx.transpose(0, 2, 1, 3).reshape(B, L, H * HD)
        return ctx @ o_proj.T

    def _L3_ffn_ref(hidden_states, gate_w, shared_gate_w, shared_gate_up_w, shared_down_w, w13, w2):
        import jax, jax.numpy as jnp
        import numpy as np
        HIDDEN = 256
        NUM_EXPERTS = 8
        TOP_K = 2
        MOE_INTER = 176
        SHARED_INTER = 704

        def _silu_and_mul(gu):
            i = gu.shape[-1] // 2
            return jax.nn.silu(gu[:, :i]) * gu[:, i:]
        orig_shape = hidden_states.shape
        x = hidden_states.reshape(-1, orig_shape[-1])
        shared = _silu_and_mul(x @ shared_gate_up_w.T) @ shared_down_w.T
        shared = shared * jax.nn.sigmoid(x @ shared_gate_w.T)
        router_logits = x @ gate_w.T
        probs = jax.nn.softmax(router_logits.astype(jnp.float32), axis=-1)
        routing_weights, selected_experts = jax.lax.top_k(probs, TOP_K)
        combined = jnp.zeros(x.shape, dtype=jnp.float32)
        E = w13.shape[0]
        for e in range(E):
            w_e = jnp.where(selected_experts == e, routing_weights, 0.0).sum(-1)
            h = _silu_and_mul(x @ w13[e].T) @ w2[e].T
            combined = combined + w_e[:, None] * h.astype(jnp.float32)
        out = shared + combined.astype(x.dtype)
        return out.reshape(orig_shape)
    x = L0_attn_x
    x = _layernorm(x + _L0_attn_ref(x, L0_attn_Wq, L0_attn_Wk, L0_attn_Wv, L0_attn_Wo, L0_attn_bo, L0_attn_q_norm_w, L0_attn_k_norm_w), axis=-1)
    x = _layernorm(x + _L0_ffn_ref(x, L0_ffn_w1, L0_ffn_b1, L0_ffn_w2, L0_ffn_b2), axis=-1)
    x = _layernorm(x + _L1_attn_ref(x, L1_attn_Wxproj, L1_attn_Winproj, L1_attn_Woutproj, L1_attn_conv_w, L1_attn_conv_b, L1_attn_A_log, L1_attn_D), axis=-1)
    x = _layernorm(x + _L1_ffn_ref(x, L1_ffn_w_gate, L1_ffn_w_up, L1_ffn_w_down), axis=-1)
    x = _layernorm(x + _L2_attn_ref(x, L2_attn_Wq, L2_attn_bq, L2_attn_Wk, L2_attn_bk, L2_attn_Wv, L2_attn_bv), axis=-1)
    x = _layernorm(x + _L2_ffn_ref(x, L2_ffn_Wa, L2_ffn_Wp, L2_ffn_w_std, L2_ffn_w_rec), axis=-1)
    x = _layernorm(x + _L3_attn_ref(x, L3_attn_q_proj, L3_attn_k_proj, L3_attn_v_proj, L3_attn_o_proj, L3_attn_q_norm, L3_attn_k_norm), axis=-1)
    x = _layernorm(x + _L3_ffn_ref(x, L3_ffn_gate_w, L3_ffn_shared_gate_w, L3_ffn_shared_gate_up_w, L3_ffn_shared_down_w, L3_ffn_w13, L3_ffn_w2), axis=-1)
    return x

_drawn_inputs = setup_inputs


def setup_inputs(seed=0):
    import zlib

    import numpy as np

    out = dict(_drawn_inputs(seed))
    spreads = {'L0_attn_bo': (0.0, 0.1),
     'L0_attn_q_norm_w': (1.0, 0.2),
     'L0_attn_k_norm_w': (1.0, 0.6),
     'L0_ffn_b1': (0.0, 0.406),
     'L0_ffn_b2': (0.0, 0.8),
     'L1_attn_D': (1.0, 0.2),
     'L2_attn_bq': (0.0, 0.1),
     'L2_attn_bk': (0.0, 0.1),
     'L2_attn_bv': (0.0, 0.1),
     'L3_attn_q_norm': (1.0, 0.6),
     'L3_attn_k_norm': (1.0, 0.6)}
    factors = {'L1_attn_Wxproj': 8.0,
     'L1_attn_Winproj': 8.0,
     'L1_attn_Woutproj': 8.0,
     'L1_attn_A_log': 8.0,
     'L2_ffn_w_std': 32.252,
     'L2_ffn_w_rec': 8.0,
     'L3_ffn_gate_w': 8.0,
     'L3_ffn_shared_gate_w': 8.0,
     'L3_ffn_shared_gate_up_w': 3.774,
     'L3_ffn_shared_down_w': 3.63,
     'L3_ffn_w13': 8.0,
     'L3_ffn_w2': 8.0}
    for name, (base, spread) in spreads.items():
        noise = np.random.default_rng([zlib.crc32(name.encode()), seed]).standard_normal(out[name].shape)
        drawn = base * np.exp(spread * noise) if base else spread * noise
        out[name] = jnp.asarray(drawn.astype(out[name].dtype))
    for name, factor in factors.items():
        out[name] = (out[name] * factor).astype(out[name].dtype)
    return out
```

```python
import math
from contextlib import ExitStack

import numpy as np

import concourse.bass as bass
from concourse import mybir

F32 = mybir.dt.float32
BF16 = mybir.dt.bfloat16
ALU = mybir.AluOpType
ACT = mybir.ActivationFunctionType
AX = mybir.AxisListType

B, T, C = 4, 1024, 256
P = 128
NT = T // P
KC = C // P
CH = 512
NCH = T // CH
FF = 1024
NF = FF // P
TERMS = 6
NEG = -1.0e30
E50 = math.exp(-50.0)
RH = 8
RD = C // RH
SS = 64
NE, EI = 8, 176
EREM = EI - P
ECOL = 2 * P + 64 + EREM
SI = 704
NSF = (SI + P - 1) // P
LN_EPS = 1e-5


class Links:

    def __init__(self, eng, sem, clear=False):
        self.eng, self.sem, self.n = eng, sem, 0
        if clear:
            eng.sem_clear(sem)

    def __call__(self, ins):
        self.n += 1
        ins.then_inc(self.sem, 1)
        self.eng.wait_ge(self.sem, self.n)


class Core:

    def __init__(self, nc):
        self.nc, self.sems = nc, []

    def __enter__(self):
        self.ctx = ExitStack()
        self.ctx.__enter__()
        return self

    def sem(self, name):
        s = self.ctx.enter_context(self.nc.semaphore(name))
        self.sems.append(s)
        return s

    def __exit__(self, *raised):
        if raised[0] is None:
            for s in self.sems:
                self.nc.sync.sem_clear(s)
            self.nc.all_engine_barrier()
        return self.ctx.__exit__(*raised)


def heads_view(ap, n):
    return ap.rearrange("p t (h d) -> p t h d", h=n)


def project_tokens(nc, core, name, XT, W, outs):
    done, free = core.sem(name + "_projected"), core.sem(name + "_taken")
    cols = W.shape[2]
    parts = [(a, min(a + 512, cols)) for a in range(0, cols, 512)]
    with ExitStack() as c:
        ps = [c.enter_context(nc.psum_tensor(f"{name}_ps{i}", [P, 512], F32)) for i in range(4)]
        with nc.Block() as block:
            @block.tensor
            def _(pe):
                n = 0
                for t in range(NT):
                    for a, e in parts:
                        if n >= 4:
                            pe.wait_ge(free, n - 3)
                        for k in range(KC):
                            last = nc.tensor.matmul(ps[n % 4][:, 0:e - a], XT[:, k, t * P:(t + 1) * P],
                                                    W[:, k, a:e], start=(k == 0), stop=(k == KC - 1))
                        last.then_inc(done, 1)
                        n += 1

            @block.scalar
            def _(act):
                n = 0
                for t in range(NT):
                    for a, e in parts:
                        act.wait_ge(done, n + 1)
                        pieces = [(max(a, u), min(e, v), f, u) for u, v, f in outs if max(a, u) < min(e, v)]
                        for j, (u, v, f, base) in enumerate(pieces):
                            src = ps[n % 4][:, u - a:v - a]
                            dst = f(t, u - base, v - base)
                            if len(dst.shape) == 3:
                                src = src.rearrange("p (h d) -> p h d", d=dst.shape[2])
                            ins = nc.scalar.activation(dst, src, ACT.Copy)
                            if j == len(pieces) - 1:
                                ins.then_inc(free, 1)
                        n += 1


def norm_rope(nc, core, name, QK, nh, D, wtab, cosd, sind, eps_in):
    ss_done, root_done, link = core.sem(name + "_ss"), core.sem(name + "_root"), core.sem(name + "_v")
    g_link, g_done = core.sem(name + "_g"), core.sem(name + "_turned")
    h2 = D // 2
    with ExitStack() as c:
        SQ = c.enter_context(nc.sbuf_tensor(name + "_sq", [P, NT, nh * D], F32))
        R = c.enter_context(nc.sbuf_tensor(name + "_rms", [P, NT, nh], F32))
        q4 = QK[:, :, :].rearrange("p t (h d) -> p t h d", d=D)
        s4 = SQ[:, :, :].rearrange("p t (h d) -> p t h d", d=D)
        with nc.Block() as block:
            @block.vector
            def _(dve):
                link_ = Links(dve, link)
                link_(nc.vector.tensor_tensor(SQ[:, :, :], QK[:, :, :], QK[:, :, :], ALU.mult))
                link_(nc.vector.tensor_reduce(R[:, :, :], s4, AX.X, ALU.add))
                nc.vector.tensor_scalar(R[:, :, :], R[:, :, :], 1.0 / D, 1e-6 if eps_in else 0.0,
                                        ALU.mult, ALU.add).then_inc(ss_done, 1)
                dve.wait_ge(root_done, 1)
                if not eps_in:
                    link_(nc.vector.tensor_scalar(R[:, :, :], R[:, :, :], 1e-6, None, ALU.add))
                link_(nc.vector.reciprocal(R[:, :, :], R[:, :, :]))
                link_(nc.vector.tensor_tensor(q4, q4, R[:, :, :].unsqueeze(3).broadcast_to([P, NT, nh, D]), ALU.mult))
                link_(nc.vector.tensor_tensor(QK[:, :, :], QK[:, :, :],
                                              wtab.unsqueeze(1).broadcast_to([P, NT, nh * D]), ALU.mult))
                for half in range(2):
                    link_(nc.vector.tensor_tensor(
                        s4[:, :, :, half * h2:(half + 1) * h2], q4[:, :, :, (1 - half) * h2:(2 - half) * h2],
                        sind[:, :, half, :].unsqueeze(2).broadcast_to([P, NT, nh, h2]), ALU.mult))
                for half in range(2):
                    v = q4[:, :, :, half * h2:(half + 1) * h2]
                    link_(nc.vector.tensor_tensor(
                        v, v, cosd.unsqueeze(2).broadcast_to([P, NT, nh, h2]), ALU.mult))
                link_(nc.vector.tensor_tensor(QK[:, :, :], QK[:, :, :], SQ[:, :, :], ALU.add))

            @block.scalar
            def _(act):
                act.wait_ge(ss_done, 1)
                nc.scalar.activation(R[:, :, :], R[:, :, :], ACT.Sqrt).then_inc(root_done, 1)


def attention(nc, core, name, QK, V, Y, consts, *, D, NH, q0, k0, kv_of, kper, cap, scale, SV, e50, U):
    NSUB = TERMS * D // 96
    ROWS = 96
    CAPB = 12 if cap else 8
    SB = CAPB // 4
    blocks = [(kb, qb) for kb in range(NT) for qb in range(kb, NT)]
    SEG = [blocks[a:a + CAPB] for a in range(0, len(blocks), CAPB)]
    NS = len(SEG)
    GW = 32 if D < 32 else 64
    NG = P // GW
    NSL = NT // NG
    place = tile_places(NG)
    caster = "dve" if cap else "act"
    kx = not cap
    KR = ROWS + 3 if kx else ROWS
    chunks = [(qb, a, min(a + 4, qb + 1)) for qb in range(NT) for a in range(0, qb + 1, 4)]
    NC = len(chunks)
    PERG = (2 if kper else 1) * NSUB
    TB0 = 0 if kper else NSUB
    S = lambda n: core.sem(f"{name}_{n}")
    q_stacked, k_stacked, v_ready, pool_link = S("q_stacked"), S("k_stacked"), S("v_ready"), S("pool")
    turned, untangled = S("turned"), S("untangled")
    s_ready, tanh_done, exp_done, pv_done = S("s_ready"), S("tanh"), S("exp"), S("pv")
    y_ready, y_done = S("y_ready"), S("y_done")
    mx_ready, mx_taken, m_split, m_turned, m_placed, vlink = (
        S("mx_ready"), S("mx_taken"), S("m_split"), S("m_turned"), S("m_placed"), S("v"))
    ones_set, v_set, k_cast, cast, cast_held = S("ones"), S("v_set"), S("k_cast"), S("cast"), S("cast_held")
    o_taken, o_turned, held = S("o_taken"), S("o_turned"), S("pool_held")
    ident, identf, negq, negk = consts
    with ExitStack() as c:
        def sb(n, shape, dt):
            return c.enter_context(nc.sbuf_tensor(f"{name}_{n}", shape, dt))

        def pb(n, shape, dt):
            return c.enter_context(nc.psum_tensor(f"{name}_{n}", shape, dt))

        Qs = sb("Qs", [P, 2, NT, NSUB * ROWS], BF16)
        nks = 2 if kper else 1
        Ks = sb("Ks", [P, nks, NT, NSUB * ROWS], BF16)
        RQ = sb("RQ", [P, NT, D], F32)
        QT = sb("QT", [P, 2, NSUB, T], BF16)
        KT = sb("KT", [P, nks, NSUB, T], BF16)
        Vh = sb("Vh", [P, 4, NT, GW], F32) if kper else sb("Vh", [P, 1, NT, GW], F32)
        SVh = sb("SVh", [P, 4, NT - 1, GW], F32) if cap else None
        OT = sb("OT", [P, NSL * P], F32)
        Pb = [sb(f"P{i}", [P, CAPB * P], F32) for i in range(2)]
        Tb = [sb(f"T{i}", [P, CAPB * P], F32) for i in range(2)] if cap else None
        RC = sb("RC", [P, NSL, NG], F32)
        if kx:
            MX = sb("MX", [P, NT, 2], F32)
            M1 = sb("M1", [P, NT], F32)
            M2 = sb("M2", [P, NT], F32)
            MS = sb("MS", [P, NT, 3], BF16)
            S1 = [pb(f"S1{i}", [P, 512], F32) for i in range(2)]
        Sp = [pb(f"S{i}", [P, SB * 512], F32) for i in range(2)]
        TP = pb("TP", [P, T], BF16)
        O = pb("O", [P, NSL * P], F32)
        TO = TP[:, :].bitcast(F32)[:, 0:NSL * P]
        tov = TO.rearrange("p (s g w) -> p s g w", s=NSL, g=NG)
        qst = Qs[:, :, :, :].rearrange("p b t (j d) -> p b t j d", d=D)
        kst = Ks[:, :, :, :].rearrange("p b t (j d) -> p b t j d", d=D)

        def qsrc(i, u):
            return QK[:, :, bass.ds(q0 + (i * U + u) * D, D)]

        def ksrc(i, u):
            return QK[:, :, bass.ds(k0 + kv_of(i, u) * D, D)]

        def cast_head(eng, copy, i, u, n):
            if late(n, 2):
                eng.wait_ge(turned, tuses(i, u) - PERG)
                eng.sem_inc(cast_held, 1)
            b = u % 2
            copy(qst[:, b, :, 0:4:3, :], qsrc(i, u).unsqueeze(2).broadcast_to([P, NT, 2, D]))
            last = copy(qst[:, b, :, 5, :], qsrc(i, u))
            if kper:
                last = copy(kst[:, b, :, 0:3, :], ksrc(i, u).unsqueeze(2).broadcast_to([P, NT, 3, D]))
            last.then_inc(cast, 1)

        def tuses(i, u):
            return i * (U * PERG) + u * PERG + TB0

        def at(i, u, d):
            return i + (u + d) // U, (u + d) % U

        def run(eng, head):
            for u in range(U):
                head(0, u, u)
            if NH // U > 2:
                with eng.Fori(1, NH // U - 1) as i:
                    for u in range(U):
                        head(i, u, None)
            for u in range(U):
                head(NH // U - 1, u, NH - U + u)

        def late(n, k):
            return n is None or n >= k

        def more(n, k):
            return n is None or n + k < NH

        with nc.Block() as block:
            @block.gpsimd
            def _(pool):
                def split_q(i, u, links):
                    st, two = qst[:, u % 2], [P, NT, 2, D]
                    links(nc.gpsimd.tensor_tensor(RQ[:, :, :], qsrc(i, u), st[:, :, 0, :], ALU.subtract))
                    links(nc.gpsimd.tensor_copy(st[:, :, 1:5:3, :], RQ[:, :, :].unsqueeze(2).broadcast_to(two)))
                    links(nc.gpsimd.tensor_tensor(st[:, :, 2, :], RQ[:, :, :], st[:, :, 1, :], ALU.subtract))

                def split_k(i, u, links, b):
                    st, two = kst[:, b], [P, NT, 2, D]
                    links(nc.gpsimd.tensor_tensor(RQ[:, :, :], ksrc(i, u), st[:, :, 0, :], ALU.subtract))
                    links(nc.gpsimd.tensor_copy(st[:, :, 3:5, :], RQ[:, :, :].unsqueeze(2).broadcast_to(two)))
                    links(nc.gpsimd.tensor_tensor(st[:, :, 5, :], RQ[:, :, :], st[:, :, 3, :], ALU.subtract))

                links = Links(pool, pool_link)
                links(nc.gpsimd.memset(Vh[:, :, :, :], 1.0))
                if cap:
                    for qb in range(NT - 1):
                        links(nc.gpsimd.memset(SVh[:, :, qb, :], float(NT - 1 - qb)))
                if not kper:
                    links(nc.gpsimd.tensor_copy(Vh[:, 0, :, 0:D], V[:, :, :]))
                    pool.sem_inc(v_set, 1)
                    pool.wait_ge(k_cast, 1)
                    split_k(0, 0, links, 0)
                    pool.sem_inc(k_stacked, 1)

                def head(i, u, n):
                    links = Links(pool, pool_link, clear=True)
                    pool.wait_ge(cast, i * U + u + 1)
                    pool.sem_inc(held, 1)
                    if kper:
                        split_k(i, u, links, u % 2)
                    split_q(i, u, links)
                    pool.sem_inc(q_stacked, 1)
                    if kper:
                        if late(n, 4):
                            pool.wait_ge(pv_done, (i * U + u - 3) * NS)
                            pool.sem_inc(held, 1)
                        g = kv_of(i, u)
                        links(nc.gpsimd.tensor_copy(Vh[:, u, :, 0:D], V[:, :, bass.ds(g * D, D)]))
                        if cap:
                            links(nc.gpsimd.tensor_copy(SVh[:, u, :, 0:D], SV[:, :, bass.ds(g * D, D)]))
                        pool.sem_inc(v_set, 1)
                run(pool, head)

            @block.tensor
            def _(pe):
                def turn(stk, use):
                    for j in range(NSUB):
                        if not isinstance(use, int) or use + j >= 1:
                            pe.wait_ge(untangled, use + j)
                        for t in range(NT):
                            last = nc.tensor.transpose(TP[0:ROWS, t * P:(t + 1) * P],
                                                       stk[:, t, j * ROWS:(j + 1) * ROWS], ident[:, :])
                        last.then_inc(turned, 1)

                def turn_head(i, u):
                    pe.wait_ge(q_stacked, i * U + u + 1)
                    if kper:
                        turn(Ks[:, u % 2], tuses(i, u))
                    turn(Qs[:, u % 2], tuses(i, u) + (NSUB if kper else 0))

                def scores(i, u, s):
                    g = (i * U + u) * NS + s
                    if s == 0:
                        pe.wait_ge(untangled, tuses(i, u) + PERG)
                        if kx:
                            pe.wait_ge(m_placed, i * U + u + 1)
                    if not (isinstance(g, int) and g < 2):
                        pe.wait_ge(tanh_done if cap else exp_done, g - 1)
                    seg, a = SEG[s], 0
                    while a < len(seg):
                        kb, qb = seg[a]
                        w = 1
                        while a + w < len(seg) and (a + w) % 4 and seg[a + w][0] == kb:
                            w += 1
                        dst = Sp[(u * NS + s) % 2][:, a * P:(a + w) * P]
                        diag = qb == kb
                        first = True
                        for j in range(NSUB):
                            r = KR if j == 0 else ROWS
                            end = j == NSUB - 1
                            last = nc.tensor.matmul(
                                dst, KT[0:r, (u % 2) if kper else 0, j, kb * P:(kb + 1) * P],
                                QT[0:r, u % 2, j, qb * P:(qb + w) * P], start=first, stop=end,
                                skip_group_check=True)
                            first = False
                        if diag:
                            last = nc.tensor.matmul(dst[:, 0:P], ident[:, :], negk[:, :], start=False,
                                                    stop=True, skip_group_check=True)
                        a += w
                    last.then_inc(s_ready, 1)

                def maxima(i, u, cs):
                    for ci in cs:
                        qb, a, e = chunks[ci]
                        n = (i * U + u) * NC + ci
                        if ci == 0:
                            pe.wait_ge(untangled, tuses(i, u) + PERG)
                        if not (isinstance(n, int) and n < 2):
                            pe.wait_ge(mx_taken, n - 1)
                        dst = S1[(u * NC + ci) % 2][:, 0:(e - a) * P]
                        for j in range(NSUB):
                            last = nc.tensor.matmul(dst, QT[0:ROWS, u % 2, j, qb * P:(qb + 1) * P],
                                                    KT[0:ROWS, (u % 2) if kper else 0, j, a * P:e * P],
                                                    start=(j == 0), stop=(j == NSUB - 1), skip_group_check=True)
                        if e == qb + 1:
                            last = nc.tensor.matmul(dst[:, (e - a - 1) * P:(e - a) * P], ident[:, :], negq[:, :],
                                                    start=False, stop=True, skip_group_check=True)
                        last.then_inc(mx_ready, 1)

                def turn_maxima(i, u):
                    pe.wait_ge(m_split, i * U + u + 1)
                    if not (isinstance(i, int) and i * U + u < 1):
                        pe.wait_ge(m_placed, i * U + u)
                    for qb in range(NT):
                        last = nc.tensor.transpose(TP[ROWS:ROWS + 3, qb * P:(qb + 1) * P], MS[:, qb, :],
                                                   ident[:, :], tile_position=(0, ROWS))
                    last.then_inc(m_turned, 1)

                def weigh(i, u, s):
                    g = (i * U + u) * NS + s
                    n = i * U + u
                    pe.wait_ge(exp_done, g + 1)
                    vv = Vh[:, u if kper else 0]
                    todo = []
                    if s == 0:
                        pe.wait_ge(v_set, n + 1 if kper else 1)
                        if not (isinstance(n, int) and n < 1):
                            pe.wait_ge(o_taken, n)
                        if cap:
                            todo += [(qb, SVh[:, u, qb, :], e50[:, :]) for qb in range(NT - 1)]
                    todo += [(qb, vv[:, kb, :], Pb[(u * NS + s) % 2][:, x * P:(x + 1) * P])
                             for x, (kb, qb) in enumerate(SEG[s])]
                    byg = [[m for m in todo if place[m[0]][1] == gr] for gr in range(NG)]
                    rounds = max(len(x) for x in byg)
                    for r in range(rounds):
                        for gr in range(NG):
                            if r < len(byg[gr]):
                                qb, v, p = byg[gr][r]
                                sl = place[qb][0]
                                last = nc.tensor.matmul(O[gr * GW:(gr + 1) * GW, sl * P:(sl + 1) * P], v, p,
                                                        start=(s == 0 and r == 0), stop=True,
                                                        skip_group_check=True)
                    last.then_inc(pv_done, 1)

                def turn_out(i, u):
                    n = i * U + u
                    pe.wait_ge(o_taken, n + 1)
                    for sl in range(NSL):
                        last = nc.tensor.transpose(TO[:, sl * P:(sl + 1) * P], OT[:, sl * P:(sl + 1) * P],
                                                   identf[:, :])
                    last.then_inc(o_turned, 1)

                if kx:
                    pe.wait_ge(ones_set, 1)
                if not kper:
                    pe.wait_ge(k_stacked, 1)
                    turn(Ks[:, 0], 0)
                turn_head(0, 0)
                turn_head(0, 1)
                if kx:
                    maxima(0, 0, range(NC))
                    turn_maxima(0, 0)

                def head(i, u, n):
                    for s in range(NS):
                        scores(i, u, s)
                        if kx and s < 4 and more(n, 1):
                            maxima(*at(i, u, 1), range(3 * s, 3 * s + 3))
                        if s == 2 and late(n, 1):
                            ii, uu = at(i, u, 1)
                            if more(n, 1):
                                pe.wait_ge(untangled, tuses(ii, uu) + PERG)
                            turn_out(*((i, u - 1) if u else (i - 1, U - 1)))
                        if s == NS - 1:
                            if late(n, 1):
                                pe.wait_ge(y_done, i * U + u)
                            if kx and more(n, 1):
                                turn_maxima(*at(i, u, 1))
                            if more(n, 2):
                                turn_head(*at(i, u, 2))
                        if s >= 2:
                            weigh(i, u, s - 2)
                        elif late(n, 1):
                            ii, uu = (i, u - 1) if u else (i - 1, U - 1)
                            weigh(ii, uu, NS - 2 + s)
                run(pe, head)
                weigh(NH // U - 1, U - 1, NS - 2)
                weigh(NH // U - 1, U - 1, NS - 1)
                turn_out(NH // U - 1, U - 1)

            @block.scalar
            def _(act):
                def squash(i, u, s):
                    g = (i * U + u) * NS + s
                    act.wait_ge(s_ready, g + 1)
                    if not (isinstance(g, int) and g < 2):
                        act.wait_ge(exp_done, g - 1)
                    w = len(SEG[s]) * P
                    b = (u * NS + s) % 2
                    nc.scalar.activation(Tb[b][:, 0:w], Sp[b][:, 0:w], ACT.Tanh,
                                         scale=scale / 50.0).then_inc(tanh_done, 1)

                def expo(i, u, s):
                    g = (i * U + u) * NS + s
                    act.wait_ge(tanh_done if cap else s_ready, g + 1)
                    if not (isinstance(g, int) and g < 2):
                        act.wait_ge(pv_done, g - 1)
                    w = len(SEG[s]) * P
                    b = (u * NS + s) % 2
                    src = Tb[b] if cap else Sp[b]
                    nc.scalar.activation(Pb[b][:, 0:w], src[:, 0:w], ACT.Exp,
                                         scale=50.0 if cap else scale).then_inc(exp_done, 1)

                def place_maxima(i, u):
                    act.wait_ge(m_turned, i * U + u + 1)
                    nc.scalar.activation(QT[ROWS:ROWS + 3, u % 2, 0, :], TP[ROWS:ROWS + 3, :],
                                         ACT.Copy).then_inc(m_placed, 1)
                copy = lambda o, x: nc.scalar.activation(o, x, ACT.Copy)
                if not cap:
                    if not kper:
                        copy(kst[:, 0, :, 0:3, :], ksrc(0, 0).unsqueeze(2).broadcast_to([P, NT, 3, D])) \
                            .then_inc(k_cast, 1)
                    cast_head(act, copy, 0, 0, 0)
                    cast_head(act, copy, 0, 1, 1)
                if kx:
                    place_maxima(0, 0)

                def head(i, u, n):
                    if not cap and more(n, 2):
                        cast_head(act, copy, *at(i, u, 2), None)
                    for s in range(NS):
                        if cap:
                            squash(i, u, s)
                            if s:
                                expo(i, u, s - 1)
                            elif late(n, 1):
                                ii, uu = (i, u - 1) if u else (i - 1, U - 1)
                                expo(ii, uu, NS - 1)
                        else:
                            expo(i, u, s)
                    if kx and more(n, 1):
                        place_maxima(*at(i, u, 1))
                run(act, head)
                if cap:
                    expo(NH // U - 1, U - 1, NS - 1)

            @block.vector
            def _(dve):
                if kx:
                    for b in range(nks):
                        nc.vector.memset(KT[ROWS:ROWS + 3, b, 0, :], 1.0)
                    nc.vector.memset(MX[:, :, :], -3.0e38).then_inc(ones_set, 1)
                    dve.wait_ge(ones_set, 1)

                def untangle(dst, use):
                    for j in range(NSUB):
                        dve.wait_ge(turned, use + j + 1)
                        nc.vector.tensor_copy(dst[0:ROWS, j, :], TP[0:ROWS, :]).then_inc(untangled, 1)

                def untangle_head(i, u):
                    if kper:
                        untangle(KT[:, u % 2], tuses(i, u))
                    untangle(QT[:, u % 2], tuses(i, u) + (NSUB if kper else 0))

                def maxima(i, u, cs):
                    for ci in cs:
                        qb, a, e = chunks[ci]
                        n = (i * U + u) * NC + ci
                        dve.wait_ge(mx_ready, n + 1)
                        nc.vector.tensor_reduce(MX[:, qb, (a // 4):(a // 4) + 1],
                                                S1[(u * NC + ci) % 2][:, 0:(e - a) * P], AX.X,
                                                ALU.max).then_inc(mx_taken, 1)

                def split_maxima(i, u):
                    n = i * U + u
                    links = Links(dve, vlink, clear=True)
                    dve.wait_ge(mx_taken, (n + 1) * NC)
                    links(nc.vector.tensor_reduce(M1[:, :], MX[:, :, :], AX.X, ALU.max))
                    if not (isinstance(n, int) and n < 1):
                        dve.wait_ge(m_turned, n)
                    links(nc.vector.tensor_scalar(MS[:, :, 0], M1[:, :], -1.0, None, ALU.mult))
                    links(nc.vector.scalar_tensor_tensor(M2[:, :], M1[:, :], -1.0, MS[:, :, 0],
                                                         ALU.mult, ALU.subtract))
                    links(nc.vector.tensor_copy(MS[:, :, 1], M2[:, :]))
                    links(nc.vector.tensor_tensor(MS[:, :, 2], M2[:, :], MS[:, :, 1], ALU.subtract))
                    dve.sem_inc(m_split, 1)

                def take_out(i, u):
                    n = i * U + u
                    dve.wait_ge(pv_done, (n + 1) * NS)
                    if not (isinstance(n, int) and n < 1):
                        dve.wait_ge(o_turned, n)
                    nc.vector.tensor_copy(OT[:, :], O[:, :]).then_inc(o_taken, 1)

                def divide(i, u):
                    n = i * U + u
                    dve.wait_ge(o_turned, n + 1)
                    if not (isinstance(n, int) and n < 1):
                        dve.wait_ge(y_done, n)
                    nc.vector.reciprocal(RC[:, :, :], tov[:, :, :, D]).then_inc(y_ready, 1)
                    dve.wait_ge(y_ready, n + 1)
                    nc.vector.tensor_tensor(Y[:, :, bass.ds(n * D, D)].rearrange("p (s g) d -> p s g d", g=NG),
                                            tov[:, :, :, 0:D],
                                            RC[:, :, :].unsqueeze(3).broadcast_to([P, NSL, NG, D]),
                                            ALU.mult).then_inc(y_done, 1)
                copy = lambda o, x: nc.vector.tensor_copy(o, x)
                if cap:
                    cast_head(dve, copy, 0, 0, 0)
                    cast_head(dve, copy, 0, 1, 1)
                if not kper:
                    untangle(KT[:, 0], 0)
                untangle_head(0, 0)
                untangle_head(0, 1)
                if kx:
                    maxima(0, 0, range(NC))
                    split_maxima(0, 0)

                def head(i, u, n):
                    before = (i, u - 1) if u else (i - 1, U - 1)
                    if cap and more(n, 2):
                        cast_head(dve, copy, *at(i, u, 2), None)
                    if kx and more(n, 1):
                        maxima(*at(i, u, 1), range(0, 6))
                    if late(n, 1):
                        take_out(*before)
                    if kx and more(n, 1):
                        maxima(*at(i, u, 1), range(6, 9))
                    if late(n, 1):
                        divide(*before)
                    if kx and more(n, 1):
                        maxima(*at(i, u, 1), range(9, NC))
                        split_maxima(*at(i, u, 1))
                    if more(n, 2):
                        untangle_head(*at(i, u, 2))
                run(dve, head)
                take_out(NH // U - 1, U - 1)
                divide(NH // U - 1, U - 1)


def tile_places(NG):
    if NG == 4:
        order = [0, 1, 2, 3, 7, 6, 5, 4]
    else:
        order = [0, 1, 3, 2, 4, 5, 7, 6]
    return {t: (x // NG, x % NG) for x, t in enumerate(order)}


def turn_tokens(nc, core, name, Y, YT, identf, NG):
    done, free = core.sem(name + "_turned"), core.sem(name + "_taken")
    at = {t: s * NG + g for t, (s, g) in tile_places(NG).items()}
    with ExitStack() as c:
        ps = [c.enter_context(nc.psum_tensor(f"{name}_ps{i}", [P, C], F32)) for i in range(4)]
        with nc.Block() as block:
            @block.tensor
            def _(pe):
                for t in range(NT):
                    if t >= 4:
                        pe.wait_ge(free, t - 3)
                    for k in range(KC):
                        last = nc.tensor.transpose(ps[t % 4][:, k * P:(k + 1) * P], Y[:, at[t], k * P:(k + 1) * P],
                                                   identf[:, :])
                    last.then_inc(done, 1)

            @block.vector
            def _(dve):
                for t in range(NT):
                    dve.wait_ge(done, t + 1)
                    nc.vector.tensor_copy(YT[:, :, t * P:(t + 1) * P],
                                          ps[t % 4][:, :].rearrange("p (k n) -> p k n", k=KC)).then_inc(free, 1)


def close_layer(nc, core, name, X, XT, identf, product, gates=None, out=None):
    gates = gates or [None]
    NP = len(gates)
    S = lambda n: core.sem(f"{name}_{n}")
    made, added, link, var_done, root, scaled, normed, turned, taken, stored = (
        S("made"), S("added"), S("v"), S("var"), S("root"), S("scaled"), S("normed"), S("turned"), S("taken"),
        S("stored"))
    with ExitStack() as c:
        ps = [c.enter_context(nc.psum_tensor(f"{name}_ps{i}", [P, C], F32)) for i in range(4)]
        tp = [c.enter_context(nc.psum_tensor(f"{name}_tp{i}", [P, C], F32)) for i in range(4)]
        ST = c.enter_context(nc.sbuf_tensor(name + "_st", [P, NT, 6], F32))
        MV = c.enter_context(nc.sbuf_tensor(name + "_mv", [P, NT, 2], F32))
        RS = c.enter_context(nc.sbuf_tensor(name + "_rs", [P, NT], F32))
        NM = c.enter_context(nc.sbuf_tensor(name + "_nm", [P, NT], F32))
        with nc.Block() as block:
            @block.tensor
            def _(pe):
                n = 0
                for t in range(NT):
                    for j in range(NP):
                        if n >= 4:
                            pe.wait_ge(added, n - 3)
                        mms = list(product(t, j))
                        for m, (lhsT, rhs, cols) in enumerate(mms):
                            last = nc.tensor.matmul(ps[n % 4][:, cols[0]:cols[1]], lhsT, rhs, start=(m == 0),
                                                    stop=(m == len(mms) - 1), skip_group_check=True)
                        last.then_inc(made, 1)
                        n += 1
                if out is None:
                    for t in range(NT):
                        pe.wait_ge(normed, t + 1)
                        if t >= 4:
                            pe.wait_ge(taken, t - 3)
                        for k in range(KC):
                            last = nc.tensor.transpose(tp[t % 4][:, k * P:(k + 1) * P], X[:, t, k * P:(k + 1) * P],
                                                       identf[:, :])
                        last.then_inc(turned, 1)

            @block.vector
            def _(dve):
                links = Links(dve, link)
                n = 0
                for t in range(NT):
                    for j in range(NP):
                        dve.wait_ge(made, n + 1)
                        if n and j:
                            dve.wait_ge(added, n)
                        src = ps[n % 4][:, :]
                        if gates[j] is None:
                            nc.vector.tensor_tensor(X[:, t, :], X[:, t, :], src, ALU.add).then_inc(added, 1)
                        else:
                            nc.vector.scalar_tensor_tensor(X[:, t, :], src, gates[j](t), X[:, t, :],
                                                           ALU.mult, ALU.add).then_inc(added, 1)
                        n += 1
                    dve.wait_ge(added, n)
                    links(nc.vector.bn_stats(ST[:, t, :], X[:, t, :]))
                    links(nc.vector.bn_aggr(MV[:, t, :], ST[:, t, :]))
                nc.vector.tensor_scalar(RS[:, :], MV[:, :, 1], LN_EPS, None, ALU.add).then_inc(var_done, 1)
                dve.wait_ge(root, 1)
                links(nc.vector.reciprocal(RS[:, :], RS[:, :]))
                nc.vector.scalar_tensor_tensor(NM[:, :], MV[:, :, 0], -1.0, RS[:, :], ALU.mult,
                                               ALU.mult).then_inc(scaled, 1)
                if out is None:
                    for t in range(NT):
                        dve.wait_ge(turned, t + 1)
                        nc.vector.tensor_copy(XT[:, :, t * P:(t + 1) * P],
                                              tp[t % 4][:, :].rearrange("p (k n) -> p k n", k=KC)).then_inc(taken, 1)

            @block.scalar
            def _(act):
                act.wait_ge(var_done, 1)
                nc.scalar.activation(RS[:, :], RS[:, :], ACT.Sqrt).then_inc(root, 1)
                act.wait_ge(scaled, 1)
                for t in range(NT):
                    nc.scalar.activation(X[:, t, :], X[:, t, :], ACT.Identity, bias=NM[:, t:t + 1],
                                         scale=RS[:, t:t + 1]).then_inc(normed, 1)

            if out is not None:
                @block.sync
                def _(sp):
                    sp.wait_ge(normed, NT)
                    sp.dma_start(out, X[:, :, :]).then_inc(stored, 16)
                    sp.wait_ge(stored, 16)


def hidden_gelu(nc, core, name, XT, W, bias, H):
    made, done = core.sem(name + "_made"), core.sem(name + "_done")
    with ExitStack() as c:
        ps = [c.enter_context(nc.psum_tensor(f"{name}_ps{i}", [P, CH], F32)) for i in range(4)]
        order = [(f, h) for f in range(NF) for h in range(NCH)]
        with nc.Block() as block:
            @block.tensor
            def _(pe):
                for n, (f, h) in enumerate(order):
                    if n >= 4:
                        pe.wait_ge(done, n - 3)
                    for k in range(KC):
                        last = nc.tensor.matmul(ps[n % 4][:, :], W[:, k, f * P:(f + 1) * P],
                                                XT[:, k, h * CH:(h + 1) * CH], start=(k == 0), stop=(k == KC - 1))
                    last.then_inc(made, 1)

            @block.scalar
            def _(act):
                for n, (f, h) in enumerate(order):
                    act.wait_ge(made, n + 1)
                    nc.scalar.activation(H[:, f, h * CH:(h + 1) * CH], ps[n % 4][:, :], ACT.Gelu,
                                         bias=bias[:, f:f + 1]).then_inc(done, 1)


def hidden_swiglu(nc, core, name, XT, items):
    gate_made, gate_done, up_done = core.sem(name + "_gmade"), core.sem(name + "_gdone"), core.sem(name + "_udone")
    with ExitStack() as c:
        pg = [c.enter_context(nc.psum_tensor(f"{name}_pg{i}", [P, CH], F32)) for i in range(4)]
        pu = [c.enter_context(nc.psum_tensor(f"{name}_pu{i}", [P, CH], F32)) for i in range(4)]
        G = [c.enter_context(nc.sbuf_tensor(f"{name}_g{i}", [P, CH], F32)) for i in range(2)]
        order = [(it, h) for it in items for h in range(NCH)]
        with nc.Block() as block:
            @block.tensor
            def _(pe):
                for n, ((gw, uw, rows, urow, M, dst), h) in enumerate(order):
                    if n >= 4:
                        pe.wait_ge(up_done, n - 3)
                    for k in range(KC):
                        last = nc.tensor.matmul(pg[n % 4][0:M, :], gw(k), XT[:, k, h * CH:(h + 1) * CH],
                                                start=(k == 0), stop=(k == KC - 1))
                    if uw is not None:
                        for k in range(KC):
                            last = nc.tensor.matmul(pu[n % 4][0:rows, :], uw(k), XT[:, k, h * CH:(h + 1) * CH],
                                                    start=(k == 0), stop=(k == KC - 1))
                    last.then_inc(gate_made, 1)

            @block.scalar
            def _(act):
                for n, ((gw, uw, rows, urow, M, dst), h) in enumerate(order):
                    act.wait_ge(gate_made, n + 1)
                    if n >= 2:
                        act.wait_ge(up_done, n - 1)
                    nc.scalar.activation(G[n % 2][0:rows, :], pg[n % 4][0:rows, :], ACT.Silu).then_inc(gate_done, 1)

            @block.vector
            def _(dve):
                for n, ((gw, uw, rows, urow, M, dst), h) in enumerate(order):
                    dve.wait_ge(gate_done, n + 1)
                    up = pu[n % 4][0:rows, :] if uw is not None else pg[n % 4][urow:urow + rows, :]
                    nc.vector.tensor_tensor(dst(h), G[n % 2][0:rows, :], up, ALU.mult).then_inc(up_done, 1)


def scan_mixer(nc, core, name, XT, W1X, W1IN, CW, CB, NA, XC, HM):
    S = lambda n: core.sem(f"{name}_{n}")
    conv, made, spd, da, bu, hm, vl, al = (S("conv"), S("made"), S("softplus"), S("decay"), S("bu"), S("hm"),
                                           S("v"), S("a"))
    with ExitStack() as c:
        ps = [c.enter_context(nc.psum_tensor(f"{name}_ps{i}", [SS, CH], F32)) for i in range(8)]

        def sb(n):
            return c.enter_context(nc.sbuf_tensor(f"{name}_{n}", [SS, CH], F32))

        AB, EX, DL, DA, BU = ([sb(f"{n}{h}") for h in range(NCH)] for n in ("ab", "ex", "dl", "da", "bu"))
        HS = [sb(f"hs{h}") for h in range(NCH)]
        with nc.Block() as block:
            @block.tensor
            def _(pe):
                for h in range(NCH):
                    for w in range(3):
                        for k in range(KC):
                            last = nc.tensor.matmul(ps[4 * h + w][:, :], W1X[:, k, w * SS:(w + 1) * SS],
                                                    XT[:, k, h * CH:(h + 1) * CH], start=(k == 0), stop=(k == KC - 1))
                    last.then_inc(made, 1)
                pe.wait_ge(conv, KC)
                for h in range(NCH):
                    for k in range(KC):
                        last = nc.tensor.matmul(ps[4 * h + 3][:, :], W1IN[:, k, :], XC[:, k, h * CH:(h + 1) * CH],
                                                start=(k == 0), stop=(k == KC - 1))
                    last.then_inc(made, 1)

            @block.vector
            def _(dve):
                links = Links(dve, vl)
                for k in range(KC):
                    links(nc.vector.tensor_scalar(XC[:, k, :], XT[:, k, :], CW[:, k, 3:4], CB[:, k:k + 1],
                                                  ALU.mult, ALU.add))
                    for j in range(1, 4):
                        ins = nc.vector.scalar_tensor_tensor(
                            XC[:, k, j:T], XT[:, k, 0:T - j], CW[:, k, 3 - j:4 - j], XC[:, k, j:T],
                            ALU.mult, ALU.add)
                        if j < 3:
                            links(ins)
                    ins.then_inc(conv, 1)
                for h in range(NCH):
                    dve.wait_ge(al, 3 * h + 3)
                    nc.vector.scalar_tensor_tensor(DL[h][:, :], ps[4 * h][:, :], 0.0, EX[h][:, :], ALU.max,
                                                   ALU.add).then_inc(spd, 1)
                dve.wait_ge(made, 4)
                for h in range(NCH):
                    dve.wait_ge(spd, h + 1)
                    links(nc.vector.tensor_tensor(BU[h][:, :], DL[h][:, :], ps[4 * h + 1][:, :], ALU.mult))
                    links(nc.vector.tensor_tensor(BU[h][:, :], BU[h][:, :], ps[4 * h + 3][:, :], ALU.mult))
                    dve.wait_ge(da, h + 1)
                    init = 0.0 if h == 0 else HS[h - 1][:, CH - 1:CH]
                    links(nc.vector.tensor_tensor_scan(HS[h][:, :], DA[h][:, :], BU[h][:, :], init,
                                                       ALU.mult, ALU.add))
                    links(nc.vector.tensor_tensor(HM[:, h * CH:(h + 1) * CH], HS[h][:, :], ps[4 * h + 2][:, :],
                                                  ALU.mult))

            @block.scalar
            def _(act):
                links = Links(act, al)
                for h in range(NCH):
                    act.wait_ge(made, h + 1)
                    links(nc.scalar.activation(AB[h][:, :], ps[4 * h][:, :], ACT.Abs))
                    links(nc.scalar.activation(EX[h][:, :], AB[h][:, :], ACT.Exp, scale=-1.0))
                    links(nc.scalar.activation(EX[h][:, :], EX[h][:, :], ACT.Ln, bias=1.0))
                for h in range(NCH):
                    act.wait_ge(spd, h + 1)
                    nc.scalar.activation(DA[h][:, :], DL[h][:, :], ACT.Exp, scale=NA[0:SS, 0:1]).then_inc(da, 1)


def retention(nc, core, name, XT, W, WB, DT, CS, KVS, GC, BM, BV, X2):
    S = lambda n: core.sem(f"{name}_{n}")
    made, moved = S("made"), S("moved")
    vmade, vmoved = S("vmade"), S("vmoved")
    qs_done, ks_done = S("qs"), S("ks")
    sc, dec, outp, outd, st, stz, link = (S("scores"), S("decayed"), S("out"), S("out_taken"), S("state_made"),
                                          S("state_ready"), S("v"))
    with ExitStack() as c:
        def sb(n, shape):
            return c.enter_context(nc.sbuf_tensor(f"{name}_{n}", shape, F32))

        Q, K, QS = sb("q", [P, KC, T]), sb("k", [P, KC, T]), sb("qs", [P, KC, T])
        KV = sb("kv", [P, NT, 2 * C])
        AT = [sb(f"at{i}", [P, 4, P]) for i in range(2)]
        SD = sb("sd", [P, KC, P])
        TM = sb("tm", [P, P])
        ps = [c.enter_context(nc.psum_tensor(f"{name}_ps{i}", [P, 512], F32)) for i in range(4)]
        PO = c.enter_context(nc.psum_tensor(name + "_po", [P, C], F32))
        PS = [c.enter_context(nc.psum_tensor(f"{name}_pst{i}", [P, P], F32)) for i in range(2)]
        with nc.Block() as block:
            @block.tensor
            def _(pe):
                n = 0
                for w in range(2):
                    for m in range(KC):
                        for h in range(NCH):
                            if n >= 4:
                                pe.wait_ge(moved, n - 3)
                            for k in range(KC):
                                a = w * C + m * P
                                last = nc.tensor.matmul(ps[n % 4][:, :], W[:, k, a:a + P],
                                                        XT[:, k, h * CH:(h + 1) * CH], start=(k == 0),
                                                        stop=(k == KC - 1))
                            last.then_inc(made, 1)
                            n += 1
                for t in range(NT):
                    if t >= 4:
                        pe.wait_ge(vmoved, t - 3)
                    else:
                        pe.wait_ge(moved, 8 - 3 + t)
                    for k in range(KC):
                        last = nc.tensor.matmul(ps[t % 4][:, :], XT[:, k, t * P:(t + 1) * P], W[:, k, C:3 * C],
                                                start=(k == 0), stop=(k == KC - 1))
                    last.then_inc(vmade, 1)

            @block.scalar
            def _(act):
                n = 0
                for w in range(2):
                    for m in range(KC):
                        for h in range(NCH):
                            act.wait_ge(made, n + 1)
                            nc.scalar.activation((Q, K)[w][:, m, h * CH:(h + 1) * CH], ps[n % 4][:, :],
                                                 ACT.Identity, bias=WB[:, w * KC + m:w * KC + m + 1]).then_inc(moved, 1)
                            n += 1

            @block.vector
            def _(dve):
                links = Links(dve, link)
                nc.vector.memset(SD[:, :, :], 0.0).then_inc(stz, 1)
                for t in range(NT):
                    dve.wait_ge(vmade, t + 1)
                    nc.vector.tensor_tensor(KV[:, t, :], ps[t % 4][:, :], BV, ALU.add).then_inc(vmoved, 1)
                    dve.wait_ge(vmoved, t + 1)
                    nc.vector.tensor_tensor(KV[:, t, 0:C], KV[:, t, 0:C], KVS, ALU.mult).then_inc(ks_done, 1)

            @block.gpsimd
            def _(pool):
                pool.wait_ge(moved, 4)
                for m in range(KC):
                    nc.gpsimd.tensor_tensor(QS[:, m, :].rearrange("p (t i) -> p t i", i=P),
                                            Q[:, m, :].rearrange("p (t i) -> p t i", i=P),
                                            CS[:, m, :].unsqueeze(1).broadcast_to([P, NT, P]),
                                            ALU.mult).then_inc(qs_done, 1)
        with nc.Block() as block:
            @block.tensor
            def _(pe):
                def scores(t, m):
                    n = t * KC + m
                    if n >= 1:
                        pe.wait_ge(dec, n)
                    for i in range(4):
                        r = slice(32 * i, 32 * i + 32)
                        last = nc.tensor.matmul(ps[i][:, 0:P], K[r, m, t * P:(t + 1) * P], Q[r, m, t * P:(t + 1) * P],
                                                start=True, stop=True)
                        last.then_inc(sc, 1)
                scores(0, 0)
                for t in range(NT):
                    for m in range(KC):
                        n = t * KC + m
                        cols = slice(m * P, (m + 1) * P)
                        if t + 1 < NT:
                            if n >= 2:
                                pe.wait_ge(st, n - 1)
                            nc.tensor.matmul(PS[m][:, :], KV[:, t, m * P:(m + 1) * P],
                                             KV[:, t, C + m * P:C + (m + 1) * P], start=True,
                                             stop=True).then_inc(made, 1)
                        if m == 0 and t:
                            pe.wait_ge(outd, t)
                        pe.wait_ge(stz, n + 1 if t == 0 and m == 0 else max(1, n - 1))
                        nc.tensor.matmul(PO[:, cols], QS[:, m, t * P:(t + 1) * P], SD[:, m, :], start=True,
                                         stop=False, skip_group_check=True)
                        pe.wait_ge(dec, n + 1)
                        for i in range(4):
                            hc = m * P + i * RD
                            last = nc.tensor.matmul(PO[:, hc:hc + RD], AT[n % 2][:, i, :],
                                                    KV[:, t, C + hc:C + hc + RD], start=False, stop=True,
                                                    skip_group_check=True)
                        last.then_inc(outp, 1)
                        if n + 1 < NT * KC:
                            scores((n + 1) // KC, (n + 1) % KC)

            @block.vector
            def _(dve):
                links = Links(dve, link)
                for t in range(NT):
                    for m in range(KC):
                        n = t * KC + m
                        dve.wait_ge(sc, 4 * n + 4)
                        if n >= 2:
                            dve.wait_ge(outp, n - 1)
                        for i in range(4):
                            ins = nc.vector.tensor_tensor(AT[n % 2][:, i, :], ps[i][:, 0:P], DT[:, m * 4 + i, :],
                                                          ALU.mult)
                        ins.then_inc(dec, 1)
                        if t + 1 < NT:
                            dve.wait_ge(made, 8 + n + 1)
                            links(nc.vector.tensor_tensor(TM[:, :], PS[m][:, :], BM, ALU.mult))
                            dve.wait_ge(outp, n + 1)
                            nc.vector.scalar_tensor_tensor(SD[:, m, :], SD[:, m, :], GC[:, m:m + 1], TM[:, :],
                                                           ALU.mult, ALU.add).then_inc(stz, 1)
                            dve.wait_ge(stz, n + 2)
                            dve.sem_inc(st, 1)
                    dve.wait_ge(outp, 2 * t + 2)
                    nc.vector.tensor_copy(X2[:, t, :], PO[:, :]).then_inc(outd, 1)


def route(nc, core, name, XT, WR, GT, IDX):
    S = lambda n: core.sem(f"{name}_{n}")
    made, sub, ex, link = S("made"), S("sub"), S("exp"), S("v")
    with ExitStack() as c:
        def sb(n, shape):
            return c.enter_context(nc.sbuf_tensor(f"{name}_{n}", shape, F32))

        LG, PR, E1, E2, RM = (sb("lg", [P, NT, 9]), sb("pr", [P, NT, 8]), sb("e1", [P, NT, 8]),
                              sb("e2", [P, NT, 8]), sb("rm", [P, NT]))
        ps = c.enter_context(nc.psum_tensor(name + "_ps", [P, NT, 9], F32))
        with nc.Block() as block:
            @block.tensor
            def _(pe):
                for t in range(NT):
                    for k in range(KC):
                        last = nc.tensor.matmul(ps[:, t, :], XT[:, k, t * P:(t + 1) * P], WR[:, k, :],
                                                start=(k == 0), stop=(k == KC - 1))
                last.then_inc(made, 1)

            @block.scalar
            def _(act):
                act.wait_ge(sub, 1)
                nc.scalar.activation(LG[:, :, :], LG[:, :, :], ACT.Exp).then_inc(ex, 1)

            @block.vector
            def _(dve):
                links = Links(dve, link)
                row = lambda a: a.unsqueeze(2).broadcast_to([P, NT, 8])
                dve.wait_ge(made, 1)
                links(nc.vector.tensor_reduce(RM[:, :], ps[:, :, 0:8], AX.X, ALU.max))
                links(nc.vector.tensor_tensor(LG[:, :, 0:8], ps[:, :, 0:8], row(RM[:, :]), ALU.subtract))
                nc.vector.tensor_scalar(LG[:, :, 8], ps[:, :, 8], -1.0, None, ALU.mult).then_inc(sub, 1)
                dve.wait_ge(ex, 1)
                links(nc.vector.tensor_scalar(E1[:, :, 0], LG[:, :, 8], 1.0, None, ALU.add))
                links(nc.vector.reciprocal(GT[:, :, 8], E1[:, :, 0]))
                links(nc.vector.tensor_reduce(RM[:, :], LG[:, :, 0:8], AX.X, ALU.add))
                links(nc.vector.reciprocal(RM[:, :], RM[:, :]))
                links(nc.vector.tensor_tensor(PR[:, :, :], LG[:, :, 0:8], row(RM[:, :]), ALU.mult))
                idx = IDX.unsqueeze(1).broadcast_to([P, NT, 8])
                for r in range(2):
                    src = PR if r == 0 else E2
                    links(nc.vector.tensor_reduce(RM[:, :], src[:, :, :], AX.X, ALU.max))
                    links(nc.vector.tensor_tensor(E1[:, :, :], src[:, :, :], row(RM[:, :]), ALU.is_equal))
                    links(nc.vector.tensor_tensor(E1[:, :, :], E1[:, :, :], idx, ALU.mult))
                    links(nc.vector.tensor_reduce(RM[:, :], E1[:, :, :], AX.X, ALU.max))
                    links(nc.vector.tensor_tensor(E1[:, :, :], row(RM[:, :]), idx, ALU.is_equal))
                    if r == 0:
                        links(nc.vector.scalar_tensor_tensor(E2[:, :, :], E1[:, :, :], -2.0, PR[:, :, :],
                                                             ALU.mult, ALU.add))
                        links(nc.vector.tensor_tensor(GT[:, :, 0:8], E1[:, :, :], PR[:, :, :], ALU.mult))
                    else:
                        links(nc.vector.tensor_tensor(E1[:, :, :], E1[:, :, :], PR[:, :, :], ALU.mult))
                        links(nc.vector.tensor_tensor(GT[:, :, 0:8], GT[:, :, 0:8], E1[:, :, :], ALU.add))


RESIDENT = {
    "w0qkv": [P, KC, 384], "w0o": [P, KC, C], "bo": [1, C], "qkw0": [P, 320],
    "w0f1": [P, KC, FF], "w0f2": [P, NF, C], "b1": [P, NF], "b2": [1, C],
    "cos0": [P, NT, 8], "sin0": [P, NT, 2, 8],
    "w1x": [P, KC, 3 * SS], "w1in": [P, KC, SS], "w1out": [SS, C], "cw": [P, KC, 4], "cb": [P, KC],
    "alog": [SS, 1], "dd": [P, KC],
    "w2": [P, KC, 3 * C], "w2b": [P, 4], "w2bv": [P, 2 * C], "dt": [P, RH, P], "cs": [P, KC, P],
    "kvs": [P, C], "gc": [P, KC], "bm": [P, P],
    "wa": [P, KC, 3 * C], "wp": [P, KC, C], "wstd": [P, 16], "wrec": [P, 16],
    "w3": [P, KC, 320], "w3o": [P, KC, C], "qkw3": [P, 288], "cos3": [P, NT, 16], "sin3": [P, NT, 2, 16],
    "wr": [P, KC, 9], "idx": [P, 8], "identf": [P, P], "negq": [P, P], "negk": [P, P],
}
STREAMED = {
    "w1g": [P, KC, FF], "w1u": [P, KC, FF], "w1d": [P, NF, C],
    "sgu": [P, KC, 2 * SI], "sdn": [P, NSF, C], "w13": [P, KC, NE * ECOL], "wdn": [P, 2 * NE, C],
}


def build(nc, dram, out, stages=99):
    ctx = ExitStack()
    with ctx:
        def sb(name, shape, dt=F32):
            return ctx.enter_context(nc.sbuf_tensor(name, shape, dt))

        W = {n: sb("s_" + n, s) for n, s in RESIDENT.items()}
        X, XT = sb("X", [P, NT, C]), sb("XT", [P, KC, T])
        ident = sb("ident", [P, P], BF16)
        negq, negk = sb("negqb", [P, P], BF16), sb("negkb", [P, P], BF16)
        onesf = sb("onesf", [P, P])
        diag = sb("diag", [P, KC, P])
        NA = sb("NA", [SS, 1])
        e50 = sb("e50", [P, P])
        onesrow = onesf[0:1, :]
        identf = W["identf"]
        with ExitStack() as c, Core(nc) as core:
            setup(nc, c, core, W, dram, ident, negq, negk, onesf, diag, NA, e50)
        with nc.Fori(0, B) as b, Core(nc) as whole:
            batch(nc, whole, b, dram, out, W, X, XT, ident, negq, negk, onesrow, onesf, diag, NA, e50, stages)


def setup(nc, c, core, W, dram, ident, negq, negk, onesf, diag, NA, e50):
    loaded, ones, link, red, summed, rooted, al = (
        core.sem(n) for n in ("loaded", "ones_made", "set_v", "reduced", "summed", "rooted", "set_a"))
    A = c.enter_context(nc.sbuf_tensor("absum", [P, 2], F32))
    A2 = c.enter_context(nc.sbuf_tensor("absum2", [P, 2], F32))
    NW = c.enter_context(nc.sbuf_tensor("neg_tern", [P, NF * C], F32))
    SC = c.enter_context(nc.sbuf_tensor("head_scales", [P, 3, 16], F32))
    WS = c.enter_context(nc.sbuf_tensor("wa_raw", [P, KC, 3 * C], F32))
    ps = c.enter_context(nc.psum_tensor("set_ps", [P, 2], F32))
    with nc.Block() as block:
        @block.sync
        def _(sp):
            for n, t in W.items():
                sp.dma_start(t[tuple(slice(None) for _ in t.shape)], dram[n]).then_inc(loaded, 16)
            sp.wait_ge(loaded, 16 * len(W))

        @block.vector
        def _(dve):
            links = Links(dve, link)
            links(nc.vector.memset(onesf[:, :], 1.0))
            links(nc.vector.memset(e50[:, :], E50))
            dve.wait_ge(loaded, 16 * len(W))
            links(nc.vector.tensor_copy(ident[:, :], W["identf"][:, :]))
            links(nc.vector.tensor_copy(negq[:, :], W["negq"][:, :]))
            links(nc.vector.tensor_copy(negk[:, :], W["negk"][:, :]))
            for k in range(KC):
                links(nc.vector.tensor_scalar(diag[:, k, :], W["identf"][:, :], W["dd"][:, k:k + 1], None, ALU.mult))
            w1, w2 = W["w0f1"][:, :, :], W["w0f2"][:, :, :]
            links(nc.vector.tensor_reduce(A[:, 0:1], w1, AX.XY, ALU.add, apply_absolute_value=True))
            nc.vector.tensor_reduce(A[:, 1:2], w2, AX.XY, ALU.add, apply_absolute_value=True).then_inc(red, 1)
            dve.wait_ge(summed, 1)
            links(nc.vector.tensor_scalar(A[:, :], ps[:, :], 1.0 / (FF * C), 0.7, ALU.mult, ALU.mult))
            links(nc.vector.tensor_scalar(A2[:, :], A[:, :], -1.0, None, ALU.mult))
            for j, w in enumerate((w1, w2)):
                nw = NW[:, :].rearrange("p (a n) -> p a n", a=w.shape[1])
                links(nc.vector.tensor_scalar(nw, w, A2[:, j:j + 1], None, ALU.is_le))
                links(nc.vector.tensor_scalar(w, w, A[:, j:j + 1], None, ALU.is_ge))
                links(nc.vector.tensor_tensor(w, w, nw, ALU.subtract))
            links(nc.vector.tensor_scalar(SC[:, 2, :], W["wrec"][:, :], 0.1, None, ALU.is_gt))
            links(nc.vector.tensor_scalar(SC[:, 0, :], W["wstd"][:, :], 1e-8, None, ALU.max))
            nc.vector.tensor_scalar(SC[:, 1, :], W["wrec"][:, :], 1e-8, None, ALU.max).then_inc(red, 1)
            dve.wait_ge(rooted, 1)
            wa = W["wa"]
            links(nc.vector.tensor_copy(WS[:, :, :], wa[:, :, :]))
            for k in range(KC):
                raw = lambda a: WS[:, k, a:a + 128].rearrange("p (h d) -> p h d", h=16)
                new = lambda a, lo: wa[:, k, a:a + 256].rearrange("p (h d) -> p h d", h=16)[:, :, lo:lo + 8]
                s = lambda j: SC[:, j, :].unsqueeze(2).broadcast_to([P, 16, 8])
                links(nc.vector.tensor_tensor(new(0, 0), raw(0), s(0), ALU.mult))
                links(nc.vector.tensor_tensor(new(C, 0), raw(128), s(0), ALU.mult))
                links(nc.vector.tensor_copy(wa[:, k, 2 * C:3 * C], WS[:, k, 256:512]))
                tq, tk = new(0, 8), new(C, 8)
                links(nc.vector.tensor_scalar(NW[:, 0:16], SC[:, 2, :], -1.0, 1.0, ALU.mult, ALU.add))
                no = NW[:, 0:16].unsqueeze(2).broadcast_to([P, 16, 8])
                t1 = NW[:, 128:256].rearrange("p (h d) -> p h d", h=16)
                for dst, keep, swap in ((tq, raw(512), raw(640)), (tk, raw(640), raw(512))):
                    links(nc.vector.tensor_tensor(dst, keep, no, ALU.mult))
                    links(nc.vector.tensor_tensor(t1, swap, s(2), ALU.mult))
                    links(nc.vector.tensor_tensor(dst, dst, t1, ALU.add))
                    links(nc.vector.tensor_tensor(dst, dst, s(1), ALU.mult))
            dve.wait_ge(al, 1)
            links(nc.vector.tensor_scalar(NA[:, :], NA[:, :], -1.0, None, ALU.mult))

        @block.tensor
        def _(pe):
            pe.wait_ge(red, 1)
            nc.tensor.matmul(ps[:, :], onesf[:, :], A[:, :], start=True, stop=True).then_inc(summed, 1)

        @block.scalar
        def _(act):
            act.wait_ge(loaded, 16 * len(W))
            nc.scalar.activation(NA[:, :], W["alog"][:, :], ACT.Exp).then_inc(al, 1)
            act.wait_ge(red, 2)
            nc.scalar.activation(SC[:, 0:2, :], SC[:, 0:2, :], ACT.Sqrt).then_inc(rooted, 1)


def batch(nc, whole, b, dram, out, W, X, XT, ident, negq, negk, onesrow, onesf, diag, NA, e50, stages):
    identf = W["identf"]
    tok = lambda t: slice(t * P, (t + 1) * P)
    got = whole.sem("tokens_loaded")
    with nc.Block() as block:
        @block.sync
        def _(sp):
            sp.dma_start(X[:, :, :], dram["x"][:, bass.ds(b * NT, NT), :]).then_inc(got, 16)
            sp.dma_start(XT[:, :, :], dram["xt"][:, :, bass.ds(b * T, T)]).then_inc(got, 16)
            sp.wait_ge(got, 32)

    def dense(YT, w, bias=None):
        def product(t, j):
            for k in range(KC):
                yield YT[:, k, tok(t)], w[:, k, :], (0, C)
            if bias is not None:
                yield onesrow, bias[0:1, :], (0, C)
        return product

    def hidden(H, w, bias=None):
        def product(t, j):
            for f in range(NF):
                yield H[:, f, tok(t)], w[:, f, :], (0, C)
            if bias is not None:
                yield onesrow, bias[0:1, :], (0, C)
        return product

    def done(i):
        return out[:, bass.ds(b * NT, NT), :] if i == min(stages, 8) else None

    with ExitStack() as c, Core(nc) as core:
        def sb(name, shape, dt=F32):
            return c.enter_context(nc.sbuf_tensor(name, shape, dt))
        QK, V, Y, YT = sb("a0qk", [P, NT, 320]), sb("a0v", [P, NT, 64]), sb("a0y", [P, NT, C]), sb("a0yt", [P, KC, T])
        SV = sb("a0sv", [P, NT - 1, 64])
        project_tokens(nc, core, "p0", XT, W["w0qkv"],
                       [(0, 320, lambda t, a, e: QK[:, t, a:e]),
                        (320, 384, lambda t, a, e: V[:, t, a:e])])
        vsum = core.sem("a0_vsum")
        with nc.Block() as block:
            @block.gpsimd
            def _(pool):
                links = Links(pool, vsum)
                links(nc.gpsimd.tensor_copy(SV[:, NT - 2, :], V[:, NT - 1, :]))
                for qb in range(NT - 3, -1, -1):
                    links(nc.gpsimd.tensor_tensor(SV[:, qb, :], SV[:, qb + 1, :], V[:, qb + 1, :], ALU.add))
        norm_rope(nc, core, "r0", QK, 20, 16, W["qkw0"][:, :], W["cos0"][:, :, :], W["sin0"][:, :, :, :], False)
        attention(nc, core, "a0", QK, V, Y, (ident, identf, negq, negk), D=16, NH=16, q0=0, k0=256,
                  kv_of=lambda i, u: i, kper=True, cap=True, scale=0.25,
                  SV=SV, e50=e50, U=4)
        turn_tokens(nc, core, "y0", Y, YT, identf, 4)
        close_layer(nc, core, "c0", X, XT, identf, dense(YT, W["w0o"], W["bo"]), out=done(1))
    if stages <= 1:
        return
    with ExitStack() as c, Core(nc) as core:
        H = c.enter_context(nc.sbuf_tensor("f0h", [P, NF, T], F32))
        hidden_gelu(nc, core, "f0", XT, W["w0f1"], W["b1"], H)
        close_layer(nc, core, "c1", X, XT, identf, hidden(H, W["w0f2"], W["b2"]), out=done(2))
    if stages <= 2:
        return
    with ExitStack() as c:
        w1 = {n: c.enter_context(nc.sbuf_tensor("s_" + n, STREAMED[n], F32)) for n in ("w1g", "w1u", "w1d")}
        sent = whole.sem("w1_loaded")
        with nc.Block() as block:
            @block.sync
            def _(sp):
                for n, t in w1.items():
                    sp.dma_start(t[:, :, :], dram[n]).then_inc(sent, 16)
        with ExitStack() as c2, Core(nc) as core:
            XC = c2.enter_context(nc.sbuf_tensor("m1xc", [P, KC, T], F32))
            HM = c2.enter_context(nc.sbuf_tensor("m1hm", [SS, T], F32))
            scan_mixer(nc, core, "m1", XT, W["w1x"], W["w1in"], W["cw"], W["cb"], NA, XC, HM)

            def product(t, j):
                yield HM[:, tok(t)], W["w1out"][:, :], (0, C)
                for k in range(KC):
                    yield XC[:, k, tok(t)], diag[:, k, :], (k * P, (k + 1) * P)
            close_layer(nc, core, "c2", X, XT, identf, product, out=done(3))
        if stages <= 3:
            return
        with nc.Block() as block:
            @block.sync
            def _(sp):
                sp.wait_ge(sent, 48)
        core = c.enter_context(Core(nc))
        H = c.enter_context(nc.sbuf_tensor("f1h", [P, NF, T], F32))
        items = [(lambda k, f=f: w1["w1g"][:, k, tok(f)], lambda k, f=f: w1["w1u"][:, k, tok(f)], P, 0, P,
                  lambda h, f=f: H[:, f, h * CH:(h + 1) * CH]) for f in range(NF)]
        hidden_swiglu(nc, core, "f1", XT, items)
        close_layer(nc, core, "c3", X, XT, identf, hidden(H, w1["w1d"]), out=done(4))
    if stages <= 4:
        return
    with ExitStack() as c, Core(nc) as core:
        X2 = c.enter_context(nc.sbuf_tensor("m2x", [P, NT, C], F32))
        retention(nc, core, "m2", XT, W["w2"], W["w2b"], W["dt"], W["cs"], W["kvs"][:, :], W["gc"], W["bm"][:, :],
                  W["w2bv"][:, :], X2)
        close_layer(nc, core, "c4", X, XT, identf, lambda t, j: iter([(identf[:, :], X2[:, t, :], (0, C))]),
                    out=done(5))
    if stages <= 5:
        return
    with ExitStack() as c, Core(nc) as core:
        def sb(name, shape, dt=F32):
            return c.enter_context(nc.sbuf_tensor(name, shape, dt))
        QK, V, Y, YT = sb("a2qk", [P, NT, 512]), sb("a2v", [P, NT, 256]), sb("a2y", [P, NT, C]), sb("a2yt", [P, KC, T])
        project_tokens(nc, core, "p2", XT, W["wa"],
                       [(0, 512, lambda t, a, e: QK[:, t, a:e]),
                        (512, 768, lambda t, a, e: V[:, t, a:e])])
        attention(nc, core, "a2", QK, V, Y, (ident, identf, negq, negk), D=16, NH=16, q0=0, k0=256,
                  kv_of=lambda i, u: i * 4 + u, kper=True, cap=False, scale=0.25,
                  SV=None, e50=None, U=4)
        turn_tokens(nc, core, "y2", Y, YT, identf, 4)
        close_layer(nc, core, "c5", X, XT, identf, dense(YT, W["wp"]), out=done(6))
    if stages <= 6:
        return
    with ExitStack() as c:
        w3 = {n: c.enter_context(nc.sbuf_tensor("s_" + n, STREAMED[n], F32)) for n in ("sgu", "sdn", "w13", "wdn")}
        sent3 = whole.sem("w3_loaded")
        with nc.Block() as block:
            @block.sync
            def _(sp):
                for n, t in w3.items():
                    sp.dma_start(t[:, :, :], dram[n]).then_inc(sent3, 16)
        with ExitStack() as c2, Core(nc) as core:
            def sb(name, shape, dt=F32):
                return c2.enter_context(nc.sbuf_tensor(name, shape, dt))
            QK, V, Y, YT = sb("a3qk", [P, NT, 288]), sb("a3v", [P, NT, 32]), sb("a3y", [P, NT, C]), sb("a3yt", [P, KC, T])
            project_tokens(nc, core, "p3", XT, W["w3"],
                           [(0, 288, lambda t, a, e: QK[:, t, a:e]),
                            (288, 320, lambda t, a, e: V[:, t, 0:32])])
            norm_rope(nc, core, "r3", QK, 9, 32, W["qkw3"][:, :], W["cos3"][:, :, :], W["sin3"][:, :, :, :], True)
            attention(nc, core, "a3", QK, V, Y, (ident, identf, negq, negk), D=32, NH=8, q0=0, k0=256,
                      kv_of=lambda i, u: 0, kper=False, cap=False, scale=1.0 / 16.0,
                      SV=None, e50=None, U=2)
            turn_tokens(nc, core, "y3", Y, YT, identf, 2)
            close_layer(nc, core, "c6", X, XT, identf, dense(YT, W["w3o"]), out=done(7))
        if stages <= 7:
            return
        with nc.Block() as block:
            @block.sync
            def _(sp):
                sp.wait_ge(sent3, 64)
        core = c.enter_context(Core(nc))
        GT = c.enter_context(nc.sbuf_tensor("f3gt", [P, NT, 9], F32))
        route(nc, core, "g3", XT, W["wr"], GT, W["idx"][:, :])
        H = c.enter_context(nc.sbuf_tensor("f3h", [P, NSF, T], F32))
        parts = [("shared", None)] + [("experts", (e, e + 2)) for e in range(0, NE, 2)]
        for pi, (kind, es) in enumerate(parts):
            items = []
            if kind == "shared":
                for f in range(NSF):
                    r = min(P, SI - f * P)
                    items.append((lambda k, f=f, r=r: w3["sgu"][:, k, f * P:f * P + r],
                                  lambda k, f=f, r=r: w3["sgu"][:, k, SI + f * P:SI + f * P + r], r, 0, r,
                                  lambda h, f=f, r=r: H[0:r, f, h * CH:(h + 1) * CH]))
            else:
                for s, e in enumerate(range(*es)):
                    a = e * ECOL
                    items.append((lambda k, a=a: w3["w13"][:, k, a:a + P], lambda k, a=a: w3["w13"][:, k, a + P:a + 2 * P],
                                  P, 0, P, lambda h, s=s: H[:, 2 * s, h * CH:(h + 1) * CH]))
                    items.append((lambda k, a=a: w3["w13"][:, k, a + 2 * P:a + ECOL], None, EREM, 64, 64 + EREM,
                                  lambda h, s=s: H[0:EREM, 2 * s + 1, h * CH:(h + 1) * CH]))
            hidden_swiglu(nc, core, f"h3_{pi}", XT, items)
            if kind == "shared":
                def product(t, j):
                    for f in range(NSF):
                        r = min(P, SI - f * P)
                        yield H[0:r, f, tok(t)], w3["sdn"][0:r, f, :], (0, C)
                gates = [lambda t: GT[:, t, 8:9]]
            else:
                def product(t, j, es=es):
                    yield H[:, 2 * j, tok(t)], w3["wdn"][:, 2 * (es[0] + j), :], (0, C)
                    yield H[0:EREM, 2 * j + 1, tok(t)], w3["wdn"][0:EREM, 2 * (es[0] + j) + 1, :], (0, C)
                gates = [lambda t, e=e: GT[:, t, e:e + 1] for e in range(*es)]
            if pi == len(parts) - 1:
                close_layer(nc, core, "c7", X, XT, identf, product, gates, out=done(8))
            else:
                add_parts(nc, core, f"d3_{pi}", X, product, gates)


def add_parts(nc, core, name, X, product, gates):
    made, added = core.sem(name + "_made"), core.sem(name + "_added")
    with ExitStack() as c:
        ps = [c.enter_context(nc.psum_tensor(f"{name}_ps{i}", [P, C], F32)) for i in range(4)]
        order = [(t, j) for t in range(NT) for j in range(len(gates))]
        with nc.Block() as block:
            @block.tensor
            def _(pe):
                for n, (t, j) in enumerate(order):
                    if n >= 4:
                        pe.wait_ge(added, n - 3)
                    mms = list(product(t, j))
                    for m, (lhsT, rhs, cols) in enumerate(mms):
                        last = nc.tensor.matmul(ps[n % 4][:, cols[0]:cols[1]], lhsT, rhs, start=(m == 0),
                                                stop=(m == len(mms) - 1))
                    last.then_inc(made, 1)

            @block.vector
            def _(dve):
                for n, (t, j) in enumerate(order):
                    dve.wait_ge(made, n + 1)
                    if j:
                        dve.wait_ge(added, n)
                    nc.vector.scalar_tensor_tensor(X[:, t, :], ps[n % 4][:, :], gates[j](t), X[:, t, :],
                                                   ALU.mult, ALU.add).then_inc(added, 1)


def tables():
    f = np.float32
    d = {}

    def rope(theta, dim, sign):
        inv = 1.0 / theta ** (np.arange(0, dim, 2, dtype=np.float64) / dim)
        fr = np.outer(np.arange(T), inv.astype(f)).astype(f)
        fr = fr.reshape(NT, P, dim // 2).transpose(1, 0, 2)
        return np.cos(fr).astype(f), np.stack([sign * np.sin(fr), -sign * np.sin(fr)], axis=2).astype(f)

    d["cos0"], d["sin0"] = rope(10000.0, 16, 1.0)
    d["cos3"], d["sin3"] = rope(1000000.0, 32, -1.0)
    betas = np.linspace(np.log2(1.0 / 32.0), np.log2(1.0 / 512.0), RH)
    g = 1.0 - np.exp2(betas)
    i = np.arange(P)
    ij = i[None, :] - i[:, None]
    d["dt"] = np.where(ij[:, None, :] >= 0, g[None, :, None] ** np.maximum(ij, 0)[:, None, :], 0.0).astype(f)
    hp = np.repeat(np.arange(4), RD)
    gh = np.stack([g[4 * m + hp] for m in range(KC)], axis=1)
    d["cs"] = (gh[:, :, None] ** (i + 1)[None, None, :]).astype(f)
    d["kvs"] = (np.repeat(g, RD)[None, :] ** (P - 1 - i)[:, None]).astype(f)
    d["gc"] = (gh ** P).astype(f)
    d["bm"] = (hp[:, None] == hp[None, :]).astype(f)
    d["idx"] = np.tile(np.arange(8, 0, -1).astype(f), (P, 1))
    d["identf"] = np.eye(P, dtype=f)
    d["negq"] = np.where(i[None, :] > i[:, None], NEG, 0.0).astype(f)
    d["negk"] = np.where(i[:, None] > i[None, :], NEG, 0.0).astype(f)
    return d


def layout(a):
    def kn(w):
        return w.reshape(w.shape[0] // P, P, w.shape[1]).transpose(1, 0, 2)

    def col(v):
        return v.reshape(-1, P).T

    def rows(v):
        return np.broadcast_to(v[None, :], (P, v.shape[0]))

    d = {}
    x = a["L0_attn_x"].reshape(B * T, C)
    d["x"] = x.reshape(B * NT, P, C).transpose(1, 0, 2)
    d["xt"] = kn(x.T)
    d["w0qkv"] = kn(np.concatenate([a["L0_attn_Wq"], a["L0_attn_Wk"], a["L0_attn_Wv"]], 0).T)
    d["w0o"], d["bo"] = kn(a["L0_attn_Wo"].T), a["L0_attn_bo"][None, :]
    d["qkw0"] = rows(np.concatenate([np.tile(a["L0_attn_q_norm_w"], 16), np.tile(a["L0_attn_k_norm_w"], 4)]))
    d["w0f1"], d["w0f2"] = kn(a["L0_ffn_w1"].T), kn(a["L0_ffn_w2"].T)
    d["b1"], d["b2"] = col(a["L0_ffn_b1"]), a["L0_ffn_b2"][None, :]
    wx = a["L1_attn_Wxproj"]
    d["w1x"] = kn(np.concatenate([np.repeat(wx[2 * SS:], SS, 0), wx[:2 * SS]], 0).T)
    d["w1in"], d["w1out"] = kn(a["L1_attn_Winproj"].T), a["L1_attn_Woutproj"].T
    d["cw"] = a["L1_attn_conv_w"].reshape(KC, P, 4).transpose(1, 0, 2)
    d["cb"], d["alog"], d["dd"] = col(a["L1_attn_conv_b"]), a["L1_attn_A_log"][:, None], col(a["L1_attn_D"])
    d["w1g"], d["w1u"], d["w1d"] = kn(a["L1_ffn_w_gate"].T), kn(a["L1_ffn_w_up"].T), kn(a["L1_ffn_w_down"].T)
    d["w2"] = kn(np.concatenate([a["L2_attn_Wq"], a["L2_attn_Wk"], a["L2_attn_Wv"]], 1))
    d["w2b"] = np.concatenate([col(a["L2_attn_bq"]), col(a["L2_attn_bk"])], 1)
    d["w2bv"] = rows(np.concatenate([a["L2_attn_bk"], a["L2_attn_bv"]]))
    d["wa"], d["wp"] = kn(a["L2_ffn_Wa"]), kn(a["L2_ffn_Wp"])
    d["wstd"], d["wrec"] = rows(a["L2_ffn_w_std"]), rows(a["L2_ffn_w_rec"])
    d["w3"] = kn(np.concatenate([a["L3_attn_q_proj"], a["L3_attn_k_proj"], a["L3_attn_v_proj"]], 0).T)
    d["w3o"] = kn(a["L3_attn_o_proj"].T)
    d["qkw3"] = rows(np.concatenate([np.tile(a["L3_attn_q_norm"], 8), a["L3_attn_k_norm"]]))
    d["wr"] = kn(np.concatenate([a["L3_ffn_gate_w"], a["L3_ffn_shared_gate_w"]], 0).T)
    d["sgu"] = kn(a["L3_ffn_shared_gate_up_w"].T)
    z = lambda *s: np.zeros(s, np.float32)
    d["sdn"] = kn(np.concatenate([a["L3_ffn_shared_down_w"].T, z(NSF * P - SI, C)], 0))
    w13 = a["L3_ffn_w13"]
    w13 = np.concatenate([w13[:, :P], w13[:, EI:EI + P], w13[:, P:EI], z(NE, 64 - EREM, C), w13[:, EI + P:]], 1)
    d["w13"] = kn(w13.reshape(NE * ECOL, C).T)
    w2 = np.concatenate([a["L3_ffn_w2"].transpose(0, 2, 1), z(NE, 2 * P - EI, C)], 1)
    d["wdn"] = kn(w2.reshape(NE * 2 * P, C))
    d.update(tables())
    return {k: np.ascontiguousarray(v) for k, v in d.items()}


def kernel(**inputs):
    import concourse.bacc as bacc
    from concourse.bass_utils import run_bass_kernel_spmd

    data = layout({k: np.asarray(v) for k, v in inputs.items()})
    nc = bacc.Bacc("TRN2", target_bir_lowering=False, num_devices=1)
    dram = {k: nc.dram_tensor(f"in_{k}", list(v.shape), F32, kind="ExternalInput").ap() for k, v in data.items()}
    out = nc.dram_tensor("out_tokens", [P, B * NT, C], F32, kind="ExternalOutput").ap()
    build(nc, dram, out, STAGES)
    r = run_bass_kernel_spmd(nc, [{f"in_{k}": v for k, v in data.items()}], core_ids=[0])
    y = r.results[0]["out_tokens"]
    return y.transpose(1, 0, 2).reshape(B, T, C)


STAGES = 99
```

```python
import math
from contextlib import ExitStack

import numpy as np

import concourse.bass as bass
from concourse import mybir

F32 = mybir.dt.float32
BF16 = mybir.dt.bfloat16
ALU = mybir.AluOpType
ACT = mybir.ActivationFunctionType
AX = mybir.AxisListType

B, T, C = 4, 1024, 256
P = 128
NT = T // P
KC = C // P
CH = 512
NCH = T // CH
FF = 1024
NF = FF // P
TERMS = 6
NEG = -1.0e30
E50 = math.exp(-50.0)
RH = 8
RD = C // RH
SS = 64
NE, EI = 8, 176
EREM = EI - P
ECOL = 2 * P + 64 + EREM
SI = 704
NSF = (SI + P - 1) // P
LN_EPS = 1e-5


class Links:

    def __init__(self, eng, sem, clear=False):
        self.eng, self.sem, self.n = eng, sem, 0
        if clear:
            eng.sem_clear(sem)

    def __call__(self, ins):
        self.n += 1
        ins.then_inc(self.sem, 1)
        self.eng.wait_ge(self.sem, self.n)


class Core:

    def __init__(self, nc):
        self.nc, self.sems = nc, []

    def __enter__(self):
        self.ctx = ExitStack()
        self.ctx.__enter__()
        return self

    def sem(self, name):
        s = self.ctx.enter_context(self.nc.semaphore(name))
        self.sems.append(s)
        return s

    def __exit__(self, *raised):
        if raised[0] is None:
            for s in self.sems:
                self.nc.sync.sem_clear(s)
            self.nc.all_engine_barrier()
        return self.ctx.__exit__(*raised)


def heads_view(ap, n):
    return ap.rearrange("p t (h d) -> p t h d", h=n)


def project_tokens(nc, core, name, XT, W, outs):
    done, free = core.sem(name + "_projected"), core.sem(name + "_taken")
    cols = W.shape[2]
    parts = [(a, min(a + 512, cols)) for a in range(0, cols, 512)]
    with ExitStack() as c:
        ps = [c.enter_context(nc.psum_tensor(f"{name}_ps{i}", [P, 512], F32)) for i in range(4)]
        with nc.Block() as block:
            @block.tensor
            def _(pe):
                n = 0
                for t in range(NT):
                    for a, e in parts:
                        if n >= 4:
                            pe.wait_ge(free, n - 3)
                        for k in range(KC):
                            last = nc.tensor.matmul(ps[n % 4][:, 0:e - a], XT[:, k, t * P:(t + 1) * P],
                                                    W[:, k, a:e], start=(k == 0), stop=(k == KC - 1))
                        last.then_inc(done, 1)
                        n += 1

            @block.scalar
            def _(act):
                n = 0
                for t in range(NT):
                    for a, e in parts:
                        act.wait_ge(done, n + 1)
                        pieces = [(max(a, u), min(e, v), f, u) for u, v, f in outs if max(a, u) < min(e, v)]
                        for j, (u, v, f, base) in enumerate(pieces):
                            src = ps[n % 4][:, u - a:v - a]
                            dst = f(t, u - base, v - base)
                            if len(dst.shape) == 3:
                                src = src.rearrange("p (h d) -> p h d", d=dst.shape[2])
                            ins = nc.scalar.activation(dst, src, ACT.Copy)
                            if j == len(pieces) - 1:
                                ins.then_inc(free, 1)
                        n += 1


def norm_rope(nc, core, name, QK, nh, D, wtab, cosd, sind, eps_in):
    ss_done, root_done, link = core.sem(name + "_ss"), core.sem(name + "_root"), core.sem(name + "_v")
    g_link, g_done = core.sem(name + "_g"), core.sem(name + "_turned")
    h2 = D // 2
    with ExitStack() as c:
        SQ = c.enter_context(nc.sbuf_tensor(name + "_sq", [P, NT, nh * D], F32))
        R = c.enter_context(nc.sbuf_tensor(name + "_rms", [P, NT, nh], F32))
        q4 = QK[:, :, :].rearrange("p t (h d) -> p t h d", d=D)
        s4 = SQ[:, :, :].rearrange("p t (h d) -> p t h d", d=D)
        with nc.Block() as block:
            @block.vector
            def _(dve):
                link_ = Links(dve, link)
                link_(nc.vector.tensor_tensor(SQ[:, :, :], QK[:, :, :], QK[:, :, :], ALU.mult))
                link_(nc.vector.tensor_reduce(R[:, :, :], s4, AX.X, ALU.add))
                nc.vector.tensor_scalar(R[:, :, :], R[:, :, :], 1.0 / D, 1e-6 if eps_in else 0.0,
                                        ALU.mult, ALU.add).then_inc(ss_done, 1)
                dve.wait_ge(root_done, 1)
                if not eps_in:
                    link_(nc.vector.tensor_scalar(R[:, :, :], R[:, :, :], 1e-6, None, ALU.add))
                link_(nc.vector.reciprocal(R[:, :, :], R[:, :, :]))
                link_(nc.vector.tensor_tensor(q4, q4, R[:, :, :].unsqueeze(3).broadcast_to([P, NT, nh, D]), ALU.mult))
                link_(nc.vector.tensor_tensor(QK[:, :, :], QK[:, :, :],
                                              wtab.unsqueeze(1).broadcast_to([P, NT, nh * D]), ALU.mult))
                for half in range(2):
                    link_(nc.vector.tensor_tensor(
                        s4[:, :, :, half * h2:(half + 1) * h2], q4[:, :, :, (1 - half) * h2:(2 - half) * h2],
                        sind[:, :, half, :].unsqueeze(2).broadcast_to([P, NT, nh, h2]), ALU.mult))
                for half in range(2):
                    v = q4[:, :, :, half * h2:(half + 1) * h2]
                    link_(nc.vector.tensor_tensor(
                        v, v, cosd.unsqueeze(2).broadcast_to([P, NT, nh, h2]), ALU.mult))
                link_(nc.vector.tensor_tensor(QK[:, :, :], QK[:, :, :], SQ[:, :, :], ALU.add))

            @block.scalar
            def _(act):
                act.wait_ge(ss_done, 1)
                nc.scalar.activation(R[:, :, :], R[:, :, :], ACT.Sqrt).then_inc(root_done, 1)


def attention(nc, core, name, QK, V, Y, consts, *, D, NH, q0, k0, kv_of, kper, cap, scale, SV, U):
    NSUB = TERMS * D // 96
    ROWS = 96
    CAPB = 12 if cap else 8
    SB = CAPB // 4
    GW = 32 if D < 32 else 64
    NG = P // GW
    NSL = NT // NG
    place = tile_places(NG)
    SEG = segments(CAPB, NG, place)
    NS = len(SEG)
    caster = "dve" if cap else "act"
    kx = not cap
    chunks = [(qb, a, min(a + 4, qb + 1)) for qb in range(NT) for a in range(0, qb + 1, 4)]
    NC = len(chunks)
    PERG = (2 if kper else 1) * NSUB
    TB0 = 0 if kper else NSUB
    S = lambda n: core.sem(f"{name}_{n}")
    q_stacked, k_stacked, v_ready, pool_link = S("q_stacked"), S("k_stacked"), S("v_ready"), S("pool")
    turned, untangled = S("turned"), S("untangled")
    s_ready, tanh_done, exp_done, pv_done = S("s_ready"), S("tanh"), S("exp"), S("pv")
    y_ready, y_done = S("y_ready"), S("y_done")
    mx_ready, mx_taken, m_split, m_turned, m_placed, vlink = (
        S("mx_ready"), S("mx_taken"), S("m_split"), S("m_turned"), S("m_placed"), S("v"))
    ones_set, v_set, k_cast, cast, cast_held = S("ones"), S("v_set"), S("k_cast"), S("cast"), S("cast_held")
    o_taken, o_turned, held = S("o_taken"), S("o_turned"), S("pool_held")
    ident, identf, negq, negk = consts
    with ExitStack() as c:
        def sb(n, shape, dt):
            return c.enter_context(nc.sbuf_tensor(f"{name}_{n}", shape, dt))

        def pb(n, shape, dt):
            return c.enter_context(nc.psum_tensor(f"{name}_{n}", shape, dt))

        Qs = sb("Qs", [P, 2, NT, NSUB * ROWS], BF16)
        nks = 2 if kper else 1
        Ks = sb("Ks", [P, nks, NT, NSUB * ROWS], BF16)
        RQ = sb("RQ", [P, NT, D], F32)
        QT = sb("QT", [P, 4, NSUB, T], BF16)
        KT = sb("KT", [P, 4 if kper else 1, NSUB, T], BF16)
        Vh = sb("Vh", [P, 4, NT, GW], F32) if kper else sb("Vh", [P, 1, NT, GW], F32)
        OT = sb("OT", [P, NSL * P], F32)
        NPB = 3 if cap else 4 if kper else 2
        Pb = [sb(f"P{i}", [P, CAPB * P], F32) for i in range(NPB)]
        Tb = [sb(f"T{i}", [P, CAPB * P], F32) for i in range(2)] if cap else None
        RC = sb("RC", [P, NSL, NG], F32)
        if kx:
            MX = sb("MX", [P, NT, 2], F32)
            M1 = sb("M1", [P, NT], F32)
            M2 = sb("M2", [P, NT], F32)
            MS = sb("MS", [P, NT, 3], BF16)
            S1 = [pb(f"S1{i}", [P, 512], F32) for i in range(2)]
        Sp = [pb(f"S{i}", [P, SB * 512], F32) for i in range(2)]
        TP = pb("TP", [P, T], BF16)
        O = pb("O", [P, NSL * P], F32)
        TO = TP[:, :].bitcast(F32)[:, 0:NSL * P]
        tov = TO.rearrange("p (s g w) -> p s g w", s=NSL, g=NG)
        qst = Qs[:, :, :, :].rearrange("p b t (j d) -> p b t j d", d=D)
        kst = Ks[:, :, :, :].rearrange("p b t (j d) -> p b t j d", d=D)

        def qsrc(i, u):
            return QK[:, :, bass.ds(q0 + (i * U + u) * D, D)]

        def ksrc(i, u):
            return QK[:, :, bass.ds(k0 + kv_of(i, u) * D, D)]

        def cast_k(copy, i, u, b):
            copy(kst[:, b, :, 0:2, :], ksrc(i, u).unsqueeze(2).broadcast_to([P, NT, 2, D]))
            return copy(kst[:, b, :, 3, :], ksrc(i, u))

        def cast_head(eng, copy, i, u, n):
            if late(n, 2):
                eng.wait_ge(turned, tuses(i, u) - PERG)
                eng.sem_inc(cast_held, 1)
            b = u % 2
            copy(qst[:, b, :, 0:3:2, :], qsrc(i, u).unsqueeze(2).broadcast_to([P, NT, 2, D]))
            last = copy(qst[:, b, :, 5, :], qsrc(i, u))
            if kper:
                last = cast_k(copy, i, u, b)
            last.then_inc(cast, 1)

        def tuses(i, u):
            return i * (U * PERG) + u * PERG + TB0

        def at(i, u, d):
            return i + (u + d) // U, (u + d) % U

        def run(eng, head):
            for u in range(U):
                head(0, u, u)
            if NH // U > 2:
                with eng.Fori(1, NH // U - 1) as i:
                    for u in range(U):
                        head(i, u, None)
            for u in range(U):
                head(NH // U - 1, u, NH - U + u)

        def late(n, k):
            return n is None or n >= k

        def more(n, k):
            return n is None or n + k < NH

        with nc.Block() as block:
            @block.gpsimd
            def _(pool):
                def split_q(i, u, links):
                    st, two = qst[:, u % 2], [P, NT, 2, D]
                    links(nc.gpsimd.tensor_tensor(RQ[:, :, :], qsrc(i, u), st[:, :, 0, :], ALU.subtract))
                    links(nc.gpsimd.tensor_copy(st[:, :, 1:5:3, :], RQ[:, :, :].unsqueeze(2).broadcast_to(two)))
                    links(nc.gpsimd.tensor_tensor(st[:, :, 3, :], RQ[:, :, :], st[:, :, 1, :], ALU.subtract))

                def split_k(i, u, links, b):
                    st, two = kst[:, b], [P, NT, 2, D]
                    links(nc.gpsimd.tensor_tensor(RQ[:, :, :], ksrc(i, u), st[:, :, 0, :], ALU.subtract))
                    links(nc.gpsimd.tensor_copy(st[:, :, 2:5:2, :], RQ[:, :, :].unsqueeze(2).broadcast_to(two)))
                    links(nc.gpsimd.tensor_tensor(st[:, :, 5, :], RQ[:, :, :], st[:, :, 2, :], ALU.subtract))

                links = Links(pool, pool_link)
                links(nc.gpsimd.memset(Vh[:, :, :, :], 1.0))
                if not kper:
                    links(nc.gpsimd.tensor_copy(Vh[:, 0, :, 0:D], V[:, :, :]))
                    pool.sem_inc(v_set, 1)
                    pool.wait_ge(k_cast, 1)
                    split_k(0, 0, links, 0)
                    pool.sem_inc(k_stacked, 1)

                def head(i, u, n):
                    links = Links(pool, pool_link, clear=True)
                    pool.wait_ge(cast, i * U + u + 1)
                    pool.sem_inc(held, 1)
                    if kper:
                        split_k(i, u, links, u % 2)
                    split_q(i, u, links)
                    pool.sem_inc(q_stacked, 1)
                    if kper:
                        if late(n, 4):
                            pool.wait_ge(pv_done, (i * U + u - 3) * NS)
                            pool.sem_inc(held, 1)
                        g = kv_of(i, u)
                        links(nc.gpsimd.tensor_copy(Vh[:, u, :, 0:D], V[:, :, bass.ds(g * D, D)]))
                        pool.sem_inc(v_set, 1)
                run(pool, head)

            @block.tensor
            def _(pe):
                def turn(stk, use, j):
                    if not (isinstance(use, int) and use < 1):
                        pe.wait_ge(untangled, use)
                    for t in range(NT):
                        last = nc.tensor.transpose(TP[0:ROWS, t * P:(t + 1) * P],
                                                   stk[:, t, j * ROWS:(j + 1) * ROWS], ident[:, :])
                    last.then_inc(turned, 1)

                def turn_part(i, u, x):
                    if x == 0:
                        pe.wait_ge(q_stacked, i * U + u + 1)
                    if kper:
                        turn((Ks, Qs)[x][:, u % 2], tuses(i, u) + x, 0)
                    else:
                        turn(Qs[:, u % 2], tuses(i, u) + x, x)

                def scores(i, u, s, between=lambda: None):
                    g = (i * U + u) * NS + s
                    if s == 0:
                        pe.wait_ge(untangled, tuses(i, u) + PERG)
                        if kx:
                            pe.wait_ge(m_placed, i * U + u + 1)
                    if not (isinstance(g, int) and g < 2):
                        pe.wait_ge(tanh_done if cap else exp_done, g - 1)
                    seg, a = SEG[s], 0
                    while a < len(seg):
                        kb, qb = seg[a]
                        w = 1
                        while a + w < len(seg) and (a + w) % 4 and seg[a + w] == (kb, qb + w):
                            w += 1
                        dst = Sp[(u * NS + s) % 2][:, a * P:(a + w) * P]
                        diag = qb == kb
                        first = True
                        for j in range(NSUB):
                            end = j == NSUB - 1
                            last = nc.tensor.matmul(
                                dst, KT[:, u if kper else 0, j, kb * P:(kb + 1) * P],
                                QT[:, u, j, qb * P:(qb + w) * P], start=first, stop=end,
                                skip_group_check=True)
                            first = False
                        if diag:
                            last = nc.tensor.matmul(dst[:, 0:P], ident[:, :], negk[:, :], start=False,
                                                    stop=True, skip_group_check=True)
                        a += w
                        if a == len(seg):
                            last.then_inc(s_ready, 1)
                        if a % 4 == 0:
                            between()

                def maxima(i, u, cs):
                    for ci in cs:
                        qb, a, e = chunks[ci]
                        n = (i * U + u) * NC + ci
                        if ci == 0:
                            pe.wait_ge(untangled, tuses(i, u) + PERG)
                        if not (isinstance(n, int) and n < 2):
                            pe.wait_ge(mx_taken, n - 1)
                        dst = S1[(u * NC + ci) % 2][:, 0:(e - a) * P]
                        last = nc.tensor.matmul(dst, QT[0:ROWS, u, 0, qb * P:(qb + 1) * P],
                                                KT[0:ROWS, u if kper else 0, 0, a * P:e * P],
                                                start=True, stop=(e <= qb), skip_group_check=True)
                        if e == qb + 1:
                            last = nc.tensor.matmul(dst[:, (e - a - 1) * P:(e - a) * P], ident[:, :], negq[:, :],
                                                    start=False, stop=True, skip_group_check=True)
                        last.then_inc(mx_ready, 1)

                def turn_maxima(i, u):
                    pe.wait_ge(m_split, i * U + u + 1)
                    if not (isinstance(i, int) and i * U + u < 1):
                        pe.wait_ge(m_placed, i * U + u)
                    for qb in range(NT):
                        last = nc.tensor.transpose(TP[ROWS:ROWS + 3, qb * P:(qb + 1) * P], MS[:, qb, :],
                                                   ident[:, :], tile_position=(0, ROWS))
                    last.then_inc(m_turned, 1)

                def weigh(i, u, s):
                    g = (i * U + u) * NS + s
                    n = i * U + u
                    pe.wait_ge(exp_done, g + 1)
                    vv = Vh[:, u if kper else 0]
                    todo = []
                    if s == 0:
                        pe.wait_ge(v_set, n + 1 if kper else 1)
                        if not (isinstance(n, int) and n < 1):
                            pe.wait_ge(o_taken, n)
                    todo += [(qb, vv[:, kb, :], Pb[(u * NS + s) % NPB][:, x * P:(x + 1) * P])
                             for x, (kb, qb) in enumerate(SEG[s])]
                    byg = [[m for m in todo if place[m[0]][1] == gr] for gr in range(NG)]
                    rounds = max(len(x) for x in byg)
                    for r in range(rounds):
                        for gr in range(NG):
                            if r < len(byg[gr]):
                                qb, v, p = byg[gr][r]
                                sl = place[qb][0]
                                last = nc.tensor.matmul(O[gr * GW:(gr + 1) * GW, sl * P:(sl + 1) * P], v, p,
                                                        start=(s == 0 and r == 0), stop=True,
                                                        skip_group_check=True)
                    last.then_inc(pv_done, 1)

                def turn_out(i, u):
                    n = i * U + u
                    pe.wait_ge(o_taken, n + 1)
                    for sl in range(NSL):
                        last = nc.tensor.transpose(TO[:, sl * P:(sl + 1) * P], OT[:, sl * P:(sl + 1) * P],
                                                   identf[:, :])
                    last.then_inc(o_turned, 1)

                pe.wait_ge(ones_set, 1)
                if not kper:
                    pe.wait_ge(k_stacked, 1)
                    for j in range(NSUB):
                        turn(Ks[:, 0], j, j)
                for u in range(3):
                    turn_part(0, u, 0)
                    turn_part(0, u, 1)
                if kx:
                    maxima(0, 0, range(NC))
                    turn_maxima(0, 0)
                    maxima(0, 1, range(NC))

                def head(i, u, n):
                    before = (i, u - 1) if u else (i - 1, U - 1)
                    chunk = iter(range(NC))

                    def one_chunk():
                        c = next(chunk, None)
                        if kx and more(n, 2) and c is not None:
                            maxima(*at(i, u, 2), [c])

                    for s in range(NS):
                        if s == 0 and late(n, 2):
                            pe.wait_ge(y_done, i * U + u - 1)
                        scores(i, u, s, one_chunk)
                        if s == 1:
                            if kx and more(n, 1):
                                turn_maxima(*at(i, u, 1))
                            if more(n, 3):
                                turn_part(*at(i, u, 3), 0)
                        if s == min(3, NS - 1) and late(n, 1):
                            if more(n, 3):
                                pe.wait_ge(untangled, tuses(*at(i, u, 3)) + PERG)
                            if kx and more(n, 1):
                                pe.wait_ge(m_placed, i * U + u + 2)
                            turn_out(*before)
                        if s >= 2:
                            weigh(i, u, s - 2)
                        elif late(n, 1):
                            weigh(*before, NS - 2 + s)
                        one_chunk()
                        if s == 1 and more(n, 3):
                            turn_part(*at(i, u, 3), 1)
                run(pe, head)
                weigh(NH // U - 1, U - 1, NS - 2)
                weigh(NH // U - 1, U - 1, NS - 1)
                turn_out(NH // U - 1, U - 1)

            @block.scalar
            def _(act):
                def squash(i, u, s):
                    g = (i * U + u) * NS + s
                    act.wait_ge(s_ready, g + 1)
                    if not (isinstance(g, int) and g < 2):
                        act.wait_ge(exp_done, g - 1)
                    w = len(SEG[s]) * P
                    b = (u * NS + s) % 2
                    nc.scalar.activation(Tb[b][:, 0:w], Sp[b][:, 0:w], ACT.Tanh,
                                         scale=scale / 50.0).then_inc(tanh_done, 1)

                def expo(i, u, s):
                    g = (i * U + u) * NS + s
                    act.wait_ge(tanh_done if cap else s_ready, g + 1)
                    if not (isinstance(g, int) and g < NPB):
                        act.wait_ge(pv_done, g - NPB + 1)
                    w = len(SEG[s]) * P
                    b = (u * NS + s) % 2
                    src = Tb[b] if cap else Sp[b]
                    nc.scalar.activation(Pb[(u * NS + s) % NPB][:, 0:w], src[:, 0:w], ACT.Exp,
                                         scale=50.0 if cap else scale).then_inc(exp_done, 1)

                def place_maxima(i, u):
                    if isinstance(i, int) and i * U + u == 0:
                        act.wait_ge(ones_set, 1)
                    act.wait_ge(m_turned, i * U + u + 1)
                    nc.scalar.activation(QT[ROWS:ROWS + 3, u, 0, :], TP[ROWS:ROWS + 3, :],
                                         ACT.Copy).then_inc(m_placed, 1)
                copy = lambda o, x: nc.scalar.activation(o, x, ACT.Copy)
                if not cap:
                    if not kper:
                        cast_k(copy, 0, 0, 0).then_inc(k_cast, 1)
                    for u in range(4):
                        cast_head(act, copy, 0, u, u)
                if kx:
                    place_maxima(0, 0)

                def head(i, u, n):
                    if not cap and more(n, 4):
                        cast_head(act, copy, *at(i, u, 4), None)
                    for s in range(NS):
                        if cap:
                            squash(i, u, s)
                            if s:
                                expo(i, u, s - 1)
                            elif late(n, 1):
                                ii, uu = (i, u - 1) if u else (i - 1, U - 1)
                                expo(ii, uu, NS - 1)
                        else:
                            expo(i, u, s)
                        if s == 1 and kx and more(n, 1):
                            place_maxima(*at(i, u, 1))
                run(act, head)
                if cap:
                    expo(NH // U - 1, U - 1, NS - 1)

            @block.vector
            def _(dve):
                links = Links(dve, vlink)
                links(nc.vector.memset(QT[ROWS:P, :, :, :], 0.0))
                links(nc.vector.memset(KT[ROWS:P, :, :, :], 0.0))
                if kx:
                    links(nc.vector.memset(KT[ROWS:ROWS + 3, :, 0, :], 1.0))
                    links(nc.vector.memset(MX[:, :, :], -3.0e38))
                dve.sem_inc(ones_set, 1)

                def untangle(dst, use):
                    dve.wait_ge(turned, use + 1)
                    nc.vector.tensor_copy(dst[0:ROWS, :], TP[0:ROWS, :]).then_inc(untangled, 1)

                def untangle_part(i, u, x):
                    if kper:
                        untangle((KT, QT)[x][:, u, 0, :], tuses(i, u) + x)
                    else:
                        untangle(QT[:, u, x, :], tuses(i, u) + x)

                def maxima(i, u, cs):
                    for ci in cs:
                        qb, a, e = chunks[ci]
                        n = (i * U + u) * NC + ci
                        dve.wait_ge(mx_ready, n + 1)
                        nc.vector.tensor_reduce(MX[:, qb, (a // 4):(a // 4) + 1],
                                                S1[(u * NC + ci) % 2][:, 0:(e - a) * P], AX.X,
                                                ALU.max).then_inc(mx_taken, 1)

                def split_maxima(i, u):
                    n = i * U + u
                    links = Links(dve, vlink, clear=True)
                    dve.wait_ge(mx_taken, (n + 1) * NC)
                    links(nc.vector.tensor_reduce(M1[:, :], MX[:, :, :], AX.X, ALU.max))
                    if not (isinstance(n, int) and n < 1):
                        dve.wait_ge(m_turned, n)
                    links(nc.vector.tensor_scalar(MS[:, :, 0], M1[:, :], -1.0, None, ALU.mult))
                    links(nc.vector.scalar_tensor_tensor(M2[:, :], M1[:, :], -1.0, MS[:, :, 0],
                                                         ALU.mult, ALU.subtract))
                    links(nc.vector.tensor_copy(MS[:, :, 1], M2[:, :]))
                    links(nc.vector.tensor_tensor(MS[:, :, 2], M2[:, :], MS[:, :, 1], ALU.subtract))
                    dve.sem_inc(m_split, 1)

                def take_out(i, u):
                    n = i * U + u
                    dve.wait_ge(pv_done, (n + 1) * NS)
                    if not (isinstance(n, int) and n < 1):
                        dve.wait_ge(o_turned, n)
                    if cap:
                        nc.vector.tensor_tensor(
                            OT[:, :].rearrange("p (s q) -> p s q", q=P), O[:, :].rearrange("p (s q) -> p s q", q=P),
                            SV[:, bass.ds(kv_of(i, u), 1), :].rearrange("p a s -> p (a s)").unsqueeze(2).broadcast_to([P, NSL, P]),
                            ALU.add).then_inc(o_taken, 1)
                    else:
                        nc.vector.tensor_copy(OT[:, :], O[:, :]).then_inc(o_taken, 1)

                def divide(i, u):
                    n = i * U + u
                    dve.wait_ge(o_turned, n + 1)
                    if not (isinstance(n, int) and n < 1):
                        dve.wait_ge(y_done, n)
                    nc.vector.reciprocal(RC[:, :, :], tov[:, :, :, D]).then_inc(y_ready, 1)
                    dve.wait_ge(y_ready, n + 1)
                    nc.vector.tensor_tensor(Y[:, :, bass.ds(n * D, D)].rearrange("p (s g) d -> p s g d", g=NG),
                                            tov[:, :, :, 0:D],
                                            RC[:, :, :].unsqueeze(3).broadcast_to([P, NSL, NG, D]),
                                            ALU.mult).then_inc(y_done, 1)
                copy = lambda o, x: nc.vector.tensor_copy(o, x)
                if cap:
                    cast_head(dve, copy, 0, 0, 0)
                    cast_head(dve, copy, 0, 1, 1)
                if not kper:
                    for j in range(NSUB):
                        untangle(KT[:, 0, j, :], j)
                for u in range(3):
                    untangle_part(0, u, 0)
                    untangle_part(0, u, 1)
                    if cap and u < 2:
                        cast_head(dve, copy, 0, u + 2, u + 2)
                if kx:
                    for u in range(2):
                        maxima(0, u, range(NC))
                        split_maxima(0, u)

                def head(i, u, n):
                    before = (i, u - 1) if u else (i - 1, U - 1)
                    if kx and more(n, 2):
                        maxima(*at(i, u, 2), range(0, 3))
                    if more(n, 3):
                        untangle_part(*at(i, u, 3), 0)
                    if kx and more(n, 2):
                        maxima(*at(i, u, 2), range(3, 6))
                    if more(n, 3):
                        untangle_part(*at(i, u, 3), 1)
                    if late(n, 1):
                        take_out(*before)
                    if kx and more(n, 2):
                        maxima(*at(i, u, 2), range(6, NC))
                    if late(n, 1):
                        divide(*before)
                    if kx and more(n, 2):
                        split_maxima(*at(i, u, 2))
                    if cap and more(n, 4):
                        cast_head(dve, copy, *at(i, u, 4), None)
                run(dve, head)
                take_out(NH // U - 1, U - 1)
                divide(NH // U - 1, U - 1)


def segments(cap, NG, place):
    lists = [[(kb, qb) for kb in range(NT) for qb in range(kb, NT) if place[qb][1] == g] for g in range(NG)]
    per = cap // NG
    return [sorted(b for x in lists for b in x[a:a + per]) for a in range(0, len(lists[0]), per)]


def tile_places(NG):
    if NG == 4:
        order = [0, 1, 2, 3, 7, 6, 5, 4]
    else:
        order = [0, 1, 3, 2, 4, 5, 7, 6]
    return {t: (x // NG, x % NG) for x, t in enumerate(order)}


def turn_tokens(nc, core, name, Y, YT, identf, NG):
    done, free = core.sem(name + "_turned"), core.sem(name + "_taken")
    at = {t: s * NG + g for t, (s, g) in tile_places(NG).items()}
    with ExitStack() as c:
        ps = [c.enter_context(nc.psum_tensor(f"{name}_ps{i}", [P, C], F32)) for i in range(4)]
        with nc.Block() as block:
            @block.tensor
            def _(pe):
                for t in range(NT):
                    if t >= 4:
                        pe.wait_ge(free, t - 3)
                    for k in range(KC):
                        last = nc.tensor.transpose(ps[t % 4][:, k * P:(k + 1) * P], Y[:, at[t], k * P:(k + 1) * P],
                                                   identf[:, :])
                    last.then_inc(done, 1)

            @block.vector
            def _(dve):
                for t in range(NT):
                    dve.wait_ge(done, t + 1)
                    nc.vector.tensor_copy(YT[:, :, t * P:(t + 1) * P],
                                          ps[t % 4][:, :].rearrange("p (k n) -> p k n", k=KC)).then_inc(free, 1)


def close_layer(nc, core, name, X, XT, identf, product, gates=None, out=None):
    gates = gates or [None]
    NP = len(gates)
    LAG = 2
    S = lambda n: core.sem(f"{name}_{n}")
    made, added, link, var_done, root, scaled, normed, turned, taken, stored = (
        S("made"), S("added"), S("v"), S("var"), S("root"), S("scaled"), S("normed"), S("turned"), S("taken"),
        S("stored"))
    with ExitStack() as c:
        ps = [c.enter_context(nc.psum_tensor(f"{name}_ps{i}", [P, C], F32)) for i in range(4)]
        tp = [c.enter_context(nc.psum_tensor(f"{name}_tp{i}", [P, C], F32)) for i in range(4)]
        ST = c.enter_context(nc.sbuf_tensor(name + "_st", [P, NT, 6], F32))
        MV = c.enter_context(nc.sbuf_tensor(name + "_mv", [P, NT, 2], F32))
        RS = c.enter_context(nc.sbuf_tensor(name + "_rs", [P, NT], F32))
        NM = c.enter_context(nc.sbuf_tensor(name + "_nm", [P, NT], F32))
        with nc.Block() as block:
            @block.tensor
            def _(pe):
                def turn(t):
                    pe.wait_ge(normed, t + 1)
                    if t >= 4:
                        pe.wait_ge(taken, t - 3)
                    for k in range(KC):
                        last = nc.tensor.transpose(tp[t % 4][:, k * P:(k + 1) * P], X[:, t, k * P:(k + 1) * P],
                                                   identf[:, :])
                    last.then_inc(turned, 1)

                n = 0
                for t in range(NT):
                    for j in range(NP):
                        if n >= 4:
                            pe.wait_ge(added, n - 3)
                        mms = list(product(t, j))
                        for m, (lhsT, rhs, cols) in enumerate(mms):
                            last = nc.tensor.matmul(ps[n % 4][:, cols[0]:cols[1]], lhsT, rhs, start=(m == 0),
                                                    stop=(m == len(mms) - 1), skip_group_check=True)
                        last.then_inc(made, 1)
                        n += 1
                    if out is None and t >= LAG:
                        turn(t - LAG)
                if out is None:
                    for t in range(NT - LAG, NT):
                        turn(t)

            @block.vector
            def _(dve):
                links = Links(dve, link)

                def scales(t):
                    dve.wait_ge(root, t + 1)
                    links(nc.vector.reciprocal(RS[:, t:t + 1], RS[:, t:t + 1]))
                    nc.vector.scalar_tensor_tensor(NM[:, t:t + 1], MV[:, t, 0:1], -1.0, RS[:, t:t + 1], ALU.mult,
                                                   ALU.mult).then_inc(scaled, 1)

                def take(t):
                    dve.wait_ge(turned, t + 1)
                    nc.vector.tensor_copy(XT[:, :, t * P:(t + 1) * P],
                                          tp[t % 4][:, :].rearrange("p (k n) -> p k n", k=KC)).then_inc(taken, 1)

                n = 0
                for t in range(NT):
                    for j in range(NP):
                        dve.wait_ge(made, n + 1)
                        if n and j:
                            dve.wait_ge(added, n)
                        src = ps[n % 4][:, :]
                        if gates[j] is None:
                            nc.vector.tensor_tensor(X[:, t, :], X[:, t, :], src, ALU.add).then_inc(added, 1)
                        else:
                            nc.vector.scalar_tensor_tensor(X[:, t, :], src, gates[j](t), X[:, t, :],
                                                           ALU.mult, ALU.add).then_inc(added, 1)
                        n += 1
                    dve.wait_ge(added, n)
                    links(nc.vector.bn_stats(ST[:, t, :], X[:, t, :]))
                    links(nc.vector.bn_aggr(MV[:, t, :], ST[:, t, :]))
                    nc.vector.tensor_scalar(RS[:, t:t + 1], MV[:, t, 1:2], LN_EPS, None, ALU.add).then_inc(var_done, 1)
                    if t:
                        scales(t - 1)
                    if out is None and t >= LAG:
                        take(t - LAG)
                scales(NT - 1)
                if out is None:
                    for t in range(NT - LAG, NT):
                        take(t)

            @block.scalar
            def _(act):
                def normalise(t):
                    act.wait_ge(scaled, t + 1)
                    nc.scalar.activation(X[:, t, :], X[:, t, :], ACT.Identity, bias=NM[:, t:t + 1],
                                         scale=RS[:, t:t + 1]).then_inc(normed, 1)

                for t in range(NT):
                    act.wait_ge(var_done, t + 1)
                    nc.scalar.activation(RS[:, t:t + 1], RS[:, t:t + 1], ACT.Sqrt).then_inc(root, 1)
                    if t:
                        normalise(t - 1)
                normalise(NT - 1)

            if out is not None:
                @block.sync
                def _(sp):
                    sp.wait_ge(normed, NT)
                    sp.dma_start(out, X[:, :, :]).then_inc(stored, 16)
                    sp.wait_ge(stored, 16)


def hidden_gelu(nc, core, name, XT, W, bias, H):
    made, done = core.sem(name + "_made"), core.sem(name + "_done")
    with ExitStack() as c:
        ps = [c.enter_context(nc.psum_tensor(f"{name}_ps{i}", [P, CH], F32)) for i in range(4)]
        order = [(f, h) for f in range(NF) for h in range(NCH)]
        with nc.Block() as block:
            @block.tensor
            def _(pe):
                for n, (f, h) in enumerate(order):
                    if n >= 4:
                        pe.wait_ge(done, n - 3)
                    for k in range(KC):
                        last = nc.tensor.matmul(ps[n % 4][:, :], W[:, k, f * P:(f + 1) * P],
                                                XT[:, k, h * CH:(h + 1) * CH], start=(k == 0), stop=(k == KC - 1))
                    last.then_inc(made, 1)

            @block.scalar
            def _(act):
                for n, (f, h) in enumerate(order):
                    act.wait_ge(made, n + 1)
                    nc.scalar.activation(H[:, f, h * CH:(h + 1) * CH], ps[n % 4][:, :], ACT.Gelu,
                                         bias=bias[:, f:f + 1]).then_inc(done, 1)


def hidden_swiglu(nc, core, name, XT, items):
    gate_made, gate_done, up_done = core.sem(name + "_gmade"), core.sem(name + "_gdone"), core.sem(name + "_udone")
    with ExitStack() as c:
        pg = [c.enter_context(nc.psum_tensor(f"{name}_pg{i}", [P, CH], F32)) for i in range(4)]
        pu = [c.enter_context(nc.psum_tensor(f"{name}_pu{i}", [P, CH], F32)) for i in range(4)]
        G = [c.enter_context(nc.sbuf_tensor(f"{name}_g{i}", [P, CH], F32)) for i in range(2)]
        order = [(it, h) for it in items for h in range(NCH)]
        with nc.Block() as block:
            @block.tensor
            def _(pe):
                for n, ((gw, uw, rows, urow, M, dst), h) in enumerate(order):
                    if n >= 4:
                        pe.wait_ge(up_done, n - 3)
                    for k in range(KC):
                        last = nc.tensor.matmul(pg[n % 4][0:M, :], gw(k), XT[:, k, h * CH:(h + 1) * CH],
                                                start=(k == 0), stop=(k == KC - 1))
                    if uw is not None:
                        for k in range(KC):
                            last = nc.tensor.matmul(pu[n % 4][0:rows, :], uw(k), XT[:, k, h * CH:(h + 1) * CH],
                                                    start=(k == 0), stop=(k == KC - 1))
                    last.then_inc(gate_made, 1)

            @block.scalar
            def _(act):
                for n, ((gw, uw, rows, urow, M, dst), h) in enumerate(order):
                    act.wait_ge(gate_made, n + 1)
                    if n >= 2:
                        act.wait_ge(up_done, n - 1)
                    nc.scalar.activation(G[n % 2][0:rows, :], pg[n % 4][0:rows, :], ACT.Silu).then_inc(gate_done, 1)

            @block.vector
            def _(dve):
                for n, ((gw, uw, rows, urow, M, dst), h) in enumerate(order):
                    dve.wait_ge(gate_done, n + 1)
                    up = pu[n % 4][0:rows, :] if uw is not None else pg[n % 4][urow:urow + rows, :]
                    nc.vector.tensor_tensor(dst(h), G[n % 2][0:rows, :], up, ALU.mult).then_inc(up_done, 1)


def scan_mixer(nc, core, name, XT, W1X, W1IN, CW, CB, NA, XC, HM):
    S = lambda n: core.sem(f"{name}_{n}")
    conv, made, spd, da, bu, hm, vl, al = (S("conv"), S("made"), S("softplus"), S("decay"), S("bu"), S("hm"),
                                           S("v"), S("a"))
    with ExitStack() as c:
        ps = [c.enter_context(nc.psum_tensor(f"{name}_ps{i}", [SS, CH], F32)) for i in range(8)]

        def sb(n):
            return c.enter_context(nc.sbuf_tensor(f"{name}_{n}", [SS, CH], F32))

        AB, EX, DL, DA, BU = ([sb(f"{n}{h}") for h in range(NCH)] for n in ("ab", "ex", "dl", "da", "bu"))
        HS = [sb(f"hs{h}") for h in range(NCH)]
        with nc.Block() as block:
            @block.tensor
            def _(pe):
                for h in range(NCH):
                    for w in range(3):
                        for k in range(KC):
                            last = nc.tensor.matmul(ps[4 * h + w][:, :], W1X[:, k, w * SS:(w + 1) * SS],
                                                    XT[:, k, h * CH:(h + 1) * CH], start=(k == 0), stop=(k == KC - 1))
                    last.then_inc(made, 1)
                pe.wait_ge(conv, KC)
                for h in range(NCH):
                    for k in range(KC):
                        last = nc.tensor.matmul(ps[4 * h + 3][:, :], W1IN[:, k, :], XC[:, k, h * CH:(h + 1) * CH],
                                                start=(k == 0), stop=(k == KC - 1))
                    last.then_inc(made, 1)

            @block.vector
            def _(dve):
                links = Links(dve, vl)
                for k in range(KC):
                    links(nc.vector.tensor_scalar(XC[:, k, :], XT[:, k, :], CW[:, k, 3:4], CB[:, k:k + 1],
                                                  ALU.mult, ALU.add))
                    for j in range(1, 4):
                        ins = nc.vector.scalar_tensor_tensor(
                            XC[:, k, j:T], XT[:, k, 0:T - j], CW[:, k, 3 - j:4 - j], XC[:, k, j:T],
                            ALU.mult, ALU.add)
                        if j < 3:
                            links(ins)
                    ins.then_inc(conv, 1)
                for h in range(NCH):
                    dve.wait_ge(al, 3 * h + 3)
                    nc.vector.scalar_tensor_tensor(DL[h][:, :], ps[4 * h][:, :], 0.0, EX[h][:, :], ALU.max,
                                                   ALU.add).then_inc(spd, 1)
                dve.wait_ge(made, 4)
                for h in range(NCH):
                    dve.wait_ge(spd, h + 1)
                    links(nc.vector.tensor_tensor(BU[h][:, :], DL[h][:, :], ps[4 * h + 1][:, :], ALU.mult))
                    links(nc.vector.tensor_tensor(BU[h][:, :], BU[h][:, :], ps[4 * h + 3][:, :], ALU.mult))
                    dve.wait_ge(da, h + 1)
                    init = 0.0 if h == 0 else HS[h - 1][:, CH - 1:CH]
                    links(nc.vector.tensor_tensor_scan(HS[h][:, :], DA[h][:, :], BU[h][:, :], init,
                                                       ALU.mult, ALU.add))
                    links(nc.vector.tensor_tensor(HM[:, h * CH:(h + 1) * CH], HS[h][:, :], ps[4 * h + 2][:, :],
                                                  ALU.mult))

            @block.scalar
            def _(act):
                links = Links(act, al)
                for h in range(NCH):
                    act.wait_ge(made, h + 1)
                    links(nc.scalar.activation(AB[h][:, :], ps[4 * h][:, :], ACT.Abs))
                    links(nc.scalar.activation(EX[h][:, :], AB[h][:, :], ACT.Exp, scale=-1.0))
                    links(nc.scalar.activation(EX[h][:, :], EX[h][:, :], ACT.Ln, bias=1.0))
                for h in range(NCH):
                    act.wait_ge(spd, h + 1)
                    nc.scalar.activation(DA[h][:, :], DL[h][:, :], ACT.Exp, scale=NA[0:SS, 0:1]).then_inc(da, 1)


def retention(nc, core, name, XT, W, WB, DT, CS, KVS, GC, BM, BV, X2):
    S = lambda n: core.sem(f"{name}_{n}")
    made, moved = S("made"), S("moved")
    vmade, vmoved = S("vmade"), S("vmoved")
    qs_done, ks_done = S("qs"), S("ks")
    zeroed, spread, smade = S("zeroed"), S("spread"), S("state_part")
    sc, dec, outp, outd, st, stz, link = (S("scores"), S("decayed"), S("out"), S("out_taken"), S("state_updated"),
                                          S("state_zeroed"), S("v"))
    with ExitStack() as c:
        def sb(n, shape):
            return c.enter_context(nc.sbuf_tensor(f"{name}_{n}", shape, F32))

        Q, K, QS = sb("q", [P, KC, T]), sb("k", [P, KC, T]), sb("qs", [P, KC, T])
        QD = sb("qd", [P, KC, NT, 4, P])
        KV = sb("kv", [P, NT, 2 * C])
        AT = [sb(f"at{i}", [P, 4, P]) for i in range(2)]
        SD = sb("sd", [P, KC, P])
        TM = sb("tm", [P, KC, P])
        ps = [c.enter_context(nc.psum_tensor(f"{name}_ps{i}", [P, 512], F32)) for i in range(4)]
        PO = [c.enter_context(nc.psum_tensor(f"{name}_po{i}", [P, C], F32)) for i in range(2)]
        PS = [c.enter_context(nc.psum_tensor(f"{name}_pst{i}", [P, P], F32)) for i in range(2)]
        with nc.Block() as block:
            @block.tensor
            def _(pe):
                n = 0
                for w in range(2):
                    for m in range(KC):
                        for h in range(NCH):
                            if n >= 4:
                                pe.wait_ge(moved, n - 3)
                            for k in range(KC):
                                a = w * C + m * P
                                last = nc.tensor.matmul(ps[n % 4][:, :], W[:, k, a:a + P],
                                                        XT[:, k, h * CH:(h + 1) * CH], start=(k == 0),
                                                        stop=(k == KC - 1))
                            last.then_inc(made, 1)
                            n += 1
                for t in range(NT):
                    if t >= 4:
                        pe.wait_ge(vmoved, t - 3)
                    else:
                        pe.wait_ge(moved, 8 - 3 + t)
                    for k in range(KC):
                        last = nc.tensor.matmul(ps[t % 4][:, :], XT[:, k, t * P:(t + 1) * P], W[:, k, C:3 * C],
                                                start=(k == 0), stop=(k == KC - 1))
                    last.then_inc(vmade, 1)

            @block.scalar
            def _(act):
                n = 0
                for w in range(2):
                    for m in range(KC):
                        for h in range(NCH):
                            act.wait_ge(made, n + 1)
                            nc.scalar.activation((Q, K)[w][:, m, h * CH:(h + 1) * CH], ps[n % 4][:, :],
                                                 ACT.Identity, bias=WB[:, w * KC + m:w * KC + m + 1]).then_inc(moved, 1)
                            n += 1
                act.wait_ge(zeroed, 1)
                act.wait_ge(moved, 4)
                for m in range(KC):
                    for i in range(4):
                        r = slice(32 * i, 32 * i + 32)
                        nc.scalar.activation(QD[r, m, :, i, :], Q[r, m, :].rearrange("p (t i) -> p t i", i=P),
                                             ACT.Copy).then_inc(spread, 1)

            @block.vector
            def _(dve):
                nc.vector.memset(SD[:, :, :], 0.0).then_inc(stz, 1)
                nc.vector.memset(QD[:, :, :, :, :], 0.0).then_inc(zeroed, 1)
                for t in range(NT):
                    dve.wait_ge(vmade, t + 1)
                    nc.vector.tensor_tensor(KV[:, t, :], ps[t % 4][:, :], BV, ALU.add).then_inc(vmoved, 1)
                    dve.wait_ge(vmoved, t + 1)
                    nc.vector.tensor_tensor(KV[:, t, 0:C], KV[:, t, 0:C], KVS, ALU.mult).then_inc(ks_done, 1)

            @block.gpsimd
            def _(pool):
                pool.wait_ge(moved, 4)
                for m in range(KC):
                    nc.gpsimd.tensor_tensor(QS[:, m, :].rearrange("p (t i) -> p t i", i=P),
                                            Q[:, m, :].rearrange("p (t i) -> p t i", i=P),
                                            CS[:, m, :].unsqueeze(1).broadcast_to([P, NT, P]),
                                            ALU.mult).then_inc(qs_done, 1)
        steps = [(t, m) for t in range(NT) for m in range(KC)]
        with nc.Block() as block:
            @block.tensor
            def _(pe):
                def scores(n):
                    t, m = steps[n]
                    if n >= 2:
                        pe.wait_ge(dec, n - 1)
                    nc.tensor.matmul(ps[n % 2][:, :], K[:, m, t * P:(t + 1) * P],
                                     QD[:, m, t, :, :].rearrange("p h i -> p (h i)"), start=True,
                                     stop=True).then_inc(sc, 1)

                scores(0)
                scores(1)
                for n, (t, m) in enumerate(steps):
                    cols = slice(m * P, (m + 1) * P)
                    if t + 1 < NT:
                        if n >= 2:
                            pe.wait_ge(st, n - 1)
                        nc.tensor.matmul(PS[m][:, :], KV[:, t, cols], KV[:, t, C + m * P:C + (m + 1) * P],
                                         start=True, stop=True).then_inc(smade, 1)
                    if m == 0 and t >= 2:
                        pe.wait_ge(outd, t - 1)
                    if t:
                        pe.wait_ge(st, n - 1)
                        nc.tensor.matmul(PO[t % 2][:, cols], QS[:, m, t * P:(t + 1) * P], SD[:, m, :], start=True,
                                         stop=False, skip_group_check=True)
                    pe.wait_ge(dec, n + 1)
                    for i in range(4):
                        hc = m * P + i * RD
                        last = nc.tensor.matmul(PO[t % 2][:, hc:hc + RD], AT[n % 2][:, i, :],
                                                KV[:, t, C + hc:C + hc + RD], start=(t == 0 and i == 0), stop=True,
                                                skip_group_check=True)
                    last.then_inc(outp, 1)
                    if n + 2 < len(steps):
                        scores(n + 2)

            @block.vector
            def _(dve):
                def decay(n):
                    t, m = steps[n]
                    dve.wait_ge(sc, n + 1)
                    if n >= 2:
                        dve.wait_ge(outp, n - 1)
                    nc.vector.tensor_tensor(AT[n % 2][:, :, :], ps[n % 2][:, :].rearrange("p (h i) -> p h i", h=4),
                                            DT[:, m * 4:m * 4 + 4, :], ALU.mult).then_inc(dec, 1)

                links = Links(dve, link)
                decay(0)
                for n, (t, m) in enumerate(steps):
                    if n + 1 < len(steps):
                        decay(n + 1)
                    if t + 1 < NT:
                        dve.wait_ge(smade, n + 1)
                        if n >= 2:
                            dve.wait_ge(st, n - 1)
                        links(nc.vector.tensor_tensor(TM[:, m, :], PS[m][:, :], BM, ALU.mult))
                        dve.wait_ge(outp, n + 1)
                        nc.vector.scalar_tensor_tensor(SD[:, m, :], SD[:, m, :], GC[:, m:m + 1], TM[:, m, :],
                                                       ALU.mult, ALU.add).then_inc(st, 1)
                    if m == 1:
                        dve.wait_ge(outp, n + 1)
                        nc.vector.tensor_copy(X2[:, t, :], PO[t % 2][:, :]).then_inc(outd, 1)


def route(nc, core, name, XT, WR, GT, IDX):
    S = lambda n: core.sem(f"{name}_{n}")
    made, sub, ex, link = S("made"), S("sub"), S("exp"), S("v")
    with ExitStack() as c:
        def sb(n, shape):
            return c.enter_context(nc.sbuf_tensor(f"{name}_{n}", shape, F32))

        LG, PR, E1, E2, RM = (sb("lg", [P, NT, 9]), sb("pr", [P, NT, 8]), sb("e1", [P, NT, 8]),
                              sb("e2", [P, NT, 8]), sb("rm", [P, NT]))
        ps = c.enter_context(nc.psum_tensor(name + "_ps", [P, NT, 9], F32))
        with nc.Block() as block:
            @block.tensor
            def _(pe):
                for t in range(NT):
                    for k in range(KC):
                        last = nc.tensor.matmul(ps[:, t, :], XT[:, k, t * P:(t + 1) * P], WR[:, k, :],
                                                start=(k == 0), stop=(k == KC - 1))
                last.then_inc(made, 1)

            @block.scalar
            def _(act):
                act.wait_ge(sub, 1)
                nc.scalar.activation(LG[:, :, :], LG[:, :, :], ACT.Exp).then_inc(ex, 1)

            @block.vector
            def _(dve):
                links = Links(dve, link)
                row = lambda a: a.unsqueeze(2).broadcast_to([P, NT, 8])
                dve.wait_ge(made, 1)
                links(nc.vector.tensor_reduce(RM[:, :], ps[:, :, 0:8], AX.X, ALU.max))
                links(nc.vector.tensor_tensor(LG[:, :, 0:8], ps[:, :, 0:8], row(RM[:, :]), ALU.subtract))
                nc.vector.tensor_scalar(LG[:, :, 8], ps[:, :, 8], -1.0, None, ALU.mult).then_inc(sub, 1)
                dve.wait_ge(ex, 1)
                links(nc.vector.tensor_scalar(E1[:, :, 0], LG[:, :, 8], 1.0, None, ALU.add))
                links(nc.vector.reciprocal(GT[:, :, 8], E1[:, :, 0]))
                links(nc.vector.tensor_reduce(RM[:, :], LG[:, :, 0:8], AX.X, ALU.add))
                links(nc.vector.reciprocal(RM[:, :], RM[:, :]))
                links(nc.vector.tensor_tensor(PR[:, :, :], LG[:, :, 0:8], row(RM[:, :]), ALU.mult))
                idx = IDX.unsqueeze(1).broadcast_to([P, NT, 8])
                for r in range(2):
                    src = PR if r == 0 else E2
                    links(nc.vector.tensor_reduce(RM[:, :], src[:, :, :], AX.X, ALU.max))
                    links(nc.vector.tensor_tensor(E1[:, :, :], src[:, :, :], row(RM[:, :]), ALU.is_equal))
                    links(nc.vector.tensor_tensor(E1[:, :, :], E1[:, :, :], idx, ALU.mult))
                    links(nc.vector.tensor_reduce(RM[:, :], E1[:, :, :], AX.X, ALU.max))
                    links(nc.vector.tensor_tensor(E1[:, :, :], row(RM[:, :]), idx, ALU.is_equal))
                    if r == 0:
                        links(nc.vector.scalar_tensor_tensor(E2[:, :, :], E1[:, :, :], -2.0, PR[:, :, :],
                                                             ALU.mult, ALU.add))
                        links(nc.vector.tensor_tensor(GT[:, :, 0:8], E1[:, :, :], PR[:, :, :], ALU.mult))
                    else:
                        links(nc.vector.tensor_tensor(E1[:, :, :], E1[:, :, :], PR[:, :, :], ALU.mult))
                        links(nc.vector.tensor_tensor(GT[:, :, 0:8], GT[:, :, 0:8], E1[:, :, :], ALU.add))


RESIDENT = {
    "w0qkv": [P, KC, 384], "w0o": [P, KC, C], "bo": [1, C], "qkw0": [P, 320],
    "w0f1": [P, KC, FF], "w0f2": [P, NF, C], "b1": [P, NF], "b2": [1, C],
    "cos0": [P, NT, 8], "sin0": [P, NT, 2, 8],
    "w1x": [P, KC, 3 * SS], "w1in": [P, KC, SS], "w1out": [SS, C], "cw": [P, KC, 4], "cb": [P, KC],
    "alog": [SS, 1], "dd": [P, KC],
    "w2": [P, KC, 3 * C], "w2b": [P, 4], "w2bv": [P, 2 * C], "dt": [P, RH, P], "cs": [P, KC, P],
    "kvs": [P, C], "gc": [P, KC], "bm": [P, P],
    "wa": [P, KC, 3 * C], "wp": [P, KC, C], "wstd": [P, 16], "wrec": [P, 16],
    "w3": [P, KC, 320], "w3o": [P, KC, C], "qkw3": [P, 288], "cos3": [P, NT, 16], "sin3": [P, NT, 2, 16],
    "wr": [P, KC, 9], "idx": [P, 8], "identf": [P, P], "negq": [P, P], "negk": [P, P],
}
STREAMED = {
    "w1g": [P, KC, FF], "w1u": [P, KC, FF], "w1d": [P, NF, C],
    "sgu": [P, KC, 2 * SI], "sdn": [P, NSF, C], "w13": [P, KC, NE * ECOL], "wdn": [P, 2 * NE, C],
}


def build(nc, dram, out, stages=99):
    ctx = ExitStack()
    with ctx:
        def sb(name, shape, dt=F32):
            return ctx.enter_context(nc.sbuf_tensor(name, shape, dt))

        W = {n: sb("s_" + n, s) for n, s in RESIDENT.items()}
        X, XT = sb("X", [P, NT, C]), sb("XT", [P, KC, T])
        ident = sb("ident", [P, P], BF16)
        negq, negk = sb("negqb", [P, P], BF16), sb("negkb", [P, P], BF16)
        onesf = sb("onesf", [P, P])
        diag = sb("diag", [P, KC, P])
        NA = sb("NA", [SS, 1])
        e50 = sb("e50", [P, 1])
        onesrow = onesf[0:1, :]
        identf = W["identf"]
        with ExitStack() as c, Core(nc) as core:
            setup(nc, c, core, W, dram, ident, negq, negk, onesf, diag, NA, e50)
        with nc.Fori(0, B) as b, Core(nc) as whole:
            batch(nc, whole, b, dram, out, W, X, XT, ident, negq, negk, onesrow, onesf, diag, NA, e50, stages)


def setup(nc, c, core, W, dram, ident, negq, negk, onesf, diag, NA, e50):
    loaded, ones, link, red, summed, rooted, al = (
        core.sem(n) for n in ("loaded", "ones_made", "set_v", "reduced", "summed", "rooted", "set_a"))
    A = c.enter_context(nc.sbuf_tensor("absum", [P, 2], F32))
    A2 = c.enter_context(nc.sbuf_tensor("absum2", [P, 2], F32))
    NW = c.enter_context(nc.sbuf_tensor("neg_tern", [P, NF * C], F32))
    SC = c.enter_context(nc.sbuf_tensor("head_scales", [P, 3, 16], F32))
    WS = c.enter_context(nc.sbuf_tensor("wa_raw", [P, KC, 3 * C], F32))
    ps = c.enter_context(nc.psum_tensor("set_ps", [P, 2], F32))
    with nc.Block() as block:
        @block.sync
        def _(sp):
            for n, t in W.items():
                sp.dma_start(t[tuple(slice(None) for _ in t.shape)], dram[n]).then_inc(loaded, 16)
            sp.wait_ge(loaded, 16 * len(W))

        @block.vector
        def _(dve):
            links = Links(dve, link)
            links(nc.vector.memset(onesf[:, :], 1.0))
            links(nc.vector.memset(e50[:, :], E50))
            dve.wait_ge(loaded, 16 * len(W))
            links(nc.vector.tensor_copy(ident[:, :], W["identf"][:, :]))
            links(nc.vector.tensor_copy(negq[:, :], W["negq"][:, :]))
            links(nc.vector.tensor_copy(negk[:, :], W["negk"][:, :]))
            for k in range(KC):
                links(nc.vector.tensor_scalar(diag[:, k, :], W["identf"][:, :], W["dd"][:, k:k + 1], None, ALU.mult))
            w1, w2 = W["w0f1"][:, :, :], W["w0f2"][:, :, :]
            links(nc.vector.tensor_reduce(A[:, 0:1], w1, AX.XY, ALU.add, apply_absolute_value=True))
            nc.vector.tensor_reduce(A[:, 1:2], w2, AX.XY, ALU.add, apply_absolute_value=True).then_inc(red, 1)
            dve.wait_ge(summed, 1)
            links(nc.vector.tensor_scalar(A[:, :], ps[:, :], 1.0 / (FF * C), 0.7, ALU.mult, ALU.mult))
            links(nc.vector.tensor_scalar(A2[:, :], A[:, :], -1.0, None, ALU.mult))
            for j, w in enumerate((w1, w2)):
                nw = NW[:, :].rearrange("p (a n) -> p a n", a=w.shape[1])
                links(nc.vector.tensor_scalar(nw, w, A2[:, j:j + 1], None, ALU.is_le))
                links(nc.vector.tensor_scalar(w, w, A[:, j:j + 1], None, ALU.is_ge))
                links(nc.vector.tensor_tensor(w, w, nw, ALU.subtract))
            links(nc.vector.tensor_scalar(SC[:, 2, :], W["wrec"][:, :], 0.1, None, ALU.is_gt))
            links(nc.vector.tensor_scalar(SC[:, 0, :], W["wstd"][:, :], 1e-8, None, ALU.max))
            nc.vector.tensor_scalar(SC[:, 1, :], W["wrec"][:, :], 1e-8, None, ALU.max).then_inc(red, 1)
            dve.wait_ge(rooted, 1)
            wa = W["wa"]
            links(nc.vector.tensor_copy(WS[:, :, :], wa[:, :, :]))
            for k in range(KC):
                raw = lambda a: WS[:, k, a:a + 128].rearrange("p (h d) -> p h d", h=16)
                new = lambda a, lo: wa[:, k, a:a + 256].rearrange("p (h d) -> p h d", h=16)[:, :, lo:lo + 8]
                s = lambda j: SC[:, j, :].unsqueeze(2).broadcast_to([P, 16, 8])
                links(nc.vector.tensor_tensor(new(0, 0), raw(0), s(0), ALU.mult))
                links(nc.vector.tensor_tensor(new(C, 0), raw(128), s(0), ALU.mult))
                links(nc.vector.tensor_copy(wa[:, k, 2 * C:3 * C], WS[:, k, 256:512]))
                tq, tk = new(0, 8), new(C, 8)
                links(nc.vector.tensor_scalar(NW[:, 0:16], SC[:, 2, :], -1.0, 1.0, ALU.mult, ALU.add))
                no = NW[:, 0:16].unsqueeze(2).broadcast_to([P, 16, 8])
                t1 = NW[:, 128:256].rearrange("p (h d) -> p h d", h=16)
                for dst, keep, swap in ((tq, raw(512), raw(640)), (tk, raw(640), raw(512))):
                    links(nc.vector.tensor_tensor(dst, keep, no, ALU.mult))
                    links(nc.vector.tensor_tensor(t1, swap, s(2), ALU.mult))
                    links(nc.vector.tensor_tensor(dst, dst, t1, ALU.add))
                    links(nc.vector.tensor_tensor(dst, dst, s(1), ALU.mult))
            dve.wait_ge(al, 1)
            links(nc.vector.tensor_scalar(NA[:, :], NA[:, :], -1.0, None, ALU.mult))

        @block.tensor
        def _(pe):
            pe.wait_ge(red, 1)
            nc.tensor.matmul(ps[:, :], onesf[:, :], A[:, :], start=True, stop=True).then_inc(summed, 1)

        @block.scalar
        def _(act):
            act.wait_ge(loaded, 16 * len(W))
            nc.scalar.activation(NA[:, :], W["alog"][:, :], ACT.Exp).then_inc(al, 1)
            act.wait_ge(red, 2)
            nc.scalar.activation(SC[:, 0:2, :], SC[:, 0:2, :], ACT.Sqrt).then_inc(rooted, 1)


def batch(nc, whole, b, dram, out, W, X, XT, ident, negq, negk, onesrow, onesf, diag, NA, e50, stages):
    identf = W["identf"]
    tok = lambda t: slice(t * P, (t + 1) * P)
    got = whole.sem("tokens_loaded")
    with nc.Block() as block:
        @block.sync
        def _(sp):
            sp.dma_start(X[:, :, :], dram["x"][:, bass.ds(b * NT, NT), :]).then_inc(got, 16)
            sp.dma_start(XT[:, :, :], dram["xt"][:, :, bass.ds(b * T, T)]).then_inc(got, 16)
            sp.wait_ge(got, 32)

    def dense(YT, w, bias=None):
        def product(t, j):
            for k in range(KC):
                yield YT[:, k, tok(t)], w[:, k, :], (0, C)
            if bias is not None:
                yield onesrow, bias[0:1, :], (0, C)
        return product

    def hidden(H, w, bias=None):
        def product(t, j):
            for f in range(NF):
                yield H[:, f, tok(t)], w[:, f, :], (0, C)
            if bias is not None:
                yield onesrow, bias[0:1, :], (0, C)
        return product

    def done(i):
        return out[:, bass.ds(b * NT, NT), :] if i == min(stages, 8) else None

    with ExitStack() as c, Core(nc) as core:
        def sb(name, shape, dt=F32):
            return c.enter_context(nc.sbuf_tensor(name, shape, dt))
        QK, V, Y, YT = sb("a0qk", [P, NT, 320]), sb("a0v", [P, NT, 64]), sb("a0y", [P, NT, C]), sb("a0yt", [P, KC, T])
        SV, SVT = sb("a0sv", [P, NT, 4, 32]), sb("a0svt", [P, 4, 2])
        project_tokens(nc, core, "p0", XT, W["w0qkv"],
                       [(0, 320, lambda t, a, e: QK[:, t, a:e]),
                        (320, 384, lambda t, a, e: V[:, t, a:e])])
        vsum, vready, vmade, vtaken = (core.sem("a0_" + n) for n in ("vsum", "vready", "vmade", "vtaken"))
        places = tile_places(4)
        with ExitStack() as c2:
            ps = c2.enter_context(nc.psum_tensor("a0_vps", [P, 4, 2], F32))
            with nc.Block() as block:
                @block.gpsimd
                def _(pool):
                    links = Links(pool, vsum)
                    for qb in range(NT - 1):
                        links(nc.gpsimd.memset(SV[:, qb, :, 16:32], float(NT - 1 - qb)))
                    v = lambda t: V[:, t, :].rearrange("p (h d) -> p h d", h=4)
                    links(nc.gpsimd.memset(SV[:, NT - 1, :, :], 0.0))
                    links(nc.gpsimd.tensor_copy(SV[:, NT - 2, :, 0:16], v(NT - 1)))
                    for qb in range(NT - 3, -1, -1):
                        links(nc.gpsimd.tensor_tensor(SV[:, qb, :, 0:16], SV[:, qb + 1, :, 0:16], v(qb + 1), ALU.add))
                    pool.sem_inc(vready, 1)

                @block.tensor
                def _(pe):
                    pe.wait_ge(vready, 1)
                    for qb in range(NT):
                        sl, gr = places[qb]
                        for h in range(4):
                            last = nc.tensor.matmul(ps[gr * 32:(gr + 1) * 32, h, sl:sl + 1], SV[:, qb, h, :],
                                                    e50[:, :], start=True, stop=True, skip_group_check=True)
                    last.then_inc(vmade, 1)

                @block.vector
                def _(dve):
                    dve.wait_ge(vmade, 1)
                    nc.vector.tensor_copy(SVT[:, :, :], ps[:, :, :]).then_inc(vtaken, 1)
        norm_rope(nc, core, "r0", QK, 20, 16, W["qkw0"][:, :], W["cos0"][:, :, :], W["sin0"][:, :, :, :], False)
        attention(nc, core, "a0", QK, V, Y, (ident, identf, negq, negk), D=16, NH=16, q0=0, k0=256,
                  kv_of=lambda i, u: i, kper=True, cap=True, scale=0.25,
                  SV=SVT, U=4)
        turn_tokens(nc, core, "y0", Y, YT, identf, 4)
        close_layer(nc, core, "c0", X, XT, identf, dense(YT, W["w0o"], W["bo"]), out=done(1))
    if stages <= 1:
        return
    with ExitStack() as c, Core(nc) as core:
        H = c.enter_context(nc.sbuf_tensor("f0h", [P, NF, T], F32))
        hidden_gelu(nc, core, "f0", XT, W["w0f1"], W["b1"], H)
        close_layer(nc, core, "c1", X, XT, identf, hidden(H, W["w0f2"], W["b2"]), out=done(2))
    if stages <= 2:
        return
    with ExitStack() as c:
        w1 = {n: c.enter_context(nc.sbuf_tensor("s_" + n, STREAMED[n], F32)) for n in ("w1g", "w1u", "w1d")}
        sent = whole.sem("w1_loaded")
        with nc.Block() as block:
            @block.sync
            def _(sp):
                for n, t in w1.items():
                    sp.dma_start(t[:, :, :], dram[n]).then_inc(sent, 16)
        with ExitStack() as c2, Core(nc) as core:
            XC = c2.enter_context(nc.sbuf_tensor("m1xc", [P, KC, T], F32))
            HM = c2.enter_context(nc.sbuf_tensor("m1hm", [SS, T], F32))
            scan_mixer(nc, core, "m1", XT, W["w1x"], W["w1in"], W["cw"], W["cb"], NA, XC, HM)

            def product(t, j):
                yield HM[:, tok(t)], W["w1out"][:, :], (0, C)
                for k in range(KC):
                    yield XC[:, k, tok(t)], diag[:, k, :], (k * P, (k + 1) * P)
            close_layer(nc, core, "c2", X, XT, identf, product, out=done(3))
        if stages <= 3:
            return
        with nc.Block() as block:
            @block.sync
            def _(sp):
                sp.wait_ge(sent, 48)
        core = c.enter_context(Core(nc))
        H = c.enter_context(nc.sbuf_tensor("f1h", [P, NF, T], F32))
        items = [(lambda k, f=f: w1["w1g"][:, k, tok(f)], lambda k, f=f: w1["w1u"][:, k, tok(f)], P, 0, P,
                  lambda h, f=f: H[:, f, h * CH:(h + 1) * CH]) for f in range(NF)]
        hidden_swiglu(nc, core, "f1", XT, items)
        close_layer(nc, core, "c3", X, XT, identf, hidden(H, w1["w1d"]), out=done(4))
    if stages <= 4:
        return
    with ExitStack() as c, Core(nc) as core:
        X2 = c.enter_context(nc.sbuf_tensor("m2x", [P, NT, C], F32))
        retention(nc, core, "m2", XT, W["w2"], W["w2b"], W["dt"], W["cs"], W["kvs"][:, :], W["gc"], W["bm"][:, :],
                  W["w2bv"][:, :], X2)
        close_layer(nc, core, "c4", X, XT, identf, lambda t, j: iter([(identf[:, :], X2[:, t, :], (0, C))]),
                    out=done(5))
    if stages <= 5:
        return
    with ExitStack() as c, Core(nc) as core:
        def sb(name, shape, dt=F32):
            return c.enter_context(nc.sbuf_tensor(name, shape, dt))
        QK, V, Y, YT = sb("a2qk", [P, NT, 512]), sb("a2v", [P, NT, 256]), sb("a2y", [P, NT, C]), sb("a2yt", [P, KC, T])
        project_tokens(nc, core, "p2", XT, W["wa"],
                       [(0, 512, lambda t, a, e: QK[:, t, a:e]),
                        (512, 768, lambda t, a, e: V[:, t, a:e])])
        attention(nc, core, "a2", QK, V, Y, (ident, identf, negq, negk), D=16, NH=16, q0=0, k0=256,
                  kv_of=lambda i, u: i * 4 + u, kper=True, cap=False, scale=0.25,
                  SV=None, U=4)
        turn_tokens(nc, core, "y2", Y, YT, identf, 4)
        close_layer(nc, core, "c5", X, XT, identf, dense(YT, W["wp"]), out=done(6))
    if stages <= 6:
        return
    with ExitStack() as c:
        w3 = {n: c.enter_context(nc.sbuf_tensor("s_" + n, STREAMED[n], F32)) for n in ("sgu", "sdn", "w13", "wdn")}
        sent3 = whole.sem("w3_loaded")
        with nc.Block() as block:
            @block.sync
            def _(sp):
                for n, t in w3.items():
                    sp.dma_start(t[:, :, :], dram[n]).then_inc(sent3, 16)
        with ExitStack() as c2, Core(nc) as core:
            def sb(name, shape, dt=F32):
                return c2.enter_context(nc.sbuf_tensor(name, shape, dt))
            QK, V, Y, YT = sb("a3qk", [P, NT, 288]), sb("a3v", [P, NT, 32]), sb("a3y", [P, NT, C]), sb("a3yt", [P, KC, T])
            project_tokens(nc, core, "p3", XT, W["w3"],
                           [(0, 288, lambda t, a, e: QK[:, t, a:e]),
                            (288, 320, lambda t, a, e: V[:, t, 0:32])])
            norm_rope(nc, core, "r3", QK, 9, 32, W["qkw3"][:, :], W["cos3"][:, :, :], W["sin3"][:, :, :, :], True)
            attention(nc, core, "a3", QK, V, Y, (ident, identf, negq, negk), D=32, NH=8, q0=0, k0=256,
                      kv_of=lambda i, u: 0, kper=False, cap=False, scale=1.0 / 16.0,
                      SV=None, U=4)
            turn_tokens(nc, core, "y3", Y, YT, identf, 2)
            close_layer(nc, core, "c6", X, XT, identf, dense(YT, W["w3o"]), out=done(7))
        if stages <= 7:
            return
        with nc.Block() as block:
            @block.sync
            def _(sp):
                sp.wait_ge(sent3, 64)
        core = c.enter_context(Core(nc))
        GT = c.enter_context(nc.sbuf_tensor("f3gt", [P, NT, 9], F32))
        route(nc, core, "g3", XT, W["wr"], GT, W["idx"][:, :])
        H = c.enter_context(nc.sbuf_tensor("f3h", [P, NSF, T], F32))
        parts = [("shared", None)] + [("experts", (e, e + 2)) for e in range(0, NE, 2)]
        for pi, (kind, es) in enumerate(parts):
            items = []
            if kind == "shared":
                for f in range(NSF):
                    r = min(P, SI - f * P)
                    items.append((lambda k, f=f, r=r: w3["sgu"][:, k, f * P:f * P + r],
                                  lambda k, f=f, r=r: w3["sgu"][:, k, SI + f * P:SI + f * P + r], r, 0, r,
                                  lambda h, f=f, r=r: H[0:r, f, h * CH:(h + 1) * CH]))
            else:
                for s, e in enumerate(range(*es)):
                    a = e * ECOL
                    items.append((lambda k, a=a: w3["w13"][:, k, a:a + P], lambda k, a=a: w3["w13"][:, k, a + P:a + 2 * P],
                                  P, 0, P, lambda h, s=s: H[:, 2 * s, h * CH:(h + 1) * CH]))
                    items.append((lambda k, a=a: w3["w13"][:, k, a + 2 * P:a + ECOL], None, EREM, 64, 64 + EREM,
                                  lambda h, s=s: H[0:EREM, 2 * s + 1, h * CH:(h + 1) * CH]))
            hidden_swiglu(nc, core, f"h3_{pi}", XT, items)
            if kind == "shared":
                def product(t, j):
                    for f in range(NSF):
                        r = min(P, SI - f * P)
                        yield H[0:r, f, tok(t)], w3["sdn"][0:r, f, :], (0, C)
                gates = [lambda t: GT[:, t, 8:9]]
            else:
                def product(t, j, es=es):
                    yield H[:, 2 * j, tok(t)], w3["wdn"][:, 2 * (es[0] + j), :], (0, C)
                    yield H[0:EREM, 2 * j + 1, tok(t)], w3["wdn"][0:EREM, 2 * (es[0] + j) + 1, :], (0, C)
                gates = [lambda t, e=e: GT[:, t, e:e + 1] for e in range(*es)]
            if pi == len(parts) - 1:
                close_layer(nc, core, "c7", X, XT, identf, product, gates, out=done(8))
            else:
                add_parts(nc, core, f"d3_{pi}", X, product, gates)


def add_parts(nc, core, name, X, product, gates):
    made, added = core.sem(name + "_made"), core.sem(name + "_added")
    with ExitStack() as c:
        ps = [c.enter_context(nc.psum_tensor(f"{name}_ps{i}", [P, C], F32)) for i in range(4)]
        order = [(t, j) for t in range(NT) for j in range(len(gates))]
        with nc.Block() as block:
            @block.tensor
            def _(pe):
                for n, (t, j) in enumerate(order):
                    if n >= 4:
                        pe.wait_ge(added, n - 3)
                    mms = list(product(t, j))
                    for m, (lhsT, rhs, cols) in enumerate(mms):
                        last = nc.tensor.matmul(ps[n % 4][:, cols[0]:cols[1]], lhsT, rhs, start=(m == 0),
                                                stop=(m == len(mms) - 1))
                    last.then_inc(made, 1)

            @block.vector
            def _(dve):
                for n, (t, j) in enumerate(order):
                    dve.wait_ge(made, n + 1)
                    if j:
                        dve.wait_ge(added, n)
                    nc.vector.scalar_tensor_tensor(X[:, t, :], ps[n % 4][:, :], gates[j](t), X[:, t, :],
                                                   ALU.mult, ALU.add).then_inc(added, 1)


def tables():
    f = np.float32
    d = {}

    def rope(theta, dim, sign):
        inv = 1.0 / theta ** (np.arange(0, dim, 2, dtype=np.float64) / dim)
        fr = np.outer(np.arange(T), inv.astype(f)).astype(f)
        fr = fr.reshape(NT, P, dim // 2).transpose(1, 0, 2)
        return np.cos(fr).astype(f), np.stack([sign * np.sin(fr), -sign * np.sin(fr)], axis=2).astype(f)

    d["cos0"], d["sin0"] = rope(10000.0, 16, 1.0)
    d["cos3"], d["sin3"] = rope(1000000.0, 32, -1.0)
    betas = np.linspace(np.log2(1.0 / 32.0), np.log2(1.0 / 512.0), RH)
    g = 1.0 - np.exp2(betas)
    i = np.arange(P)
    ij = i[None, :] - i[:, None]
    d["dt"] = np.where(ij[:, None, :] >= 0, g[None, :, None] ** np.maximum(ij, 0)[:, None, :], 0.0).astype(f)
    hp = np.repeat(np.arange(4), RD)
    gh = np.stack([g[4 * m + hp] for m in range(KC)], axis=1)
    d["cs"] = (gh[:, :, None] ** (i + 1)[None, None, :]).astype(f)
    d["kvs"] = (np.repeat(g, RD)[None, :] ** (P - 1 - i)[:, None]).astype(f)
    d["gc"] = (gh ** P).astype(f)
    d["bm"] = (hp[:, None] == hp[None, :]).astype(f)
    d["idx"] = np.tile(np.arange(8, 0, -1).astype(f), (P, 1))
    d["identf"] = np.eye(P, dtype=f)
    d["negq"] = np.where(i[None, :] > i[:, None], NEG, 0.0).astype(f)
    d["negk"] = np.where(i[:, None] > i[None, :], NEG, 0.0).astype(f)
    return d


def layout(a):
    def kn(w):
        return w.reshape(w.shape[0] // P, P, w.shape[1]).transpose(1, 0, 2)

    def col(v):
        return v.reshape(-1, P).T

    def rows(v):
        return np.broadcast_to(v[None, :], (P, v.shape[0]))

    d = {}
    x = a["L0_attn_x"].reshape(B * T, C)
    d["x"] = x.reshape(B * NT, P, C).transpose(1, 0, 2)
    d["xt"] = kn(x.T)
    d["w0qkv"] = kn(np.concatenate([a["L0_attn_Wq"], a["L0_attn_Wk"], a["L0_attn_Wv"]], 0).T)
    d["w0o"], d["bo"] = kn(a["L0_attn_Wo"].T), a["L0_attn_bo"][None, :]
    d["qkw0"] = rows(np.concatenate([np.tile(a["L0_attn_q_norm_w"], 16), np.tile(a["L0_attn_k_norm_w"], 4)]))
    d["w0f1"], d["w0f2"] = kn(a["L0_ffn_w1"].T), kn(a["L0_ffn_w2"].T)
    d["b1"], d["b2"] = col(a["L0_ffn_b1"]), a["L0_ffn_b2"][None, :]
    wx = a["L1_attn_Wxproj"]
    d["w1x"] = kn(np.concatenate([np.repeat(wx[2 * SS:], SS, 0), wx[:2 * SS]], 0).T)
    d["w1in"], d["w1out"] = kn(a["L1_attn_Winproj"].T), a["L1_attn_Woutproj"].T
    d["cw"] = a["L1_attn_conv_w"].reshape(KC, P, 4).transpose(1, 0, 2)
    d["cb"], d["alog"], d["dd"] = col(a["L1_attn_conv_b"]), a["L1_attn_A_log"][:, None], col(a["L1_attn_D"])
    d["w1g"], d["w1u"], d["w1d"] = kn(a["L1_ffn_w_gate"].T), kn(a["L1_ffn_w_up"].T), kn(a["L1_ffn_w_down"].T)
    d["w2"] = kn(np.concatenate([a["L2_attn_Wq"], a["L2_attn_Wk"], a["L2_attn_Wv"]], 1))
    d["w2b"] = np.concatenate([col(a["L2_attn_bq"]), col(a["L2_attn_bk"])], 1)
    d["w2bv"] = rows(np.concatenate([a["L2_attn_bk"], a["L2_attn_bv"]]))
    d["wa"], d["wp"] = kn(a["L2_ffn_Wa"]), kn(a["L2_ffn_Wp"])
    d["wstd"], d["wrec"] = rows(a["L2_ffn_w_std"]), rows(a["L2_ffn_w_rec"])
    d["w3"] = kn(np.concatenate([a["L3_attn_q_proj"], a["L3_attn_k_proj"], a["L3_attn_v_proj"]], 0).T)
    d["w3o"] = kn(a["L3_attn_o_proj"].T)
    d["qkw3"] = rows(np.concatenate([np.tile(a["L3_attn_q_norm"], 8), a["L3_attn_k_norm"]]))
    d["wr"] = kn(np.concatenate([a["L3_ffn_gate_w"], a["L3_ffn_shared_gate_w"]], 0).T)
    d["sgu"] = kn(a["L3_ffn_shared_gate_up_w"].T)
    z = lambda *s: np.zeros(s, np.float32)
    d["sdn"] = kn(np.concatenate([a["L3_ffn_shared_down_w"].T, z(NSF * P - SI, C)], 0))
    w13 = a["L3_ffn_w13"]
    w13 = np.concatenate([w13[:, :P], w13[:, EI:EI + P], w13[:, P:EI], z(NE, 64 - EREM, C), w13[:, EI + P:]], 1)
    d["w13"] = kn(w13.reshape(NE * ECOL, C).T)
    w2 = np.concatenate([a["L3_ffn_w2"].transpose(0, 2, 1), z(NE, 2 * P - EI, C)], 1)
    d["wdn"] = kn(w2.reshape(NE * 2 * P, C))
    d.update(tables())
    return {k: np.ascontiguousarray(v) for k, v in d.items()}


def kernel(**inputs):
    import concourse.bacc as bacc
    from concourse.bass_utils import run_bass_kernel_spmd

    data = layout({k: np.asarray(v) for k, v in inputs.items()})
    nc = bacc.Bacc("TRN2", target_bir_lowering=False, num_devices=1)
    dram = {k: nc.dram_tensor(f"in_{k}", list(v.shape), F32, kind="ExternalInput").ap() for k, v in data.items()}
    out = nc.dram_tensor("out_tokens", [P, B * NT, C], F32, kind="ExternalOutput").ap()
    build(nc, dram, out, STAGES)
    r = run_bass_kernel_spmd(nc, [{f"in_{k}": v for k, v in data.items()}], core_ids=[0])
    y = r.results[0]["out_tokens"]
    return y.transpose(1, 0, 2).reshape(B, T, C)


STAGES = 99
```

```python
import math
from contextlib import ExitStack

import numpy as np

import concourse.bass as bass
from concourse import mybir

F32 = mybir.dt.float32
BF16 = mybir.dt.bfloat16
FR = mybir.dt.float32r
ALU = mybir.AluOpType
ACT = mybir.ActivationFunctionType
AX = mybir.AxisListType

B, T, C = 4, 1024, 256
P = 128
NT = T // P
KC = C // P
CH = 512
NCH = T // CH
FF = 1024
NF = FF // P
TERMS = 6
NEG = -1.0e30
E50 = math.exp(-50.0)
RH = 8
RD = C // RH
LOW = 32
SS = 64
NE, EI = 8, 176
EREM = EI - P
ECOL = 2 * P + 64 + EREM
SI = 704
NSF = (SI + P - 1) // P
LN_EPS = 1e-5


class Links:

    def __init__(self, eng, sem, clear=False):
        self.eng, self.sem, self.n = eng, sem, 0
        if clear:
            eng.sem_clear(sem)

    def later(self, ins):
        self.n += 1
        ins.then_inc(self.sem, 1)

    def __call__(self, ins):
        self.later(ins)
        self.eng.wait_ge(self.sem, self.n)


class Core:

    def __init__(self, nc):
        self.nc, self.sems = nc, []

    def __enter__(self):
        self.ctx = ExitStack()
        self.ctx.__enter__()
        return self

    def sem(self, name):
        s = self.ctx.enter_context(self.nc.semaphore(name))
        self.sems.append(s)
        return s

    def __exit__(self, *raised):
        if raised[0] is None:
            nc = self.nc
            for i, s in enumerate(self.sems):
                (nc.sync, nc.gpsimd, nc.scalar, nc.vector)[i % 4].sem_clear(s)
            self.nc.all_engine_barrier()
        return self.ctx.__exit__(*raised)


def high_part(nc, dst, src):
    return nc.vector.tensor_copy(dst, src)


def low_part(nc, dst, src, high):
    return nc.vector.tensor_tensor(dst, src, f32(high), ALU.subtract)


def cut_in_two(nc, links, high, low, raw):
    links(high_part(nc, high, raw))
    links(low_part(nc, low, raw, high))


def raw_and_low(nc, c, name, shape):
    with nc.sbuf_tensor(name + "_raw", shape, F32) as raw:
        pass
    return raw, c.enter_context(nc.sbuf_tensor(name, shape, FR))


def pairs(left, right):
    (lh, ll), (rh, rl) = left, right
    return [(lh, rh), (ll, rh)] if rl is None else [(lh, rh), (lh, rl), (ll, rh)]


def start_loads(sp, loads):
    for place, source, sem in loads:
        sp.dma_start(place, source).then_inc(sem, 16)


def f32(ap):
    return ap.bitcast(F32)


def project_tokens(nc, core, name, XT, W, outs, squares=None, loads=()):
    done, free = core.sem(name + "_projected"), core.sem(name + "_taken")
    cols = W[0].shape[2]
    parts = [(a, min(a + 512, cols)) for a in range(0, cols, 512)]
    with ExitStack() as c:
        ps = [c.enter_context(nc.psum_tensor(f"{name}_ps{i}", [P, 512], F32)) for i in range(4)]
        with nc.Block() as block:
            @block.sync
            def _(sp):
                start_loads(sp, loads)

            @block.tensor
            def _(pe):
                n = 0
                for t in range(NT):
                    for a, e in parts:
                        if n >= 4:
                            pe.wait_ge(free, n - 3)
                        mms = [m for k in range(KC) for m in pairs([x[:, k, t * P:(t + 1) * P] for x in XT],
                                                                   [w[:, k, a:e] for w in W])]
                        for i, (x, w) in enumerate(mms):
                            last = nc.tensor.matmul(ps[n % 4][:, 0:e - a], x, w, start=(i == 0),
                                                    stop=(i == len(mms) - 1))
                        last.then_inc(done, 1)
                        n += 1

            @block.scalar
            def _(act):
                n = 0
                for t in range(NT):
                    for a, e in parts:
                        act.wait_ge(done, n + 1)
                        if squares is not None and a == 0:
                            nc.scalar.activation(squares[:, t, :], ps[n % 4][:, 0:squares.shape[2]], ACT.Square)
                        pieces = [(max(a, u), min(e, v), f, u) for u, v, f in outs if max(a, u) < min(e, v)]
                        for j, (u, v, f, base) in enumerate(pieces):
                            src = ps[n % 4][:, u - a:v - a]
                            dst = f(t, u - base, v - base)
                            if len(dst.shape) == 3:
                                src = src.rearrange("p (h d) -> p h d", d=dst.shape[2])
                            ins = nc.scalar.activation(dst, src, ACT.Copy)
                            if j == len(pieces) - 1:
                                ins.then_inc(free, 1)
                        n += 1


def norm_rope(nc, core, name, QK, SQ, nh, D, cosw, sinw, eps_in, PT, sums=None):
    S = lambda n: core.sem(f"{name}_{n}")
    ss_done, root_done, link, scaled, p_link = S("ss"), S("root"), S("v"), S("inverse"), S("p")
    vready, vmade, vtaken = S("vready"), S("vmade"), S("vtaken")
    h2 = D // 2
    nq = 16 if nh == 20 else nh - 1
    with ExitStack() as c:
        RT = c.enter_context(nc.sbuf_tensor(name + "_rot", [P, NT, nh * D], F32))
        R = c.enter_context(nc.sbuf_tensor(name + "_rms", [P, NT, nh], F32))
        if sums is not None:
            V, SV, SVT, e50 = sums
            ps = c.enter_context(nc.psum_tensor(name + "_vps", [P, 4, 2], F32))
        q4 = QK[:, :, :].rearrange("p t (h d) -> p t h d", d=D)
        r4 = RT[:, :, :].rearrange("p t (h d) -> p t h d", d=D)

        def rotate(eng, links, a, e):
            for g, (u, v) in enumerate(((0, nq), (nq, nh))):
                n = v - u
                for half in range(2):
                    to, other = slice(half * h2, (half + 1) * h2), slice((1 - half) * h2, (2 - half) * h2)
                    step = links if (g, half) == (1, 1) else links.later
                    step(eng.tensor_tensor(
                        r4[:, a:e, u:v, to], q4[:, a:e, u:v, other],
                        sinw[:, a:e, g, to].unsqueeze(2).broadcast_to([P, e - a, n, h2]), ALU.mult))
            for g, (u, v) in enumerate(((0, nq), (nq, nh))):
                step = links if g else links.later
                step(eng.tensor_tensor(
                    q4[:, a:e, u:v, :], q4[:, a:e, u:v, :],
                    cosw[:, a:e, g, :].unsqueeze(2).broadcast_to([P, e - a, v - u, D]), ALU.mult))
            links(eng.tensor_tensor(QK[:, a:e, :], QK[:, a:e, :], RT[:, a:e, :], ALU.add))

        def normalise(eng, links, a, e):
            links(eng.tensor_tensor(q4[:, a:e], q4[:, a:e],
                                    R[:, a:e, :].unsqueeze(3).broadcast_to([P, e - a, nh, D]), ALU.mult))

        with nc.Block() as block:
            @block.vector
            def _(dve):
                link_ = Links(dve, link)
                link_(nc.vector.tensor_reduce(R[:, :, :], SQ[:, :, :].rearrange("p t (h d) -> p t h d", d=D),
                                              AX.X, ALU.add))
                nc.vector.tensor_scalar(R[:, :, :], R[:, :, :], 1.0 / D, 1e-6 if eps_in else 0.0,
                                        ALU.mult, ALU.add).then_inc(ss_done, 1)
                rotate(nc.vector, link_, 0, NT - PT)
                dve.wait_ge(root_done, 1)
                if not eps_in:
                    link_(nc.vector.tensor_scalar(R[:, :, :], R[:, :, :], 1e-6, None, ALU.add))
                nc.vector.reciprocal(R[:, :, :], R[:, :, :]).then_inc(scaled, 1)
                dve.wait_ge(scaled, 1)
                normalise(nc.vector, link_, 0, NT - PT)
                if sums is not None:
                    dve.wait_ge(vmade, 1)
                    nc.vector.tensor_copy(SVT[:, :, :], ps[:, :, :]).then_inc(vtaken, 1)

            @block.scalar
            def _(act):
                act.wait_ge(ss_done, 1)
                nc.scalar.activation(R[:, :, :], R[:, :, :], ACT.Sqrt).then_inc(root_done, 1)

            @block.gpsimd
            def _(pool):
                links = Links(pool, p_link)
                if sums is not None:
                    v = lambda t: V[:, t, :].rearrange("p (h d) -> p h d", h=4)
                    links(nc.gpsimd.memset(SV[:, NT - 1, :, :], 0.0))
                    for qb in range(NT - 1):
                        links(nc.gpsimd.memset(SV[:, qb, :, 16:32], float(NT - 1 - qb)))
                    links(nc.gpsimd.tensor_copy(SV[:, NT - 2, :, 0:16], v(NT - 1)))
                    for qb in range(NT - 3, -1, -1):
                        links(nc.gpsimd.tensor_tensor(SV[:, qb, :, 0:16], SV[:, qb + 1, :, 0:16], v(qb + 1), ALU.add))
                    pool.sem_inc(vready, 1)
                rotate(nc.gpsimd, links, NT - PT, NT)
                pool.wait_ge(scaled, 1)
                normalise(nc.gpsimd, links, NT - PT, NT)

            if sums is not None:
                @block.tensor
                def _(pe):
                    pe.wait_ge(vready, 1)
                    places = tile_places(4)
                    for qb in range(NT):
                        sl, gr = places[qb]
                        for h in range(4):
                            last = nc.tensor.matmul(ps[gr * 32:(gr + 1) * 32, h, sl:sl + 1], SV[:, qb, h, :],
                                                    e50[:, :], start=True, stop=True, skip_group_check=True)
                    last.then_inc(vmade, 1)


def attention(nc, core, name, QK, V, Y, consts, *, D, NH, q0, k0, kv_of, kper, cap, scale, SV, U):
    NSUB = TERMS * D // 96
    ROWS = 96
    CAPB = 12 if cap else 8
    SB = CAPB // 4
    GW = 32 if D < 32 else 64
    NG = P // GW
    NSL = NT // NG
    place = tile_places(NG)
    SEG = segments(CAPB, NG, place)
    NS = len(SEG)
    kx = not cap
    AHEAD = 1 if cap else 3
    chunks = [(qb, a, min(a + 4, qb + 1)) for qb in range(NT) for a in range(0, qb + 1, 4)]
    NC = len(chunks)
    PERG = (2 if kper else 1) * NSUB
    TB0 = 0 if kper else NSUB
    S = lambda n: core.sem(f"{name}_{n}")
    q_stacked, k_stacked, pool_link = S("q_stacked"), S("k_stacked"), S("pool")
    turned, untangled = S("turned"), S("untangled")
    s_ready, tanh_done, exp_done, pv_done = S("s_ready"), S("tanh"), S("exp"), S("pv")
    y_ready, y_done = S("y_ready"), S("y_done")
    mx_ready, mx_taken, m_split, m_turned, m_placed, vlink = (
        S("mx_ready"), S("mx_taken"), S("m_split"), S("m_turned"), S("m_placed"), S("v"))
    ones_set, v_set, k_cast, cast, cast_held = S("ones"), S("v_set"), S("k_cast"), S("cast"), S("cast_held")
    o_taken, o_turned, held = S("o_taken"), S("o_turned"), S("pool_held")
    ident, identf, negq, negk = consts
    with ExitStack() as c:
        def sb(n, shape, dt):
            return c.enter_context(nc.sbuf_tensor(f"{name}_{n}", shape, dt))

        def pb(n, shape, dt):
            return c.enter_context(nc.psum_tensor(f"{name}_{n}", shape, dt))

        Qs = sb("Qs", [P, 2, NT, NSUB * ROWS], BF16)
        nks = 2 if kper else 1
        Ks = sb("Ks", [P, nks, NT, NSUB * ROWS], BF16)
        RQ = sb("RQ", [P, NT, D], F32)
        QT = sb("QT", [P, 4, NSUB, T], BF16)
        KT = sb("KT", [P, 4 if kper else 1, NSUB, T], BF16)
        Vh = sb("Vh", [P, 4, NT, GW], F32) if kper else sb("Vh", [P, 1, NT, GW], F32)
        OT = sb("OT", [P, NSL * P], F32)
        NPB = 3 if cap else 4 if kper else 2
        Pb = [sb(f"P{i}", [P, CAPB * P], F32) for i in range(NPB)]
        Tb = [sb(f"T{i}", [P, CAPB * P], F32) for i in range(2)] if cap else None
        RC = sb("RC", [P, NSL, NG], F32)
        if kx:
            MX = sb("MX", [P, NT, 2], F32)
            M1 = sb("M1", [P, NT], F32)
            M2 = sb("M2", [P, NT], F32)
            MS = sb("MS", [P, NT, 3], BF16)
            S1 = [pb(f"S1{i}", [P, 512], F32) for i in range(2)]
        Sp = [pb(f"S{i}", [P, SB * 512], F32) for i in range(2)]
        TP = pb("TP", [P, T], BF16)
        O = pb("O", [P, NSL * P], F32)
        TO = TP[:, :].bitcast(F32)[:, 0:NSL * P]
        tov = TO.rearrange("p (s g w) -> p s g w", s=NSL, g=NG)
        qst = Qs[:, :, :, :].rearrange("p b t (j d) -> p b t j d", d=D)
        kst = Ks[:, :, :, :].rearrange("p b t (j d) -> p b t j d", d=D)

        def qsrc(i, u):
            return QK[:, :, bass.ds(q0 + (i * U + u) * D, D)]

        def ksrc(i, u):
            return QK[:, :, bass.ds(k0 + kv_of(i, u) * D, D)]

        def cast_k(copy, i, u, b):
            copy(kst[:, b, :, 0:2, :], ksrc(i, u).unsqueeze(2).broadcast_to([P, NT, 2, D]))
            return copy(kst[:, b, :, 3, :], ksrc(i, u))

        def cast_head(eng, copy, i, u, n):
            if late(n, 2):
                eng.wait_ge(turned, tuses(i, u) - PERG)
                eng.sem_inc(cast_held, 1)
            b = u % 2
            copy(qst[:, b, :, 0:3:2, :], qsrc(i, u).unsqueeze(2).broadcast_to([P, NT, 2, D]))
            last = copy(qst[:, b, :, 5, :], qsrc(i, u))
            if kper:
                last = cast_k(copy, i, u, b)
            last.then_inc(cast, 1)

        def tuses(i, u):
            return i * (U * PERG) + u * PERG + TB0

        def at(i, u, d):
            return i + (u + d) // U, (u + d) % U

        def run(eng, head):
            for u in range(U):
                head(0, u, u)
            if NH // U > 2:
                with eng.Fori(1, NH // U - 1) as i:
                    for u in range(U):
                        head(i, u, None)
            for u in range(U):
                head(NH // U - 1, u, NH - U + u)

        def late(n, k):
            return n is None or n >= k

        def more(n, k):
            return n is None or n + k < NH

        with nc.Block() as block:
            @block.gpsimd
            def _(pool):
                def split_q(i, u, links):
                    st, two = qst[:, u % 2], [P, NT, 2, D]
                    links(nc.gpsimd.tensor_tensor(RQ[:, :, :], qsrc(i, u), st[:, :, 0, :], ALU.subtract))
                    links(nc.gpsimd.tensor_copy(st[:, :, 1:5:3, :], RQ[:, :, :].unsqueeze(2).broadcast_to(two)))
                    links(nc.gpsimd.tensor_tensor(st[:, :, 3, :], RQ[:, :, :], st[:, :, 1, :], ALU.subtract))

                def split_k(i, u, links, b):
                    st, two = kst[:, b], [P, NT, 2, D]
                    links(nc.gpsimd.tensor_tensor(RQ[:, :, :], ksrc(i, u), st[:, :, 0, :], ALU.subtract))
                    links(nc.gpsimd.tensor_copy(st[:, :, 2:5:2, :], RQ[:, :, :].unsqueeze(2).broadcast_to(two)))
                    links(nc.gpsimd.tensor_tensor(st[:, :, 5, :], RQ[:, :, :], st[:, :, 2, :], ALU.subtract))

                links = Links(pool, pool_link)
                links(nc.gpsimd.memset(Vh[:, :, :, :], 1.0))
                if not kper:
                    links(nc.gpsimd.tensor_copy(Vh[:, 0, :, 0:D], V[:, :, :]))
                    pool.sem_inc(v_set, 1)
                    pool.wait_ge(k_cast, 1)
                    split_k(0, 0, links, 0)
                    pool.sem_inc(k_stacked, 1)

                def head(i, u, n):
                    links = Links(pool, pool_link, clear=True)
                    pool.wait_ge(cast, i * U + u + 1)
                    pool.sem_inc(held, 1)
                    if kper:
                        split_k(i, u, links, u % 2)
                    split_q(i, u, links)
                    pool.sem_inc(q_stacked, 1)
                    if kper:
                        if late(n, 4):
                            pool.wait_ge(pv_done, (i * U + u - 3) * NS)
                            pool.sem_inc(held, 1)
                        g = kv_of(i, u)
                        links(nc.gpsimd.tensor_copy(Vh[:, u, :, 0:D], V[:, :, bass.ds(g * D, D)]))
                        pool.sem_inc(v_set, 1)
                run(pool, head)

            @block.tensor
            def _(pe):
                def turn(stk, use, j):
                    if not (isinstance(use, int) and use < 1):
                        pe.wait_ge(untangled, use)
                    for t in range(NT):
                        last = nc.tensor.transpose(TP[0:ROWS, t * P:(t + 1) * P],
                                                   stk[:, t, j * ROWS:(j + 1) * ROWS], ident[:, :])
                    last.then_inc(turned, 1)

                def turn_part(i, u, x):
                    if x == 0:
                        pe.wait_ge(q_stacked, i * U + u + 1)
                    if kper:
                        turn((Ks, Qs)[x][:, u % 2], tuses(i, u) + x, 0)
                    else:
                        turn(Qs[:, u % 2], tuses(i, u) + x, x)

                def scores(i, u, s, between=lambda: None):
                    g = (i * U + u) * NS + s
                    if s == 0:
                        pe.wait_ge(untangled, tuses(i, u) + PERG)
                        if kx:
                            pe.wait_ge(m_placed, i * U + u + 1)
                    if not (isinstance(g, int) and g < 2):
                        pe.wait_ge(tanh_done if cap else exp_done, g - 1)
                    seg, a = SEG[s], 0
                    while a < len(seg):
                        kb, qb = seg[a]
                        w = 1
                        while a + w < len(seg) and (a + w) % 4 and seg[a + w] == (kb, qb + w):
                            w += 1
                        dst = Sp[(u * NS + s) % 2][:, a * P:(a + w) * P]
                        diag = qb == kb
                        first = True
                        for j in range(NSUB):
                            end = j == NSUB - 1
                            r = P if cap else ROWS + 3 if j == 0 else ROWS
                            last = nc.tensor.matmul(
                                dst, KT[0:r, u if kper else 0, j, kb * P:(kb + 1) * P],
                                QT[0:r, u, j, qb * P:(qb + w) * P], start=first, stop=end,
                                skip_group_check=True)
                            first = False
                        if diag:
                            last = nc.tensor.matmul(dst[:, 0:P], ident[:, :], negk[:, :], start=False,
                                                    stop=True, skip_group_check=True)
                        a += w
                        if a == len(seg):
                            last.then_inc(s_ready, 1)
                        if a % 4 == 0:
                            between()

                def maxima(i, u, cs):
                    for ci in cs:
                        qb, a, e = chunks[ci]
                        n = (i * U + u) * NC + ci
                        if ci == 0:
                            pe.wait_ge(untangled, tuses(i, u) + PERG)
                        if not (isinstance(n, int) and n < 2):
                            pe.wait_ge(mx_taken, n - 1)
                        dst = S1[(u * NC + ci) % 2][:, 0:(e - a) * P]
                        last = nc.tensor.matmul(dst, QT[0:ROWS, u, 0, qb * P:(qb + 1) * P],
                                                KT[0:ROWS, u if kper else 0, 0, a * P:e * P],
                                                start=True, stop=(e <= qb), skip_group_check=True)
                        if e == qb + 1:
                            last = nc.tensor.matmul(dst[:, (e - a - 1) * P:(e - a) * P], ident[:, :], negq[:, :],
                                                    start=False, stop=True, skip_group_check=True)
                        last.then_inc(mx_ready, 1)

                def turn_maxima(i, u):
                    pe.wait_ge(m_split, i * U + u + 1)
                    if not (isinstance(i, int) and i * U + u < 1):
                        pe.wait_ge(m_placed, i * U + u)
                    for qb in range(NT):
                        last = nc.tensor.transpose(TP[ROWS:ROWS + 3, qb * P:(qb + 1) * P], MS[:, qb, :],
                                                   ident[:, :], tile_position=(0, ROWS))
                    last.then_inc(m_turned, 1)

                def weigh(i, u, s):
                    g = (i * U + u) * NS + s
                    n = i * U + u
                    pe.wait_ge(exp_done, g + 1)
                    vv = Vh[:, u if kper else 0]
                    todo = []
                    if s == 0:
                        pe.wait_ge(v_set, n + 1 if kper else 1)
                        if not (isinstance(n, int) and n < 1):
                            pe.wait_ge(o_taken, n)
                    todo += [(qb, vv[:, kb, :], Pb[(u * NS + s) % NPB][:, x * P:(x + 1) * P])
                             for x, (kb, qb) in enumerate(SEG[s])]
                    byg = [[m for m in todo if place[m[0]][1] == gr] for gr in range(NG)]
                    rounds = max(len(x) for x in byg)
                    for r in range(rounds):
                        for gr in range(NG):
                            if r < len(byg[gr]):
                                qb, v, p = byg[gr][r]
                                sl = place[qb][0]
                                last = nc.tensor.matmul(O[gr * GW:(gr + 1) * GW, sl * P:(sl + 1) * P], v, p,
                                                        start=(s == 0 and r == 0), stop=True,
                                                        skip_group_check=True)
                    last.then_inc(pv_done, 1)

                def turn_out(i, u):
                    n = i * U + u
                    pe.wait_ge(o_taken, n + 1)
                    for sl in range(NSL):
                        last = nc.tensor.transpose(TO[:, sl * P:(sl + 1) * P], OT[:, sl * P:(sl + 1) * P],
                                                   identf[:, :])
                    last.then_inc(o_turned, 1)

                if not kper:
                    pe.wait_ge(k_stacked, 1)
                    for j in range(NSUB):
                        turn(Ks[:, 0], j, j)
                for u in range(AHEAD):
                    turn_part(0, u, 0)
                    turn_part(0, u, 1)
                    if kx and u == 1:
                        turn_maxima(0, 0)
                    if kx and u < 2:
                        maxima(0, u, range(NC))
                pe.wait_ge(ones_set, 2 if cap else KT.shape[1])

                def head(i, u, n):
                    before = (i, u - 1) if u else (i - 1, U - 1)
                    chunk = iter(range(NC))

                    def one_chunk():
                        c = next(chunk, None)
                        if kx and more(n, 2) and c is not None:
                            maxima(*at(i, u, 2), [c])

                    for s in range(NS):
                        if s == 0 and late(n, 2):
                            pe.wait_ge(y_done, i * U + u - 1)
                        scores(i, u, s, one_chunk)
                        if kx and s == 2 and more(n, AHEAD):
                            turn_part(*at(i, u, AHEAD), 1)
                        if s == 1:
                            if kx and more(n, 1):
                                turn_maxima(*at(i, u, 1))
                            if more(n, AHEAD):
                                turn_part(*at(i, u, AHEAD), 0)
                        if s == min(3, NS - 1) and late(n, 1):
                            if more(n, AHEAD):
                                pe.wait_ge(untangled, tuses(*at(i, u, AHEAD)) + PERG)
                            if kx and more(n, 1):
                                pe.wait_ge(m_placed, i * U + u + 2)
                            turn_out(*before)
                        if s >= 2:
                            weigh(i, u, s - 2)
                        elif late(n, 1):
                            weigh(*before, NS - 2 + s)
                        one_chunk()
                        if cap and s == 1 and more(n, AHEAD):
                            turn_part(*at(i, u, AHEAD), 1)
                run(pe, head)
                weigh(NH // U - 1, U - 1, NS - 2)
                weigh(NH // U - 1, U - 1, NS - 1)
                turn_out(NH // U - 1, U - 1)

            @block.scalar
            def _(act):
                def squash(i, u, s):
                    g = (i * U + u) * NS + s
                    act.wait_ge(s_ready, g + 1)
                    if not (isinstance(g, int) and g < 2):
                        act.wait_ge(exp_done, g - 1)
                    w = len(SEG[s]) * P
                    b = (u * NS + s) % 2
                    nc.scalar.activation(Tb[b][:, 0:w], Sp[b][:, 0:w], ACT.Tanh,
                                         scale=scale / 50.0).then_inc(tanh_done, 1)

                def expo(i, u, s):
                    g = (i * U + u) * NS + s
                    act.wait_ge(tanh_done if cap else s_ready, g + 1)
                    if not (isinstance(g, int) and g < NPB):
                        act.wait_ge(pv_done, g - NPB + 1)
                    w = len(SEG[s]) * P
                    b = (u * NS + s) % 2
                    src = Tb[b] if cap else Sp[b]
                    nc.scalar.activation(Pb[(u * NS + s) % NPB][:, 0:w], src[:, 0:w], ACT.Exp,
                                         scale=50.0 if cap else scale).then_inc(exp_done, 1)

                def place_maxima(i, u):
                    act.wait_ge(m_turned, i * U + u + 1)
                    nc.scalar.activation(QT[ROWS:ROWS + 3, u, 0, :], TP[ROWS:ROWS + 3, :],
                                         ACT.Copy).then_inc(m_placed, 1)
                copy = lambda o, x: nc.scalar.activation(o, x, ACT.Copy)
                if not cap:
                    if not kper:
                        cast_k(copy, 0, 0, 0).then_inc(k_cast, 1)
                    for u in range(AHEAD + 1):
                        cast_head(act, copy, 0, u, u)
                if kx:
                    place_maxima(0, 0)

                def head(i, u, n):
                    if not cap and more(n, AHEAD + 1):
                        cast_head(act, copy, *at(i, u, AHEAD + 1), None)
                    for s in range(NS):
                        if cap:
                            squash(i, u, s)
                            if s:
                                expo(i, u, s - 1)
                            elif late(n, 1):
                                ii, uu = (i, u - 1) if u else (i - 1, U - 1)
                                expo(ii, uu, NS - 1)
                        else:
                            expo(i, u, s)
                        if s == 1 and kx and more(n, 1):
                            place_maxima(*at(i, u, 1))
                run(act, head)
                if cap:
                    expo(NH // U - 1, U - 1, NS - 1)

            @block.vector
            def _(dve):
                links = Links(dve, vlink)
                if kx:
                    links(nc.vector.memset(MX[:, :, :], -3.0e38))

                def untangle(dst, use):
                    dve.wait_ge(turned, use + 1)
                    nc.vector.tensor_copy(dst[0:ROWS, :], TP[0:ROWS, :]).then_inc(untangled, 1)

                def untangle_part(i, u, x):
                    if kper:
                        untangle((KT, QT)[x][:, u, 0, :], tuses(i, u) + x)
                    else:
                        untangle(QT[:, u, x, :], tuses(i, u) + x)

                def maxima(i, u, cs):
                    for ci in cs:
                        qb, a, e = chunks[ci]
                        n = (i * U + u) * NC + ci
                        dve.wait_ge(mx_ready, n + 1)
                        nc.vector.tensor_reduce(MX[:, qb, (a // 4):(a // 4) + 1],
                                                S1[(u * NC + ci) % 2][:, 0:(e - a) * P], AX.X,
                                                ALU.max).then_inc(mx_taken, 1)

                def split_maxima(i, u):
                    n = i * U + u
                    links = Links(dve, vlink, clear=True)
                    dve.wait_ge(mx_taken, (n + 1) * NC)
                    links(nc.vector.tensor_reduce(M1[:, :], MX[:, :, :], AX.X, ALU.max))
                    if not (isinstance(n, int) and n < 1):
                        dve.wait_ge(m_turned, n)
                    links(nc.vector.tensor_scalar(MS[:, :, 0], M1[:, :], -1.0, None, ALU.mult))
                    links(nc.vector.scalar_tensor_tensor(M2[:, :], M1[:, :], -1.0, MS[:, :, 0],
                                                         ALU.mult, ALU.subtract))
                    links(nc.vector.tensor_copy(MS[:, :, 1], M2[:, :]))
                    links(nc.vector.tensor_tensor(MS[:, :, 2], M2[:, :], MS[:, :, 1], ALU.subtract))
                    dve.sem_inc(m_split, 1)

                def take_out(i, u):
                    n = i * U + u
                    dve.wait_ge(pv_done, (n + 1) * NS)
                    if not (isinstance(n, int) and n < 1):
                        dve.wait_ge(o_turned, n)
                    if cap:
                        nc.vector.tensor_tensor(
                            OT[:, :].rearrange("p (s q) -> p s q", q=P), O[:, :].rearrange("p (s q) -> p s q", q=P),
                            SV[:, bass.ds(kv_of(i, u), 1), :].rearrange("p a s -> p (a s)").unsqueeze(2)
                            .broadcast_to([P, NSL, P]), ALU.add).then_inc(o_taken, 1)
                    else:
                        nc.vector.tensor_copy(OT[:, :], O[:, :]).then_inc(o_taken, 1)

                def divide(i, u):
                    n = i * U + u
                    dve.wait_ge(o_turned, n + 1)
                    if not (isinstance(n, int) and n < 1):
                        dve.wait_ge(y_done, n)
                    nc.vector.reciprocal(RC[:, :, :], tov[:, :, :, D]).then_inc(y_ready, 1)
                    dve.wait_ge(y_ready, n + 1)
                    nc.vector.tensor_tensor(Y[:, :, bass.ds(n * D, D)].rearrange("p (s g) d -> p s g d", g=NG),
                                            tov[:, :, :, 0:D],
                                            RC[:, :, :].unsqueeze(3).broadcast_to([P, NSL, NG, D]),
                                            ALU.mult).then_inc(y_done, 1)
                copy = lambda o, x: nc.vector.tensor_copy(o, x)
                if cap:
                    cast_head(dve, copy, 0, 0, 0)
                    cast_head(dve, copy, 0, 1, 1)
                if not kper:
                    for j in range(NSUB):
                        untangle(KT[:, 0, j, :], j)
                if cap:
                    nc.vector.memset(QT[ROWS:P, :, :, :], 0.0).then_inc(ones_set, 1)
                    nc.vector.memset(KT[ROWS:P, :, :, :], 0.0).then_inc(ones_set, 1)
                for u in range(AHEAD):
                    untangle_part(0, u, 0)
                    untangle_part(0, u, 1)
                    if kx and u < 2:
                        maxima(0, u, range(NC))
                        split_maxima(0, u)
                    if kx and u < 2:
                        for x in range(u * KT.shape[1] // 2, (u + 1) * KT.shape[1] // 2):
                            nc.vector.memset(KT[ROWS:ROWS + 3, x, 0, :], 1.0).then_inc(ones_set, 1)

                def head(i, u, n):
                    before = (i, u - 1) if u else (i - 1, U - 1)
                    if kx and more(n, 2):
                        maxima(*at(i, u, 2), range(0, 5))
                    if more(n, AHEAD):
                        untangle_part(*at(i, u, AHEAD), 0)
                    if late(n, 1):
                        take_out(*before)
                    if kx and more(n, 2):
                        maxima(*at(i, u, 2), range(5, 8))
                    if more(n, AHEAD):
                        untangle_part(*at(i, u, AHEAD), 1)
                    if kx and more(n, 2):
                        maxima(*at(i, u, 2), range(8, 10))
                    if late(n, 1):
                        divide(*before)
                    if kx and more(n, 2):
                        maxima(*at(i, u, 2), range(10, NC))
                    if kx and more(n, 2):
                        split_maxima(*at(i, u, 2))
                    if cap and more(n, AHEAD + 1):
                        cast_head(dve, copy, *at(i, u, AHEAD + 1), None)
                run(dve, head)
                take_out(NH // U - 1, U - 1)
                divide(NH // U - 1, U - 1)


def segments(cap, NG, place):
    lists = [[(kb, qb) for kb in range(NT) for qb in range(kb, NT) if place[qb][1] == g] for g in range(NG)]
    per = cap // NG
    return [sorted(b for x in lists for b in x[a:a + per]) for a in range(0, len(lists[0]), per)]


def tile_places(NG):
    if NG == 4:
        order = [0, 1, 2, 3, 7, 6, 5, 4]
    else:
        order = [0, 1, 3, 2, 4, 5, 7, 6]
    return {t: (x // NG, x % NG) for x, t in enumerate(order)}


def close_layer(nc, core, name, X, XT, identf, eps, product, gates=None, out=None, weights=(), sent=None,
                light=False, turning=None, front=None, arrives=None, loads=(), first_cut=0):
    gates = gates or [None]
    NP = len(gates)
    LAG = 2
    S = lambda n: core.sem(f"{name}_{n}")
    made, added, link, var_done, root, scaled, normed, turned, high_taken, taken, stored = (
        S("made"), S("added"), S("v"), S("var"), S("root"), S("scaled"), S("normed"), S("turned"),
        S("high_taken"), S("taken"), S("stored"))
    with ExitStack() as c:
        NB = 3 if turning else 4
        bank = lambda n: c.enter_context(nc.psum_tensor(f"{name}_{n}", [P, CH], F32))
        full = [[bank(f"{n}{i}") for i in range(NB)] for n in ("ps", "tp")]
        ps, tp = ([b[:, 0:C] for b in banks] for banks in full)
        if front:
            front.place(c, *full)
        if turning:
            Y, YT, NG = turning
            at = {t: s * NG + g for t, (s, g) in tile_places(NG).items()}
            y_turned, y_taken = S("y_turned"), S("y_taken")
            yp = [c.enter_context(nc.psum_tensor(f"{name}_yp{i}", [P, C], F32)) for i in range(2)]
        ST = c.enter_context(nc.sbuf_tensor(name + "_st", [P, NT, 6], F32))
        MV = c.enter_context(nc.sbuf_tensor(name + "_mv", [P, NT, 2], F32))
        RS = c.enter_context(nc.sbuf_tensor(name + "_rs", [P, NT], F32))
        NM = c.enter_context(nc.sbuf_tensor(name + "_nm", [P, NT], F32))
        turned_tile = lambda t: tp[t % NB][:, :].rearrange("p (k n) -> p k n", k=KC)
        place = lambda i, t: XT[i][:, :, t * P:(t + 1) * P]
        summed = lambda t: ps[t % NB][:, :] if light else X[:, t, :]
        with nc.Block() as block:
            @block.tensor
            def _(pe):
                def turn(t):
                    pe.wait_ge(normed, t + 1)
                    if front and t < NB:
                        front.wait_bank(pe, t)
                    if t >= NB:
                        pe.wait_ge(taken, t - NB + 1)
                    for k in range(KC):
                        last = nc.tensor.transpose(tp[t % NB][:, k * P:(k + 1) * P], X[:, t, k * P:(k + 1) * P],
                                                   identf[:, :])
                    last.then_inc(turned, 1)

                def turn_y(t):
                    if t >= 2:
                        pe.wait_ge(y_taken, t - 1)
                    for k in range(KC):
                        last = nc.tensor.transpose(yp[t % 2][:, k * P:(k + 1) * P], Y[:, at[t], k * P:(k + 1) * P],
                                                   identf[:, :])
                    last.then_inc(y_turned, 1)

                n = 0
                if arrives:
                    pe.wait_ge(*arrives)
                if front:
                    front.tensor(pe)
                if turning:
                    turn_y(0)
                    turn_y(1)
                for t in range(NT):
                    if turning:
                        pe.wait_ge(y_taken, t + 1)
                    if front:
                        front.wait_tile(pe, t)
                        if t < NB:
                            front.wait_bank(pe, t)
                    for j in range(NP):
                        if n >= NB:
                            pe.wait_ge(normed if light else added, n - NB + 1)
                        mms = ([(identf[:, :], X[:, t, :], (0, C))] if light else []) + list(product(t, j))
                        for m, (lhsT, rhs, cols) in enumerate(mms):
                            if front and t == 0:
                                front.wait_weights(pe, m)
                            last = nc.tensor.matmul(ps[n % NB][:, cols[0]:cols[1]], lhsT, rhs, start=(m == 0),
                                                    stop=(m == len(mms) - 1), skip_group_check=True)
                        last.then_inc(made, 1)
                        n += 1
                    if turning and t + 2 < NT:
                        turn_y(t + 2)
                    if out is None and t >= LAG:
                        turn(t - LAG)
                if out is None:
                    for t in range(NT - LAG, NT):
                        turn(t)

            @block.vector
            def _(dve):
                links = Links(dve, link)
                if front:
                    front.vector(dve)

                def scales(t):
                    dve.wait_ge(root, t + 1)
                    links(nc.vector.reciprocal(RS[:, t:t + 1], RS[:, t:t + 1]))
                    nc.vector.scalar_tensor_tensor(NM[:, t:t + 1], MV[:, t, 0:1], -1.0, RS[:, t:t + 1], ALU.mult,
                                                   ALU.mult).then_inc(scaled, 1)

                def take(t):
                    dve.wait_ge(high_taken, t + 1)
                    low_part(nc, place(1, t), turned_tile(t), place(0, t)).then_inc(taken, 1)

                n = 0
                for t in range(NT):
                    for j in range(NP):
                        dve.wait_ge(made, n + 1)
                        if n and j:
                            dve.wait_ge(added, n)
                        src = ps[n % NB][:, :]
                        if light:
                            pass
                        elif gates[j] is None:
                            nc.vector.tensor_tensor(X[:, t, :], X[:, t, :], src, ALU.add).then_inc(added, 1)
                        else:
                            nc.vector.scalar_tensor_tensor(X[:, t, :], src, gates[j](t), X[:, t, :],
                                                           ALU.mult, ALU.add).then_inc(added, 1)
                        n += 1
                    if not light:
                        dve.wait_ge(added, n)
                    links(nc.vector.bn_stats(ST[:, t, :], summed(t)))
                    nc.vector.bn_aggr(MV[:, t, :], ST[:, t, :]).then_inc(var_done, 1)
                    if t:
                        scales(t - 1)
                    if out is None and t >= LAG + 2:
                        take(t - LAG - 2)
                    if first_cut <= t < first_cut + len(weights):
                        if t == first_cut:
                            dve.wait_ge(*sent)
                        cut_in_two(nc, links, *weights[t - first_cut])
                scales(NT - 1)
                if out is None:
                    for t in range(NT - LAG - 2, NT):
                        take(t)

            @block.scalar
            def _(act):
                def normalise(t):
                    act.wait_ge(scaled, t + 1)
                    nc.scalar.activation(X[:, t, :], summed(t), ACT.Identity, bias=NM[:, t:t + 1],
                                         scale=RS[:, t:t + 1]).then_inc(normed, 1)

                def take(t):
                    act.wait_ge(turned, t + 1)
                    nc.scalar.activation(place(0, t), turned_tile(t), ACT.Copy).then_inc(high_taken, 1)

                def take_y(t):
                    act.wait_ge(y_turned, t + 1)
                    nc.scalar.activation(YT[:, :, t * P:(t + 1) * P],
                                         yp[t % 2][:, :].rearrange("p (k n) -> p k n", k=KC),
                                         ACT.Copy).then_inc(y_taken, 1)

                if front:
                    front.scalar(act)
                if turning:
                    take_y(0)
                    take_y(1)
                for t in range(NT):
                    if turning and t + 2 < NT:
                        take_y(t + 2)
                    act.wait_ge(var_done, t + 1)
                    nc.scalar.activation(RS[:, t:t + 1], MV[:, t, 1:2], ACT.Sqrt, bias=eps[:, :]).then_inc(root, 1)
                    if out is None and t >= LAG + 1:
                        take(t - LAG - 1)
                    if t:
                        normalise(t - 1)
                normalise(NT - 1)
                if out is None:
                    for t in range(NT - LAG - 1, NT):
                        take(t)

            if front:
                @block.gpsimd
                def _(pool):
                    front.gpsimd(pool)

            if out is not None:
                @block.sync
                def _(sp):
                    start_loads(sp, loads)
                    sp.wait_ge(normed, NT)
                    sp.dma_start(out, X[:, :, :]).then_inc(stored, 16)
                    sp.wait_ge(stored, 16)


class Hidden:

    def __init__(self, nc, core, name, XT, H, weights, bias=None, late=()):
        self.nc, self.name, self.XT, self.H, self.weights, self.bias, self.late = (
            nc, name, XT, H, weights, bias, late)
        self.order = [(h, f) for h in range(NCH) for f in range(NF)]
        S = lambda n: core.sem(f"{name}_{n}")
        self.made, self.activated, self.read, self.high_done, self.split, self.cut, self.link = (
            S("made"), S("activated"), S("read"), S("high"), S("split"), S("cut"), S("v"))

    def place(self, c, first, second):
        self.first, self.second = first, second
        self.G = [c.enter_context(self.nc.sbuf_tensor(f"{self.name}_g{i}", [P, CH], F32)) for i in range(2)]

    def parts(self, n):
        h, f = self.order[n]
        return [x[:, f, h * CH:(h + 1) * CH] for x in self.H]

    def wait_tile(self, pe, t):
        if t % (NT // NCH) == 0:
            pe.wait_ge(self.split, (1 + t * NCH // NT) * NF)

    def wait_bank(self, pe, t):
        pe.wait_ge(self.read, len(self.order) - 4 + t + 1)

    def wait_weights(self, pe, m):
        if self.late and m % 6 == 0:
            pe.wait_ge(self.cut, m // 6 + 1)

    def tensor(self, pe):
        for n, (h, f) in enumerate(self.order):
            if n >= 4:
                pe.wait_ge(self.read, n - 3)
            x = [x[:, :, h * CH:(h + 1) * CH] for x in self.XT]
            for side, bank in enumerate((self.first, self.second)[:1 if self.bias is not None else 2]):
                mms = []
                for k in range(KC):
                    w = self.weights(f, side, k)
                    if len(w) == 1:
                        mms += [(w[0], x[0][:, k, :]), (w[0], x[1][:, k, :])]
                    else:
                        mms += pairs(w, [v[:, k, :] for v in x])
                for i, (w, v) in enumerate(mms):
                    last = self.nc.tensor.matmul(bank[n % 4][:, :], w, v, start=(i == 0), stop=(i == len(mms) - 1))
            last.then_inc(self.made, 1)

    def scalar(self, act):
        for n, (h, f) in enumerate(self.order):
            act.wait_ge(self.made, n + 1)
            if n >= 2:
                act.wait_ge(self.split, n - 1)
            src, g = self.first[n % 4][:, :], self.G[n % 2][:, :]
            if self.bias is not None:
                self.nc.scalar.activation(g, src, ACT.Gelu, bias=self.bias[:, f:f + 1]).then_inc(self.read, 1)
            else:
                self.nc.scalar.activation(g, src, ACT.Silu).then_inc(self.activated, 1)

    def vector(self, dve):
        links = Links(dve, self.link)
        for n in range(len(self.order)):
            g = self.G[n % 2][:, :]
            if self.bias is None:
                dve.wait_ge(self.activated, n + 1)
                self.nc.vector.tensor_tensor(g, g, self.second[n % 4][:, :], ALU.mult).then_inc(self.read, 1)
            dve.wait_ge(self.read, n + 1)
            high, low = self.parts(n)
            if self.bias is None:
                high_part(self.nc, high, g).then_inc(self.high_done, 1)
            else:
                links(high_part(self.nc, high, g))
                low_part(self.nc, low, g, high).then_inc(self.split, 1)
        if self.late:
            dve.wait_ge(self.made, len(self.order))
        for high, low, raw in self.late:
            links(high_part(self.nc, high, raw))
            low_part(self.nc, low, raw, high).then_inc(self.cut, 1)

    def gpsimd(self, pool):
        if self.bias is not None:
            return
        for n in range(len(self.order)):
            pool.wait_ge(self.high_done, n + 1)
            high, low = self.parts(n)
            self.nc.gpsimd.tensor_tensor(low, self.G[n % 2][:, :], f32(high), ALU.subtract).then_inc(self.split, 1)


def scan_mixer(nc, core, name, loads, XTP, XT, W1X, W1IN, CW, CB, NA, XC, HM):
    S = lambda n: core.sem(f"{name}_{n}")
    w_cut, joined, conv, made, spd, da, vl, al = (
        S("w_cut"), S("joined"), S("conv"), S("made"), S("softplus"), S("decay"), S("v"), S("a"))
    with ExitStack() as c:
        ps = [c.enter_context(nc.psum_tensor(f"{name}_ps{i}", [SS, CH], F32)) for i in range(8)]

        def sb(n):
            return c.enter_context(nc.sbuf_tensor(f"{name}_{n}", [SS, CH], F32))

        AB, EX, DL, DA, BU = ([sb(f"{n}{h}") for h in range(NCH)] for n in ("ab", "ex", "dl", "da", "bu"))
        HS = [sb(f"hs{h}") for h in range(NCH)]
        WX = [c.enter_context(nc.sbuf_tensor(f"{name}_wx{n}", [P, KC, 3 * SS], FR)) for n in "hl"]
        with nc.Block() as block:
            @block.sync
            def _(sp):
                start_loads(sp, loads)

            @block.tensor
            def _(pe):
                pe.wait_ge(w_cut, 2)
                for h in range(NCH):
                    for w in range(3):
                        mms = [p for k in range(KC) for p in pairs([x[:, k, w * SS:(w + 1) * SS] for x in WX],
                                                                   [x[:, k, h * CH:(h + 1) * CH] for x in XTP])]
                        for i, (v, x) in enumerate(mms):
                            last = nc.tensor.matmul(ps[4 * h + w][:, :], v, x, start=(i == 0),
                                                    stop=(i == len(mms) - 1))
                    last.then_inc(made, 1)
                pe.wait_ge(conv, KC)
                for h in range(NCH):
                    for k in range(KC):
                        last = nc.tensor.matmul(ps[4 * h + 3][:, :], W1IN[:, k, :], XC[:, k, h * CH:(h + 1) * CH],
                                                start=(k == 0), stop=(k == KC - 1))
                    last.then_inc(made, 1)

            @block.vector
            def _(dve):
                links = Links(dve, vl)
                high_part(nc, WX[0][:, :, :], W1X[:, :, :]).then_inc(w_cut, 1)
                dve.wait_ge(w_cut, 1)
                low_part(nc, WX[1][:, :, :], W1X[:, :, :], WX[0][:, :, :]).then_inc(w_cut, 1)
                links(nc.vector.tensor_tensor(XT[:, 0, :], f32(XTP[0][:, 0, :]), f32(XTP[1][:, 0, :]), ALU.add))
                for k in range(KC):
                    if k:
                        dve.wait_ge(joined, 1)
                    links(nc.vector.tensor_scalar(XC[:, k, :], XT[:, k, :], CW[:, k, 3:4], CB[:, k:k + 1],
                                                  ALU.mult, ALU.add))
                    for j in range(1, 4):
                        ins = nc.vector.scalar_tensor_tensor(
                            XC[:, k, j:T], XT[:, k, 0:T - j], CW[:, k, 3 - j:4 - j], XC[:, k, j:T],
                            ALU.mult, ALU.add)
                        if j < 3:
                            links(ins)
                    ins.then_inc(conv, 1)
                for h in range(NCH):
                    dve.wait_ge(al, 3 * h + 3)
                    nc.vector.scalar_tensor_tensor(DL[h][:, :], ps[4 * h][:, :], 0.0, EX[h][:, :], ALU.max,
                                                   ALU.add).then_inc(spd, 1)
                dve.wait_ge(made, 4)
                for h in range(NCH):
                    dve.wait_ge(spd, h + 1)
                    links(nc.vector.tensor_tensor(BU[h][:, :], DL[h][:, :], ps[4 * h + 1][:, :], ALU.mult))
                    links(nc.vector.tensor_tensor(BU[h][:, :], BU[h][:, :], ps[4 * h + 3][:, :], ALU.mult))
                    dve.wait_ge(da, h + 1)
                    init = 0.0 if h == 0 else HS[h - 1][:, CH - 1:CH]
                    links(nc.vector.tensor_tensor_scan(HS[h][:, :], DA[h][:, :], BU[h][:, :], init,
                                                       ALU.mult, ALU.add))
                    links(nc.vector.tensor_tensor(HM[:, h * CH:(h + 1) * CH], HS[h][:, :], ps[4 * h + 2][:, :],
                                                  ALU.mult))

            @block.gpsimd
            def _(pool):
                nc.gpsimd.tensor_tensor(XT[:, 1, :], f32(XTP[0][:, 1, :]), f32(XTP[1][:, 1, :]),
                                        ALU.add).then_inc(joined, 1)

            @block.scalar
            def _(act):
                links = Links(act, al)
                for h in range(NCH):
                    act.wait_ge(made, h + 1)
                    links(nc.scalar.activation(AB[h][:, :], ps[4 * h][:, :], ACT.Abs))
                    links(nc.scalar.activation(EX[h][:, :], AB[h][:, :], ACT.Exp, scale=-1.0))
                    links(nc.scalar.activation(EX[h][:, :], EX[h][:, :], ACT.Ln, bias=1.0))
                for h in range(NCH):
                    act.wait_ge(spd, h + 1)
                    nc.scalar.activation(DA[h][:, :], DL[h][:, :], ACT.Exp, scale=NA[0:SS, 0:1]).then_inc(da, 1)


def retention(nc, core, name, loads, XT, W, WB, DT, dt_sent, CS, KVS, GC, BM, BV, X2T):
    S = lambda n: core.sem(f"{name}_{n}")
    made, moved = S("made"), S("moved")
    vmade, vmoved = S("vmade"), S("vmoved")
    qs_done, ks_done = S("qs"), S("ks")
    zeroed, spread, smade = S("zeroed"), S("spread"), S("state_part")
    sc, dec, outp, outd, st, stz, link = (S("scores"), S("decayed"), S("out"), S("out_taken"), S("state_updated"),
                                          S("state_zeroed"), S("v"))
    with ExitStack() as c:
        def sb(n, shape):
            return c.enter_context(nc.sbuf_tensor(f"{name}_{n}", shape, F32))

        Q, K, QS = sb("q", [P, KC, T]), sb("k", [P, KC, T]), sb("qs", [P, KC, T])
        QD = sb("qd", [P, KC, NT, 4, P])
        KV = sb("kv", [P, NT, 2 * C])
        AT = [sb(f"at{i}", [P, 4, P]) for i in range(2)]
        SD = sb("sd", [P, KC, P])
        TM = sb("tm", [P, KC, P])
        ps = [c.enter_context(nc.psum_tensor(f"{name}_ps{i}", [P, 512], F32)) for i in range(4)]
        PO = [c.enter_context(nc.psum_tensor(f"{name}_po{i}", [P, C], F32)) for i in range(2)]
        PS = [c.enter_context(nc.psum_tensor(f"{name}_pst{i}", [P, P], F32)) for i in range(2)]
        with nc.Block() as block:
            @block.sync
            def _(sp):
                start_loads(sp, loads)

            @block.tensor
            def _(pe):
                n = 0
                for w in range(2):
                    for m in range(KC):
                        for h in range(NCH):
                            if n >= 4:
                                pe.wait_ge(moved, n - 3)
                            a = w * C + m * P
                            mms = [p for k in range(KC) for p in pairs([v[:, k, a:a + P] for v in W],
                                                                       [x[:, k, h * CH:(h + 1) * CH] for x in XT])]
                            for i, (v, x) in enumerate(mms):
                                last = nc.tensor.matmul(ps[n % 4][:, :], v, x, start=(i == 0),
                                                        stop=(i == len(mms) - 1))
                            last.then_inc(made, 1)
                            n += 1
                for t in range(NT):
                    if t >= 4:
                        pe.wait_ge(vmoved, t - 3)
                    else:
                        pe.wait_ge(moved, 8 - 3 + t)
                    mms = [p for k in range(KC) for p in pairs([x[:, k, t * P:(t + 1) * P] for x in XT],
                                                               [v[:, k, C:3 * C] for v in W])]
                    for i, (x, v) in enumerate(mms):
                        last = nc.tensor.matmul(ps[t % 4][:, :], x, v, start=(i == 0), stop=(i == len(mms) - 1))
                    last.then_inc(vmade, 1)

            @block.scalar
            def _(act):
                n = 0
                for w in range(2):
                    for m in range(KC):
                        for h in range(NCH):
                            act.wait_ge(made, n + 1)
                            nc.scalar.activation((Q, K)[w][:, m, h * CH:(h + 1) * CH], ps[n % 4][:, :],
                                                 ACT.Identity, bias=WB[:, w * KC + m:w * KC + m + 1]).then_inc(moved, 1)
                            n += 1
                act.wait_ge(zeroed, 1)
                act.wait_ge(moved, 4)
                for m in range(KC):
                    for i in range(4):
                        r = slice(32 * i, 32 * i + 32)
                        nc.scalar.activation(QD[r, m, :, i, :], Q[r, m, :].rearrange("p (t i) -> p t i", i=P),
                                             ACT.Copy).then_inc(spread, 1)

            @block.vector
            def _(dve):
                nc.vector.memset(SD[:, :, :], 0.0).then_inc(stz, 1)
                nc.vector.memset(QD[:, :, :, :, :], 0.0).then_inc(zeroed, 1)
                for t in range(NT):
                    dve.wait_ge(vmade, t + 1)
                    nc.vector.tensor_tensor(KV[:, t, :], ps[t % 4][:, :], BV, ALU.add).then_inc(vmoved, 1)
                    dve.wait_ge(vmoved, t + 1)
                    k = KV[:, t, 0:C].rearrange("p (h d) -> p h d", h=RH)
                    nc.vector.tensor_tensor(k, k, KVS.unsqueeze(2).broadcast_to([P, RH, RD]),
                                            ALU.mult).then_inc(ks_done, 1)

            @block.gpsimd
            def _(pool):
                pool.wait_ge(moved, 4)
                for m in range(KC):
                    nc.gpsimd.tensor_tensor(QS[:, m, :].rearrange("p (t i) -> p t i", i=P),
                                            Q[:, m, :].rearrange("p (t i) -> p t i", i=P),
                                            CS[:, m, :].unsqueeze(1).broadcast_to([P, NT, P]),
                                            ALU.mult).then_inc(qs_done, 1)
        steps = [(t, m) for t in range(NT) for m in range(KC)]
        with nc.Block() as block:
            @block.tensor
            def _(pe):
                def scores(n):
                    t, m = steps[n]
                    if n >= 2:
                        pe.wait_ge(dec, n - 1)
                    nc.tensor.matmul(ps[n % 2][:, :], K[:, m, t * P:(t + 1) * P],
                                     QD[:, m, t, :, :].rearrange("p h i -> p (h i)"), start=True,
                                     stop=True).then_inc(sc, 1)

                scores(0)
                scores(1)
                for n, (t, m) in enumerate(steps):
                    cols = slice(m * P, (m + 1) * P)
                    if t + 1 < NT:
                        if n >= 2:
                            pe.wait_ge(st, n - 1)
                        nc.tensor.matmul(PS[m][:, :], KV[:, t, cols], KV[:, t, C + m * P:C + (m + 1) * P],
                                         start=True, stop=True).then_inc(smade, 1)
                    if m == 0 and t >= 2:
                        pe.wait_ge(outd, t - 1)
                    if t:
                        pe.wait_ge(st, n - 1)
                        nc.tensor.matmul(PO[t % 2][:, cols], SD[:, m, :], QS[:, m, t * P:(t + 1) * P], start=True,
                                         stop=False, skip_group_check=True)
                    pe.wait_ge(dec, n + 1)
                    for i in range(4):
                        hc = m * P + i * RD
                        last = nc.tensor.matmul(PO[t % 2][i * RD:(i + 1) * RD, cols], KV[:, t, C + hc:C + hc + RD],
                                                AT[n % 2][:, i, :], start=(t == 0), stop=True,
                                                skip_group_check=True)
                    last.then_inc(outp, 1)
                    if n + 2 < len(steps):
                        scores(n + 2)

            @block.vector
            def _(dve):
                def decay(n):
                    t, m = steps[n]
                    dve.wait_ge(sc, n + 1)
                    if n >= 2:
                        dve.wait_ge(outp, n - 1)
                    nc.vector.tensor_tensor(AT[n % 2][:, :, :], ps[n % 2][:, :].rearrange("p (h i) -> p h i", h=4),
                                            DT[:, m * 4:m * 4 + 4, :], ALU.mult).then_inc(dec, 1)

                links = Links(dve, link)
                dve.wait_ge(dt_sent, 16)
                decay(0)
                for n, (t, m) in enumerate(steps):
                    if n + 1 < len(steps):
                        decay(n + 1)
                    if t + 1 < NT:
                        dve.wait_ge(smade, n + 1)
                        if n >= 2:
                            dve.wait_ge(st, n - 1)
                        links(nc.vector.tensor_tensor(TM[:, m, :], PS[m][:, :], BM, ALU.mult))
                        dve.wait_ge(outp, n + 1)
                        nc.vector.scalar_tensor_tensor(SD[:, m, :], SD[:, m, :], GC[:, m:m + 1], TM[:, m, :],
                                                       ALU.mult, ALU.add).then_inc(st, 1)
                    if m == 1:
                        dve.wait_ge(outp, n + 1)
                        nc.vector.tensor_copy(X2T[:, :, t * P:(t + 1) * P],
                                              PO[t % 2][:, :].rearrange("p (k n) -> p k n", k=KC)).then_inc(outd, 1)


RESIDENT = {
    "w0qkv": [P, KC, 384], "w0o": [P, KC, C],
    "w0f1": [P, KC, FF], "w0f2": [P, NF, C], "b1": [P, NF],
    "w1x": [P, KC, 3 * SS], "w1in": [P, KC, SS], "w1out": [SS, C], "cw": [P, KC, 4], "cb": [P, KC],
    "alog": [SS, 1], "dd": [P, KC],
    "w2": [P, KC, 3 * C], "w2b": [P, 4], "w2bv": [P, 2 * C], "cs": [P, KC, P],
    "kvs": [P, RH], "gc": [P, KC], "bm": [P, P],
    "wa": [P, KC, 3 * C], "wp": [P, KC, C],
    "w3": [P, KC, 320], "w3o": [P, KC, C],
    "wr": [P, KC, 10], "idx": [P, 8], "identf": [P, P],
}
PREPARE = {
    "bo": [LOW + 1, C], "b2": [LOW + 1, C],
    "qkw0": [P, 2, 16], "cos0": [P, NT, 8], "sin0": [P, NT, 2, 8], "qkw3": [P, 2, 32], "cos3": [P, NT, 16],
    "sin3": [P, NT, 2, 16], "wstd": [P, 16], "wrec": [P, 16], "negq": [P, P], "negk": [P, P],
}
SPLIT = ("w0qkv", "w2", "wa", "w3", "wr")
TERNARY = ("w0f1", "w0f2")
STREAMED = {
    "dt": [P, RH, P],
    "w1g": [P, KC, FF], "w1u": [P, KC, FF], "w1d": [P, NF, C],
    "sgu": [P, KC, 2 * SI], "sdn": [P, NSF, C], "w13": [P, KC, NE * ECOL], "wdn": [P, 2 * NE, C],
}


def build(nc, dram, out):
    ctx = ExitStack()
    with ctx:
        def sb(name, shape, dt=F32):
            return ctx.enter_context(nc.sbuf_tensor(name, shape, dt))

        W, RAW = {}, {}
        for n, s in RESIDENT.items():
            if n in SPLIT + TERNARY:
                RAW[n], W[n] = raw_and_low(nc, ctx, "s_" + n, s)
            else:
                RAW[n] = W[n] = sb("s_" + n, s)
        WH = {n: sb("h_" + n, RESIDENT[n], FR) for n in SPLIT}
        X, XTH = sb("X", [P, NT, C]), sb("XTh", [P, KC, T], FR)
        XTR, XTL = raw_and_low(nc, ctx, "XTl", [P, KC, T])
        XT = (XTH, XTL)
        ident = sb("ident", [P, P], BF16)
        negq, negk = sb("negqb", [P, P], BF16), sb("negkb", [P, P], BF16)
        ones = sb("ones", [LOW + 1, P], FR)
        BIAS = {n: sb("bias_" + n, [LOW + 1, C], FR) for n in ("bo", "b2")}
        diag = sb("diag", [P, KC, P])
        NA = sb("NA", [SS, 1])
        e50, eps = sb("e50", [P, 1]), sb("eps", [P, 1])
        ROPE = [[sb(f"{n}w{i}", [P, NT, 2, D]) for n in ("cos", "sin")] for i, D in ((0, 16), (3, 32))]
        with ExitStack() as c, Core(nc) as core:
            setup(nc, c, core, W, WH, RAW, XT, XTR, dram, ident, negq, negk, ones, BIAS, diag, NA, e50, eps,
                  ROPE)
        with nc.Fori(0, B) as b, Core(nc) as whole:
            batch(nc, whole, b, dram, out, W, WH, X, XT, XTR, ident, negq, negk, ones, BIAS, diag, NA, e50, eps,
                  ROPE)


def setup(nc, c, core, W, WH, RAW, XT, XTR, dram, ident, negq, negk, ones, BIAS, diag, NA, e50, eps, ROPE):
    tern_loaded, loaded, ones_made, link, red, summed, rooted, al = (
        core.sem(n) for n in ("tern_loaded", "loaded", "ones_made", "set_v", "reduced", "summed", "rooted", "set_a"))
    A = c.enter_context(nc.sbuf_tensor("absum", [P, 2], F32))
    onesf = c.enter_context(nc.sbuf_tensor("onesf", [P, P], F32))
    zeros = c.enter_context(nc.sbuf_tensor("zeros", [LOW + 1, C], F32))
    BH = c.enter_context(nc.sbuf_tensor("bias_high", [LOW + 1, C], F32))
    A2 = c.enter_context(nc.sbuf_tensor("absum2", [P, 2], F32))
    NW = c.enter_context(nc.sbuf_tensor("neg_tern", [P, NF * C], F32))
    SC = c.enter_context(nc.sbuf_tensor("head_scales", [P, 3, 16], F32))
    WS = c.enter_context(nc.sbuf_tensor("wa_raw", [P, KC, 3 * C], F32))
    PR = {n: c.enter_context(nc.sbuf_tensor("s_" + n, s, F32)) for n, s in PREPARE.items()}
    ps = c.enter_context(nc.psum_tensor("set_ps", [P, 2], F32))
    rest = {n: t for n, t in (PR | RAW).items() if n not in TERNARY}
    all_loaded = 16 * (len(rest) + 1)
    with nc.Block() as block:
        @block.sync
        def _(sp):
            for n in TERNARY:
                sp.dma_start(RAW[n][:, :, :], dram[n]).then_inc(tern_loaded, 16)
            for n, t in rest.items():
                sp.dma_start(t[tuple(slice(None) for _ in t.shape)], dram[n]).then_inc(loaded, 16)
            sp.dma_start(XTR[:, :, :], dram["xt"][:, :, 0:T]).then_inc(loaded, 16)
            sp.wait_ge(loaded, all_loaded)

        @block.vector
        def _(dve):
            links = Links(dve, link)
            links(nc.vector.memset(onesf[:, :], 1.0))
            links(nc.vector.memset(zeros[:, :], 0.0))
            links(nc.vector.tensor_copy(ones[:, :], onesf[0:LOW + 1, :]))
            links(nc.vector.memset(e50[:, :], E50))
            links(nc.vector.memset(eps[:, :], LN_EPS))
            dve.wait_ge(tern_loaded, 16 * len(TERNARY))
            w1, w2 = RAW["w0f1"][:, :, :], RAW["w0f2"][:, :, :]
            links(nc.vector.tensor_reduce(A[:, 0:1], w1, AX.XY, ALU.add, apply_absolute_value=True))
            nc.vector.tensor_reduce(A[:, 1:2], w2, AX.XY, ALU.add, apply_absolute_value=True).then_inc(red, 1)
            dve.wait_ge(summed, 1)
            links(nc.vector.tensor_scalar(A[:, :], ps[:, :], 1.0 / (FF * C), 0.7, ALU.mult, ALU.mult))
            links(nc.vector.tensor_scalar(A2[:, :], A[:, :], -1.0, None, ALU.mult))
            for j, (n, w) in enumerate(zip(TERNARY, (w1, w2))):
                nw = NW[:, :].rearrange("p (a n) -> p a n", a=w.shape[1])
                links(nc.vector.tensor_scalar(nw, w, A2[:, j:j + 1], None, ALU.is_le))
                links(nc.vector.tensor_scalar(w, w, A[:, j:j + 1], None, ALU.is_ge))
                links(nc.vector.tensor_tensor(W[n][:, :, :], w, nw, ALU.subtract))
            dve.wait_ge(loaded, all_loaded)
            for n, bias in BIAS.items():
                links(nc.vector.tensor_copy(bias[:, :], PR[n][:, :]))
                links(nc.vector.tensor_copy(BH[:, :], f32(bias[:, :])))
                links(nc.vector.tensor_copy(bias[:, :], zeros[:, :]))
                links(high_part(nc, bias[0:1, :], PR[n][0:1, :]))
                links(low_part(nc, bias[LOW:LOW + 1, :], PR[n][LOW:LOW + 1, :], BH[LOW:LOW + 1, :]))
            links(nc.vector.tensor_copy(ident[:, :], W["identf"][:, :]))
            links(nc.vector.tensor_copy(negq[:, :], PR["negq"][:, :]))
            links(nc.vector.tensor_copy(negk[:, :], PR["negk"][:, :]))
            for k in range(KC):
                links(nc.vector.tensor_scalar(diag[:, k, :], W["identf"][:, :], W["dd"][:, k:k + 1], None, ALU.mult))
            for rope, i in zip(ROPE, (0, 3)):
                cosw, sinw = rope
                w, cos, sin = PR[f"qkw{i}"], PR[f"cos{i}"], PR[f"sin{i}"]
                h2 = cos.shape[2]
                for g in range(2):
                    for half in range(2):
                        to, other = slice(half * h2, (half + 1) * h2), slice((1 - half) * h2, (2 - half) * h2)
                        wide = lambda x: w[:, g, x].unsqueeze(1).broadcast_to([P, NT, h2])
                        nc.vector.tensor_tensor(cosw[:, :, g, to], cos[:, :, :], wide(to), ALU.mult)
                        links(nc.vector.tensor_tensor(sinw[:, :, g, to], sin[:, :, half, :], wide(other), ALU.mult))
            links(nc.vector.tensor_scalar(SC[:, 2, :], PR["wrec"][:, :], 0.1, None, ALU.is_gt))
            links(nc.vector.tensor_scalar(SC[:, 0, :], PR["wstd"][:, :], 1e-8, None, ALU.max))
            nc.vector.tensor_scalar(SC[:, 1, :], PR["wrec"][:, :], 1e-8, None, ALU.max).then_inc(red, 1)
            dve.wait_ge(rooted, 1)
            wa = RAW["wa"]
            links(nc.vector.tensor_copy(WS[:, :, :], wa[:, :, :]))
            for k in range(KC):
                raw = lambda a: WS[:, k, a:a + 128].rearrange("p (h d) -> p h d", h=16)
                new = lambda a, lo: wa[:, k, a:a + 256].rearrange("p (h d) -> p h d", h=16)[:, :, lo:lo + 8]
                s = lambda j: SC[:, j, :].unsqueeze(2).broadcast_to([P, 16, 8])
                links(nc.vector.tensor_tensor(new(0, 0), raw(0), s(0), ALU.mult))
                links(nc.vector.tensor_tensor(new(C, 0), raw(128), s(0), ALU.mult))
                links(nc.vector.tensor_copy(wa[:, k, 2 * C:3 * C], WS[:, k, 256:512]))
                tq, tk = new(0, 8), new(C, 8)
                links(nc.vector.tensor_scalar(NW[:, 0:16], SC[:, 2, :], -1.0, 1.0, ALU.mult, ALU.add))
                no = NW[:, 0:16].unsqueeze(2).broadcast_to([P, 16, 8])
                t1 = NW[:, 128:256].rearrange("p (h d) -> p h d", h=16)
                for dst, keep, swap in ((tq, raw(512), raw(640)), (tk, raw(640), raw(512))):
                    links(nc.vector.tensor_tensor(dst, keep, no, ALU.mult))
                    links(nc.vector.tensor_tensor(t1, swap, s(2), ALU.mult))
                    links(nc.vector.tensor_tensor(dst, dst, t1, ALU.add))
                    links(nc.vector.tensor_tensor(dst, dst, s(1), ALU.mult))
            cut_in_two(nc, links, XT[0][:, :, :], XT[1][:, :, :], XTR[:, :, :])
            for n in SPLIT:
                cut_in_two(nc, links, WH[n][:, :, :], W[n][:, :, :], RAW[n][:, :, :])
            dve.wait_ge(al, 1)
            links(nc.vector.tensor_scalar(NA[:, :], NA[:, :], -1.0, None, ALU.mult))

        @block.tensor
        def _(pe):
            pe.wait_ge(red, 1)
            nc.tensor.matmul(ps[:, :], onesf[:, :], A[:, :], start=True, stop=True).then_inc(summed, 1)

        @block.scalar
        def _(act):
            act.wait_ge(loaded, all_loaded)
            nc.scalar.activation(NA[:, :], W["alog"][:, :], ACT.Exp).then_inc(al, 1)
            act.wait_ge(red, 2)
            nc.scalar.activation(SC[:, 0:2, :], SC[:, 0:2, :], ACT.Sqrt).then_inc(rooted, 1)


def batch(nc, whole, b, dram, out, W, WH, X, XT, XTR, ident, negq, negk, ones, BIAS, diag, NA, e50, eps, ROPE):
    identf = W["identf"]
    tok = lambda t: slice(t * P, (t + 1) * P)
    x_loaded, xt_loaded = whole.sem("x_loaded"), whole.sem("xt_loaded")
    both = lambda n: (WH[n], W[n])

    def dense(YT, w, bias=None):
        def product(t, j):
            for k in range(KC):
                yield YT[:, k, tok(t)], w[:, k, :], (0, C)
            if bias is not None:
                yield ones[:, :], bias[:, :], (0, C)
        return product

    def hidden(H, w, bias=None):
        def product(t, j):
            for f in range(NF):
                right = w[0][:, f, :], (w[1][:, f, :] if len(w) > 1 else None)
                for a, b in pairs([x[:, f, tok(t)] for x in H], right):
                    yield a, b, (0, C)
            if bias is not None:
                yield ones[:, :], bias[:, :], (0, C)
        return product

    with Core(nc) as core:
        with ExitStack() as c:
            def sb(name, shape, dt=F32):
                return c.enter_context(nc.sbuf_tensor(name, shape, dt))
            QK, V = sb("a0qk", [P, NT, 320]), sb("a0v", [P, NT, 64])
            Y, YT = sb("a0y", [P, NT, C]), sb("a0yt", [P, KC, T])
            SV, SVT = sb("a0sv", [P, NT, 4, 32]), sb("a0svt", [P, 4, 2])
            with ExitStack() as c2:
                SQ = c2.enter_context(nc.sbuf_tensor("a0sq", [P, NT, 320], F32))
                project_tokens(nc, core, "p0", XT, both("w0qkv"),
                               [(0, 320, lambda t, a, e: QK[:, t, a:e]),
                                (320, 384, lambda t, a, e: V[:, t, a:e])], SQ,
                               [(X[:, :, :], dram["x"][:, bass.ds(b * NT, NT), :], x_loaded)])
                norm_rope(nc, core, "r0", QK, SQ, 20, 16, *ROPE[0], False, 2, (V, SV, SVT, e50))
            attention(nc, core, "a0", QK, V, Y, (ident, identf, negq, negk), D=16, NH=16, q0=0, k0=256,
                      kv_of=lambda i, u: i, kper=True, cap=True, scale=0.25,
                      SV=SVT, U=4)
            close_layer(nc, core, "c0", X, XT, identf, eps, dense(YT, W["w0o"], BIAS["bo"]), light=True,
                        arrives=(x_loaded, 16), turning=(Y, YT, 4))
        with ExitStack() as c:
            H = [c.enter_context(nc.sbuf_tensor("f0h" + n, [P, NF, T], FR)) for n in "hl"]
            front = Hidden(nc, core, "f0", XT, H, lambda f, side, k: (W["w0f1"][:, k, tok(f)],), bias=W["b1"])
            close_layer(nc, core, "c1", X, XT, identf, eps, hidden(H, (W["w0f2"],), BIAS["b2"]), front=front)
    with Core(nc) as core:
        with ExitStack() as c:
            r1, w1 = {}, {}
            for n in ("w1g", "w1u", "w1d"):
                r1[n], w1[n] = raw_and_low(nc, c, "s_" + n, STREAMED[n])
            w1h = {n: c.enter_context(nc.sbuf_tensor("h_" + n, STREAMED[n], FR)) for n in ("w1g", "w1u")}
            w1dh = w1h["w1g"][:, :, :].rearrange("p k n -> p (k n)").rearrange("p (f n) -> p f n", f=NF)
            sent = whole.sem("w1_loaded")
            with ExitStack() as c2:
                XC = c2.enter_context(nc.sbuf_tensor("m1xc", [P, KC, T], F32))
                HM = c2.enter_context(nc.sbuf_tensor("m1hm", [SS, T], F32))
                XTF = c2.enter_context(nc.sbuf_tensor("m1xt", [P, KC, T], F32))
                scan_mixer(nc, core, "m1", [(t[:, :, :], dram[n], sent) for n, t in r1.items()], XT, XTF, W["w1x"],
                           W["w1in"], W["cw"], W["cb"], NA, XC, HM)

                def product(t, j):
                    yield HM[:, tok(t)], W["w1out"][:, :], (0, C)
                    for k in range(KC):
                        yield XC[:, k, tok(t)], diag[:, k, :], (k * P, (k + 1) * P)
                close_layer(nc, core, "c2", X, XT, identf, eps, product, light=True, sent=(sent, 48),
                            weights=[tuple(w[n][:, k, :] for w in (w1h, w1, r1)) for n in w1h for k in range(KC)])
            H = [c.enter_context(nc.sbuf_tensor("f1h" + n, [P, NF, T], FR)) for n in "hl"]
            late = [tuple(w[:, f:f + 2, :] for w in (w1dh, w1["w1d"], r1["w1d"])) for f in range(0, NF, 2)]
            both_parts = lambda f, side, k: [w[("w1g", "w1u")[side]][:, k, tok(f)] for w in (w1h, w1)]
            front = Hidden(nc, core, "f1", XT, H, both_parts, late=late)
            close_layer(nc, core, "c3", X, XT, identf, eps, hidden(H, (w1dh, w1["w1d"])), front=front)

    with Core(nc) as core:
        with ExitStack() as c:
            X2T = c.enter_context(nc.sbuf_tensor("m2x", [P, KC, T], F32))
            DT = c.enter_context(nc.sbuf_tensor("m2dt", STREAMED["dt"], F32))
            dt_sent = whole.sem("m2_decays_loaded")
            retention(nc, core, "m2", [(DT[:, :, :], dram["dt"], dt_sent)], XT, both("w2"), W["w2b"], DT, dt_sent,
                      W["cs"], W["kvs"][:, :], W["gc"], W["bm"][:, :], W["w2bv"][:, :], X2T)

            def product(t, j):
                for k in range(KC):
                    yield X2T[:, k, tok(t)], identf[:, :], (k * P, (k + 1) * P)
            close_layer(nc, core, "c4", X, XT, identf, eps, product, light=True)
        with ExitStack() as c:
            def sb(name, shape, dt=F32):
                return c.enter_context(nc.sbuf_tensor(name, shape, dt))
            QK, V = sb("a2qk", [P, NT, 512]), sb("a2v", [P, NT, 256])
            Y, YT = sb("a2y", [P, NT, C]), sb("a2yt", [P, KC, T])
            project_tokens(nc, core, "p2", XT, both("wa"),
                           [(0, 512, lambda t, a, e: QK[:, t, a:e]),
                            (512, 768, lambda t, a, e: V[:, t, a:e])])
            attention(nc, core, "a2", QK, V, Y, (ident, identf, negq, negk), D=16, NH=16, q0=0, k0=256,
                      kv_of=lambda i, u: i * 4 + u, kper=True, cap=False, scale=0.25,
                      SV=None, U=4)
            close_layer(nc, core, "c5", X, XT, identf, eps, dense(YT, W["wp"]), light=True,
                        turning=(Y, YT, 4))
    with Core(nc) as core:
        with ExitStack() as c:
            r3, w3 = {}, {}
            for n in ("sgu", "sdn"):
                r3[n], w3[n] = raw_and_low(nc, c, "s_" + n, STREAMED[n])
            half = NSF // 2 * P
            UH = c.enter_context(nc.sbuf_tensor("f3uh", [P, KC, 2 * max(ECOL, half)], FR))

            def up_weights(kind, a, e):
                if kind == "experts":
                    return [(UH[:, k, 0:2 * ECOL], *(w["w13"][:, k, a * ECOL:e * ECOL] for w in (w3, r3)))
                            for k in range(KC)]
                n = e - a
                return [(UH[:, :, g * n:(g + 1) * n], *(w["sgu"][:, :, g * SI + a:g * SI + e] for w in (w3, r3)))
                        for g in range(2)]

            sent3, sent_experts = whole.sem("w3_shared_loaded"), whole.sem("w3_experts_loaded")
            with ExitStack() as c2:
                def sb(name, shape, dt=F32):
                    return c2.enter_context(nc.sbuf_tensor(name, shape, dt))
                QK, V = sb("a3qk", [P, NT, 288]), sb("a3v", [P, NT, 32])
                Y, YT = sb("a3y", [P, NT, C]), sb("a3yt", [P, KC, T])
                with ExitStack() as c4:
                    SQ = c4.enter_context(nc.sbuf_tensor("a3sq", [P, NT, 288], F32))
                    project_tokens(nc, core, "p3", XT, both("w3"),
                                   [(0, 288, lambda t, a, e: QK[:, t, a:e]),
                                    (288, 320, lambda t, a, e: V[:, t, 0:32])], SQ,
                                   [(r3[n][:, :, :], dram[n], sent3) for n in ("sgu", "sdn")])
                    norm_rope(nc, core, "r3", QK, SQ, 9, 32, *ROPE[1], True, 3)
                attention(nc, core, "a3", QK, V, Y, (ident, identf, negq, negk), D=32, NH=8, q0=0, k0=256,
                          kv_of=lambda i, u: 0, kper=False, cap=False, scale=1.0 / 16.0,
                          SV=None, U=4)
                close_layer(nc, core, "c6", X, XT, identf, eps, dense(YT, W["w3o"]), light=True,
                            turning=(Y, YT, 2), sent=(sent3, 32), weights=up_weights("shared", 0, half))
            for n in ("w13", "wdn"):
                r3[n], w3[n] = raw_and_low(nc, c, "s_" + n, STREAMED[n])
            GT = c.enter_context(nc.sbuf_tensor("f3gt", [P, NT, 9], F32))
            H = [c.enter_context(nc.sbuf_tensor("f3h" + n, [P, 4, T], FR)) for n in "hl"]
            DH = c.enter_context(nc.sbuf_tensor("f3dh", [P, 4, C], FR))
            parts = [("shared", (0, half)), ("shared", (half, SI))]
            parts += [("experts", (e, e + 2)) for e in range(0, NE, 2)]

            def down_weights(kind, a, e):
                if kind == "experts":
                    return DH[:, :, :], *(w["wdn"][:, 2 * a:2 * e, :] for w in (w3, r3))
                n = (e - a + P - 1) // P
                return DH[:, 0:n, :], *(w["sdn"][:, a // P:a // P + n, :] for w in (w3, r3))

            into = lambda r, i: (lambda h: [x[0:r, i, h * CH:(h + 1) * CH] for x in H])
            work = []
            for kind, (a, e) in parts:
                items = []
                if kind == "shared":
                    for i, f in enumerate(range(a, e, P)):
                        r = min(P, e - f)

                        def side(k, g, f=f, r=r, a=a, e=e):
                            u = g * (e - a) + f - a
                            return UH[:, k, u:u + r], w3["sgu"][:, k, g * SI + f:g * SI + f + r]
                        items.append((lambda k, side=side: side(k, 0), lambda k, side=side: side(k, 1), r, 0, r,
                                      into(r, i)))

                    def product(t, j, a=a, e=e):
                        for i, f in enumerate(range(a, e, P)):
                            r = min(P, e - f)
                            for p in pairs([x[0:r, i, tok(t)] for x in H],
                                           (DH[0:r, i, :], w3["sdn"][0:r, f // P, :])):
                                yield (*p, (0, C))
                    gates = [lambda t: GT[:, t, 8:9]]
                else:
                    for s in range(e - a):
                        def side(k, u, v, s=s, a=a):
                            return (UH[:, k, s * ECOL + u:s * ECOL + v],
                                    w3["w13"][:, k, (a + s) * ECOL + u:(a + s) * ECOL + v])
                        items.insert(s, (lambda k, side=side: side(k, 2 * P, ECOL), None, EREM, 64, 64 + EREM,
                                         into(EREM, 2 * s + 1)))
                        items.append((lambda k, side=side: side(k, 0, P), lambda k, side=side: side(k, P, 2 * P),
                                      P, 0, P, into(P, 2 * s)))

                    def product(t, j, a=a):
                        for i, r in ((2 * j, P), (2 * j + 1, EREM)):
                            for p in pairs([x[0:r, i, tok(t)] for x in H],
                                           (DH[0:r, i, :], w3["wdn"][0:r, 2 * a + i, :])):
                                yield (*p, (0, C))
                    gates = [lambda t, g=g: GT[:, t, g:g + 1] for g in range(a, e)]
                work.append(dict(items=items, product=product, gates=gates, up=up_weights(kind, a, e),
                                 down=down_weights(kind, a, e)))
            expert_parts(nc, core, "h3", [(r3[n][:, :, :], dram[n], sent_experts) for n in ("w13", "wdn")], X, XT,
                         identf, work, (2, (sent_experts, 32)), both("wr"), GT, W["idx"][:, :])
            close_layer(nc, core, "c7", X, XT, identf, eps, work[-1]["product"], work[-1]["gates"],
                        out=out[:, bass.ds(b * NT, NT), :],
                        loads=[(XTR[:, :, :], dram["xt"][:, :, T:(B + 1) * T][:, :, bass.ds(b * T, T)], xt_loaded)],
                        weights=[(*(x[:, k, :] for x in XT), XTR[:, k, :]) for k in range(KC)],
                        sent=(xt_loaded, 16), first_cut=4)


def expert_parts(nc, core, name, loads, X, XT, identf, parts, sent, WR, GT, IDX):
    S = lambda n: core.sem(f"{name}_{n}")
    hidden_made, gate_done, up_done, high_done, split, made, added, up_high, up_cut, down_high, down_cut = (
        S("hidden_made"), S("gate_done"), S("up_done"), S("high_done"), S("split"), S("made"), S("added"),
        S("up_high"), S("up_cut"), S("down_high"), S("down_cut"))
    r_made, r_taken, routed, logits, ex, r_link = (S("r_made"), S("r_taken"), S("routed"), S("logits"), S("exp"),
                                                   S("r"))
    NR = WR[0].shape[2]
    BANKS, UBANKS, OBANKS, SLOTS = 3, 2, 3, 3
    with ExitStack() as c:
        pg = [c.enter_context(nc.psum_tensor(f"{name}_pg{i}", [P, CH], F32)) for i in range(BANKS)]
        pu = [c.enter_context(nc.psum_tensor(f"{name}_pu{i}", [P, CH], F32)) for i in range(UBANKS)]
        po = [c.enter_context(nc.psum_tensor(f"{name}_po{i}", [P, CH], F32)) for i in range(OBANKS)]
        G = [c.enter_context(nc.sbuf_tensor(f"{name}_g{i}", [P, CH], F32)) for i in range(SLOTS)]
        sb = lambda n, w: c.enter_context(nc.sbuf_tensor(f"{name}_{n}", [P, NT, w], F32))
        LG, PR, E1, E2, RM = sb("lg", 9), sb("pr", 8), sb("e1", 8), sb("e2", 8), sb("rm", 1)
        LT = [G[1 + h][0:NR, :] for h in range(NCH)]
        pr = po[0][:, 0:NT * NR].rearrange("p (t n) -> p t n", t=NT)
        with nc.Block() as block:
            @block.sync
            def _(sp):
                start_loads(sp, loads)

            @block.tensor
            def _(pe):
                for h in range(NCH):
                    mms = [p for k in range(KC) for p in pairs([w[:, k, :] for w in WR],
                                                               [x[:, k, h * CH:(h + 1) * CH] for x in XT])]
                    for i, (w, x) in enumerate(mms):
                        last = nc.tensor.matmul(po[1 + h][0:NR, :], w, x, start=(i == 0), stop=(i == len(mms) - 1))
                    last.then_inc(r_made, 1)

                def turn_logits():
                    pe.wait_ge(r_taken, NCH)
                    for t in range(NT):
                        h, a = divmod(t * P, CH)
                        last = nc.tensor.transpose(pr[:, t, :], LT[h][:, a:a + P], identf[0:NR, 0:NR])
                    last.then_inc(routed, 1)

                n = d = 0
                for p, part in enumerate(parts):
                    if p:
                        pe.wait_ge(up_cut, KC * p)
                    for h in range(NCH):
                        for gw, uw, rows, urow, M, dst in part["items"]:
                            if n >= UBANKS:
                                pe.wait_ge(up_done, n - UBANKS + 1)
                            for bank, lhs in ((pg[n % BANKS][0:M, :], gw), (pu[n % UBANKS][0:rows, :], uw)):
                                if lhs is None:
                                    continue
                                mms = [m for k in range(KC)
                                       for m in pairs(lhs(k), [x[:, k, h * CH:(h + 1) * CH] for x in XT])]
                                for i, (w, x) in enumerate(mms):
                                    last = nc.tensor.matmul(bank, w, x, start=(i == 0), stop=(i == len(mms) - 1))
                            last.then_inc(hidden_made, 1)
                            if n == 0:
                                turn_logits()
                            n += 1
                    if p == len(parts) - 1:
                        break
                    pe.wait_ge(down_cut, p + 1)
                    for t in range(NT):
                        if t % (NT // NCH) == 0:
                            pe.wait_ge(split, n - (NCH - 1 - t * NCH // NT) * len(part["items"]))
                        for j in range(len(part["gates"])):
                            if d >= OBANKS:
                                pe.wait_ge(added, d - OBANKS + 1)
                            mms = list(part["product"](t, j))
                            for i, (x, w, cols) in enumerate(mms):
                                last = nc.tensor.matmul(po[d % OBANKS][:, 0:C], x, w, start=(i == 0),
                                                        stop=(i == len(mms) - 1))
                            last.then_inc(made, 1)
                            d += 1

            @block.scalar
            def _(act):
                for h in range(NCH):
                    act.wait_ge(r_made, h + 1)
                    nc.scalar.activation(LT[h], po[1 + h][0:NR, :], ACT.Copy).then_inc(r_taken, 1)
                n = 0
                for part in parts:
                    for h in range(NCH):
                        for gw, uw, rows, urow, M, dst in part["items"]:
                            act.wait_ge(hidden_made, n + 1)
                            if n == 1:
                                act.wait_ge(routed, 1)
                            if n >= SLOTS:
                                act.wait_ge(split, n - SLOTS + 1)
                            nc.scalar.activation(G[n % SLOTS][0:rows, :], pg[n % BANKS][0:rows, :],
                                                 ACT.Silu).then_inc(gate_done, 1)
                            if n == 1:
                                act.wait_ge(logits, 1)
                                nc.scalar.activation(LG[:, :, :], LG[:, :, :], ACT.Exp).then_inc(ex, 1)
                            n += 1

            @block.gpsimd
            def _(pool):
                n = 0
                for p, part in enumerate(parts):
                    for h in range(NCH):
                        for i, (gw, uw, rows, urow, M, dst) in enumerate(part["items"]):
                            if h == 0 and i == 2:
                                pool.wait_ge(down_high, p + 1)
                                high, low, raw = part["down"]
                                nc.gpsimd.tensor_tensor(low, raw, f32(high), ALU.subtract).then_inc(down_cut, 1)
                            pool.wait_ge(high_done, n + 1)
                            nc.gpsimd.tensor_tensor(dst(h)[1], G[n % SLOTS][0:rows, :], f32(dst(h)[0]),
                                                    ALU.subtract).then_inc(split, 1)
                            n += 1
                    for k, (high, low, raw) in enumerate(parts[p + 1]["up"] if p + 1 < len(parts) else ()):
                        pool.wait_ge(up_high, p * KC + k + 1)
                        nc.gpsimd.tensor_tensor(low, raw, f32(high), ALU.subtract).then_inc(up_cut, 1)

            @block.vector
            def _(dve):
                rlinks = Links(dve, r_link)
                row = lambda a: a[:, :, :].broadcast_to([P, NT, 8])
                idx = IDX.unsqueeze(1).broadcast_to([P, NT, 8])

                def route_logits():
                    dve.wait_ge(routed, 1)
                    rlinks(nc.vector.tensor_reduce(RM[:, :, 0], pr[:, :, 0:8], AX.X, ALU.max))
                    rlinks(nc.vector.tensor_tensor(LG[:, :, 0:8], pr[:, :, 0:8], row(RM), ALU.subtract))
                    nc.vector.tensor_scalar(LG[:, :, 8], pr[:, :, 8], -1.0, None, ALU.mult).then_inc(logits, 1)

                def route_shares():
                    dve.wait_ge(ex, 1)
                    rlinks(nc.vector.tensor_scalar(E1[:, :, 0], LG[:, :, 8], 1.0, None, ALU.add))
                    rlinks(nc.vector.reciprocal(GT[:, :, 8], E1[:, :, 0]))
                    rlinks(nc.vector.tensor_reduce(RM[:, :, 0], LG[:, :, 0:8], AX.X, ALU.add))
                    rlinks(nc.vector.reciprocal(RM[:, :, :], RM[:, :, :]))
                    rlinks(nc.vector.tensor_tensor(PR[:, :, :], LG[:, :, 0:8], row(RM), ALU.mult))

                def route_pick(r):
                    src = (PR, E2)[r]
                    rlinks(nc.vector.tensor_reduce(RM[:, :, 0], src[:, :, :], AX.X, ALU.max))
                    rlinks(nc.vector.tensor_tensor(E1[:, :, :], src[:, :, :], row(RM), ALU.is_equal))
                    rlinks(nc.vector.tensor_tensor(E1[:, :, :], E1[:, :, :], idx, ALU.mult))
                    rlinks(nc.vector.tensor_reduce(RM[:, :, 0], E1[:, :, :], AX.X, ALU.max))
                    rlinks(nc.vector.tensor_tensor(E1[:, :, :], row(RM), idx, ALU.is_equal))
                    if r == 0:
                        rlinks(nc.vector.scalar_tensor_tensor(E2[:, :, :], E1[:, :, :], -2.0, PR[:, :, :],
                                                              ALU.mult, ALU.add))
                        rlinks(nc.vector.tensor_tensor(GT[:, :, 0:8], E1[:, :, :], PR[:, :, :], ALU.mult))
                    else:
                        rlinks(nc.vector.tensor_tensor(E1[:, :, :], E1[:, :, :], PR[:, :, :], ALU.mult))
                        rlinks(nc.vector.tensor_tensor(GT[:, :, 0:8], GT[:, :, 0:8], E1[:, :, :], ALU.add))

                n = d = 0
                for p, part in enumerate(parts):
                    for h in range(NCH):
                        for i, (gw, uw, rows, urow, M, dst) in enumerate(part["items"]):
                            dve.wait_ge(gate_done, n + 1)
                            up = (pu[n % UBANKS][0:rows, :] if uw is not None
                                  else pg[n % BANKS][urow:urow + rows, :])
                            g = G[n % SLOTS][0:rows, :]
                            nc.vector.tensor_tensor(g, g, up, ALU.mult).then_inc(up_done, 1)
                            dve.wait_ge(up_done, n + 1)
                            high_part(nc, dst(h)[0], g).then_inc(high_done, 1)
                            if n == 0:
                                route_logits()
                            elif n == 1:
                                route_shares()
                            elif n in (2, 3):
                                route_pick(n - 2)
                            n += 1
                            if h == 0 and i == 1:
                                high, low, raw = part["down"]
                                high_part(nc, high, raw).then_inc(down_high, 1)
                    if p == len(parts) - 1:
                        break
                    for t in range(NT):
                        for j, gate in enumerate(part["gates"]):
                            dve.wait_ge(made, d + 1)
                            if j:
                                dve.wait_ge(added, d)
                            nc.vector.scalar_tensor_tensor(X[:, t, :], po[d % OBANKS][:, 0:C], gate(t), X[:, t, :],
                                                           ALU.mult, ALU.add).then_inc(added, 1)
                            d += 1
                        if t < KC:
                            if p + 1 == sent[0] and t == 0:
                                dve.wait_ge(*sent[1])
                            high, low, raw = parts[p + 1]["up"][t]
                            high_part(nc, high, raw).then_inc(up_high, 1)


def tables():
    f = np.float32
    d = {}

    def rope(theta, dim, sign):
        inv = 1.0 / theta ** (np.arange(0, dim, 2, dtype=np.float64) / dim)
        fr = np.outer(np.arange(T), inv.astype(f)).astype(f)
        fr = fr.reshape(NT, P, dim // 2).transpose(1, 0, 2)
        return np.cos(fr).astype(f), np.stack([sign * np.sin(fr), -sign * np.sin(fr)], axis=2).astype(f)

    d["cos0"], d["sin0"] = rope(10000.0, 16, 1.0)
    d["cos3"], d["sin3"] = rope(1000000.0, 32, -1.0)
    betas = np.linspace(np.log2(1.0 / 32.0), np.log2(1.0 / 512.0), RH)
    g = 1.0 - np.exp2(betas)
    i = np.arange(P)
    ij = i[None, :] - i[:, None]
    d["dt"] = np.where(ij[:, None, :] >= 0, g[None, :, None] ** np.maximum(ij, 0)[:, None, :], 0.0).astype(f)
    hp = np.repeat(np.arange(4), RD)
    gh = np.stack([g[4 * m + hp] for m in range(KC)], axis=1)
    d["cs"] = (gh[:, :, None] ** (i + 1)[None, None, :]).astype(f)
    d["kvs"] = (g[None, :] ** (P - 1 - i)[:, None]).astype(f)
    d["gc"] = (gh ** P).astype(f)
    d["bm"] = (hp[:, None] == hp[None, :]).astype(f)
    d["idx"] = np.tile(np.arange(8, 0, -1).astype(f), (P, 1))
    d["identf"] = np.eye(P, dtype=f)
    d["negq"] = np.where(i[None, :] > i[:, None], NEG, 0.0).astype(f)
    d["negk"] = np.where(i[:, None] > i[None, :], NEG, 0.0).astype(f)
    return d


def layout(a):
    def kn(w):
        return w.reshape(w.shape[0] // P, P, w.shape[1]).transpose(1, 0, 2)

    def col(v):
        return v.reshape(-1, P).T

    def rows(v):
        return np.broadcast_to(v[None, :], (P, v.shape[0]))

    d = {}
    x = a["L0_attn_x"].reshape(B * T, C)
    d["x"] = x.reshape(B * NT, P, C).transpose(1, 0, 2)
    d["xt"] = kn(np.concatenate([x, x[:T]]).T)
    d["w0qkv"] = kn(np.concatenate([a["L0_attn_Wq"], a["L0_attn_Wk"], a["L0_attn_Wv"]], 0).T)
    d["w0o"], d["bo"] = kn(a["L0_attn_Wo"].T), rows(a["L0_attn_bo"])[:LOW + 1]
    d["qkw0"] = rows(np.concatenate([a["L0_attn_q_norm_w"], a["L0_attn_k_norm_w"]])).reshape(P, 2, 16)
    d["w0f1"], d["w0f2"] = kn(a["L0_ffn_w1"].T), kn(a["L0_ffn_w2"].T)
    d["b1"], d["b2"] = col(a["L0_ffn_b1"]), rows(a["L0_ffn_b2"])[:LOW + 1]
    wx = a["L1_attn_Wxproj"]
    d["w1x"] = kn(np.concatenate([np.repeat(wx[2 * SS:], SS, 0), wx[:2 * SS]], 0).T)
    d["w1in"], d["w1out"] = kn(a["L1_attn_Winproj"].T), a["L1_attn_Woutproj"].T
    d["cw"] = a["L1_attn_conv_w"].reshape(KC, P, 4).transpose(1, 0, 2)
    d["cb"], d["alog"], d["dd"] = col(a["L1_attn_conv_b"]), a["L1_attn_A_log"][:, None], col(a["L1_attn_D"])
    d["w1g"], d["w1u"], d["w1d"] = kn(a["L1_ffn_w_gate"].T), kn(a["L1_ffn_w_up"].T), kn(a["L1_ffn_w_down"].T)
    d["w2"] = kn(np.concatenate([a["L2_attn_Wq"], a["L2_attn_Wk"], a["L2_attn_Wv"]], 1))
    d["w2b"] = np.concatenate([col(a["L2_attn_bq"]), col(a["L2_attn_bk"])], 1)
    d["w2bv"] = rows(np.concatenate([a["L2_attn_bk"], a["L2_attn_bv"]]))
    d["wa"], d["wp"] = kn(a["L2_ffn_Wa"]), kn(a["L2_ffn_Wp"])
    d["wstd"], d["wrec"] = rows(a["L2_ffn_w_std"]), rows(a["L2_ffn_w_rec"])
    d["w3"] = kn(np.concatenate([a["L3_attn_q_proj"], a["L3_attn_k_proj"], a["L3_attn_v_proj"]], 0).T)
    d["w3o"] = kn(a["L3_attn_o_proj"].T)
    d["qkw3"] = rows(np.concatenate([a["L3_attn_q_norm"], a["L3_attn_k_norm"]])).reshape(P, 2, 32)
    d["wr"] = kn(np.concatenate([a["L3_ffn_gate_w"], a["L3_ffn_shared_gate_w"], np.zeros((1, C), np.float32)], 0).T)
    d["sgu"] = kn(a["L3_ffn_shared_gate_up_w"].T)
    z = lambda *s: np.zeros(s, np.float32)
    d["sdn"] = kn(np.concatenate([a["L3_ffn_shared_down_w"].T, z(NSF * P - SI, C)], 0))
    w13 = a["L3_ffn_w13"]
    w13 = np.concatenate([w13[:, :P], w13[:, EI:EI + P], w13[:, P:EI], z(NE, 64 - EREM, C), w13[:, EI + P:]], 1)
    d["w13"] = kn(w13.reshape(NE * ECOL, C).T)
    w2 = np.concatenate([a["L3_ffn_w2"].transpose(0, 2, 1), z(NE, 2 * P - EI, C)], 1)
    d["wdn"] = kn(w2.reshape(NE * 2 * P, C))
    d.update(tables())
    return {k: np.ascontiguousarray(v) for k, v in d.items()}


def kernel(**inputs):
    import concourse.bacc as bacc
    from concourse.bass_utils import run_bass_kernel_spmd

    data = layout({k: np.asarray(v) for k, v in inputs.items()})
    nc = bacc.Bacc("TRN2", target_bir_lowering=False, num_devices=1)
    dram = {k: nc.dram_tensor(f"in_{k}", list(v.shape), F32, kind="ExternalInput").ap() for k, v in data.items()}
    out = nc.dram_tensor("out_tokens", [P, B * NT, C], F32, kind="ExternalOutput").ap()
    build(nc, dram, out)
    r = run_bass_kernel_spmd(nc, [{f"in_{k}": v for k, v in data.items()}], core_ids=[0])
    y = r.results[0]["out_tokens"]
    return y.transpose(1, 0, 2).reshape(B, T, C)
```
